# Optimizing a Trainium2 kernel written in Bass

```python
import numpy as np
import jax
import jax.numpy as jnp

def _softmax(x, axis=-1):
    return jax.nn.softmax(x, axis=axis)

def _gelu(x):
    return jax.nn.gelu(x, approximate=True)

def _silu(x):
    return jax.nn.silu(x)

def _sigmoid(x):
    return jax.nn.sigmoid(x)

def _layernorm(x, axis=-1, eps=1e-05):
    m = jnp.mean(x, axis=axis, keepdims=True)
    v = jnp.var(x, axis=axis, keepdims=True)
    return (x - m) / jnp.sqrt(v + eps)

def _scatter_add(tgt, idx, src, axis=0):
    return tgt.at[idx].add(src)

def _segment_sum(src, seg, n):
    return jax.ops.segment_sum(src, seg, n)
kernel_name = 'mk_xattn_ffn_d2_seqx_r4_a4835b'

def setup_inputs(seed: int=0):
    np.random.seed(seed)
    _w = jnp.asarray

    def _rec_inputs():
        import jax
        import jax.numpy as jnp
        _rk = jax.random.key(seed)
        x = -0.0002928 + 1 * jax.random.normal(jax.random.fold_in(_rk, 1), (32, 128, 256), jnp.float32)
        _lenS = 128 - jax.random.randint(jax.random.fold_in(_rk, 7), (32,), 0, max(1, 128 // 4) + 1, jnp.int32)
        _lenS2 = 128 - jax.random.randint(jax.random.fold_in(_rk, 8), (32,), 0, max(1, 128 // 4) + 1, jnp.int32)
        _ctx_1024P = jax.random.normal(jax.random.fold_in(_rk, 11), (32, 16, 256), jnp.float32)
        _ctx_1024c = jax.random.dirichlet(jax.random.fold_in(_rk, 511), 0.3 * jnp.ones((16,), jnp.float32), (32, 128))
        _ctx_1024t = jnp.einsum('bsk,bkd->bsd', _ctx_1024c, _ctx_1024P)
        _ctx_1024t = _ctx_1024t * jax.lax.rsqrt(jnp.mean(jnp.square(_ctx_1024t)) + 1e-12) * 0.953939
        ctx_1024 = -1.39393e-06 + 0.999914 * (_ctx_1024t + 0.3 * jax.random.normal(jax.random.fold_in(_rk, 611), (32, 128, 256), jnp.float32))
        return (x, ctx_1024)
    x, ctx_1024 = _rec_inputs()

    def _L0_xattn_setup():
        import jax, jax.numpy as jnp
        import numpy as np
        NUM_HEADS = 16
        key = jax.random.key(seed)
        kq, kk, kv = jax.random.split(key, 3)
        B, S, DIM = (2, 512, 256)
        q = jax.random.normal(kq, (B, S, DIM), dtype=jnp.float32)
        k = jax.random.normal(kk, (B, S, DIM), dtype=jnp.float32)
        v = jax.random.normal(kv, (B, S, DIM), dtype=jnp.float32)
        return {'q': q, 'k': k, 'v': v}
    _L0_xattn_all = _L0_xattn_setup()
    _L0_xattn_in = {k: v for k, v in _L0_xattn_all.items() if k in ()}
    del _L0_xattn_all

    def _L0_ffn_setup():
        import jax, jax.numpy as jnp
        import numpy as np
        B, S, D = (2, 512, 256)
        H = 512
        E = 8
        K = 2
        HS = 512 * 1
        SCALE = 1.0 / float(np.sqrt(D))
        key = jax.random.key(seed)
        ks = jax.random.split(key, 9)
        init = 0.02
        return {'x': jax.random.normal(ks[0], (B, S, D), dtype=jnp.float32), 'Wr': jax.random.normal(ks[1], (D, E), dtype=jnp.float32) * init, 'rb': jnp.zeros((E,), dtype=jnp.float32), 'W1': jax.random.normal(ks[2], (E, D, H), dtype=jnp.float32) * init, 'W2': jax.random.normal(ks[3], (E, H, D), dtype=jnp.float32) * init, 'W3': jax.random.normal(ks[4], (E, D, H), dtype=jnp.float32) * init, 'Ws1': jax.random.normal(ks[5], (D, HS), dtype=jnp.float32) * init, 'Ws2': jax.random.normal(ks[6], (HS, D), dtype=jnp.float32) * init, 'Ws3': jax.random.normal(ks[7], (D, HS), dtype=jnp.float32) * init}
    _L0_ffn_all = _L0_ffn_setup()
    _L0_ffn_in = {k: v for k, v in _L0_ffn_all.items() if k in ('Wr', 'rb', 'W1', 'W2', 'W3', 'Ws1', 'Ws2', 'Ws3')}
    del _L0_ffn_all

    def _L1_xattn_setup():
        import jax, jax.numpy as jnp
        import numpy as np
        B, C_LEN, Q_LEN, D = (8, 512, 128, 256)
        key = jax.random.key(seed)
        ks = jax.random.split(key, 10)
        scale = 1.0 / np.sqrt(D)
        return {'c': jax.random.normal(ks[0], (B, C_LEN, D), dtype=jnp.float32), 'q': jax.random.normal(ks[1], (B, Q_LEN, D), dtype=jnp.float32), 'w_cq': jax.random.normal(ks[2], (D,), dtype=jnp.float32) * scale, 'b_cq': jax.random.normal(ks[3], (), dtype=jnp.float32) * scale, 'w_c': jax.random.normal(ks[4], (D,), dtype=jnp.float32) * scale, 'b_c': jax.random.normal(ks[5], (), dtype=jnp.float32) * scale, 'w_q': jax.random.normal(ks[6], (D,), dtype=jnp.float32) * scale, 'b_q': jax.random.normal(ks[7], (), dtype=jnp.float32) * scale, 'W_l': jax.random.normal(ks[8], (D, 4 * D), dtype=jnp.float32) * (1.0 / np.sqrt(4 * D)), 'b_l': jax.random.normal(ks[9], (D,), dtype=jnp.float32) * (1.0 / np.sqrt(4 * D))}
    _L1_xattn_all = _L1_xattn_setup()
    _L1_xattn_in = {k: v for k, v in _L1_xattn_all.items() if k in ('w_cq', 'b_cq', 'w_c', 'b_c', 'w_q', 'b_q', 'W_l', 'b_l')}
    del _L1_xattn_all

    def _L1_ffn_setup():
        import jax, jax.numpy as jnp
        import numpy as np
        D_MODEL = 256
        EXPANSION = 4
        D_HIDDEN = D_MODEL * EXPANSION
        NUM_STAGES = int(np.log2(D_HIDDEN))

        def butterfly(y, weights, dim):
            lead = y.shape[:-1]
            for stage in range(weights.shape[0]):
                s = 2 ** stage
                nb = dim // (2 * s)
                yr = y.reshape(*lead, nb, 2, s)
                a = yr[..., 0, :]
                b = yr[..., 1, :]
                w = weights[stage].reshape(nb, s, 2, 2)
                na = w[..., 0, 0] * a + w[..., 0, 1] * b
                nb2 = w[..., 1, 0] * a + w[..., 1, 1] * b
                y = jnp.stack([na, nb2], axis=-2).reshape(*lead, dim)
            return y
        key = jax.random.key(seed)
        ks = jax.random.split(key, 6)
        B, S = (4, 512)
        x = jax.random.normal(ks[0], (B, S, D_MODEL), jnp.float32)
        W_exp = jax.random.normal(ks[1], (D_MODEL, D_HIDDEN), jnp.float32) * 0.02
        b_exp = jnp.zeros((D_HIDDEN,), jnp.float32)
        up_weights = jax.random.normal(ks[2], (NUM_STAGES, D_HIDDEN // 2, 2, 2), jnp.float32) * 0.02
        up_bias = jnp.zeros((D_HIDDEN,), jnp.float32)
        down_weights = jax.random.normal(ks[3], (NUM_STAGES, D_HIDDEN // 2, 2, 2), jnp.float32) * 0.02
        W_con = jax.random.normal(ks[4], (D_HIDDEN, D_MODEL), jnp.float32) * 0.02
        b_con = jnp.zeros((D_MODEL,), jnp.float32)
        down_bias = jnp.zeros((D_MODEL,), jnp.float32)
        return dict(x=x, W_exp=W_exp, b_exp=b_exp, up_weights=up_weights, up_bias=up_bias, down_weights=down_weights, W_con=W_con, b_con=b_con, down_bias=down_bias)
    _L1_ffn_all = _L1_ffn_setup()
    _L1_ffn_in = {k: v for k, v in _L1_ffn_all.items() if k in ('W_exp', 'b_exp', 'up_weights', 'up_bias', 'down_weights', 'W_con', 'b_con', 'down_bias')}
    del _L1_ffn_all
    return {'x': x, 'ctx_1024': ctx_1024, 'L0_ffn_Wr': _L0_ffn_in['Wr'], 'L0_ffn_rb': _L0_ffn_in['rb'], 'L0_ffn_W1': _L0_ffn_in['W1'], 'L0_ffn_W2': _L0_ffn_in['W2'], 'L0_ffn_W3': _L0_ffn_in['W3'], 'L0_ffn_Ws1': _L0_ffn_in['Ws1'], 'L0_ffn_Ws2': _L0_ffn_in['Ws2'], 'L0_ffn_Ws3': _L0_ffn_in['Ws3'], 'L1_xattn_w_cq': _L1_xattn_in['w_cq'], 'L1_xattn_b_cq': _L1_xattn_in['b_cq'], 'L1_xattn_w_c': _L1_xattn_in['w_c'], 'L1_xattn_b_c': _L1_xattn_in['b_c'], 'L1_xattn_w_q': _L1_xattn_in['w_q'], 'L1_xattn_b_q': _L1_xattn_in['b_q'], 'L1_xattn_W_l': _L1_xattn_in['W_l'], 'L1_xattn_b_l': _L1_xattn_in['b_l'], 'L1_ffn_W_exp': _L1_ffn_in['W_exp'], 'L1_ffn_b_exp': _L1_ffn_in['b_exp'], 'L1_ffn_up_weights': _L1_ffn_in['up_weights'], 'L1_ffn_up_bias': _L1_ffn_in['up_bias'], 'L1_ffn_down_weights': _L1_ffn_in['down_weights'], 'L1_ffn_W_con': _L1_ffn_in['W_con'], 'L1_ffn_b_con': _L1_ffn_in['b_con'], 'L1_ffn_down_bias': _L1_ffn_in['down_bias']}

def reference(x, ctx_1024, L0_ffn_Wr, L0_ffn_rb, L0_ffn_W1, L0_ffn_W2, L0_ffn_W3, L0_ffn_Ws1, L0_ffn_Ws2, L0_ffn_Ws3, L1_xattn_w_cq, L1_xattn_b_cq, L1_xattn_w_c, L1_xattn_b_c, L1_xattn_w_q, L1_xattn_b_q, L1_xattn_W_l, L1_xattn_b_l, L1_ffn_W_exp, L1_ffn_b_exp, L1_ffn_up_weights, L1_ffn_up_bias, L1_ffn_down_weights, L1_ffn_W_con, L1_ffn_b_con, L1_ffn_down_bias):
    import jax
    import jax.numpy as jnp

    def _L0_xattn_ref(q, k, v):
        import jax, jax.numpy as jnp
        import numpy as np
        NUM_HEADS = 16
        B, S, dim = q.shape
        H = NUM_HEADS
        D = dim // H
        scale = D ** (-0.5)
        qh = q.reshape(B, S, H, D) * scale
        kh = k.reshape(B, S, H, D)
        vh = v.reshape(B, S, H, D)
        scores = jnp.einsum('bqhd,bkhd->bhqk', qh, kh)
        weights = jax.nn.softmax(scores, axis=-1)
        out = jnp.einsum('bhqk,bkhd->bqhd', weights, vh)
        return out.reshape(B, S, dim)

    def _L0_ffn_ref(x, Wr, rb, W1, W2, W3, Ws1, Ws2, Ws3):
        import jax, jax.numpy as jnp
        import numpy as np
        B, S, D = (2, 512, 256)
        H = 512
        E = 8
        K = 2
        HS = 512 * 1
        SCALE = 1.0 / float(np.sqrt(D))
        logits = jnp.einsum('bsd,de->bse', x, Wr) * SCALE
        _, idx = jax.lax.top_k(logits + rb, K)
        gathered = jnp.take_along_axis(logits, idx, axis=-1)
        w = jax.nn.softmax(gathered, axis=-1)
        w_full = jnp.sum(jax.nn.one_hot(idx, E, dtype=x.dtype) * w[..., None], axis=-2)
        h = jnp.einsum('bsd,edh->bseh', x, W1) * jax.nn.silu(jnp.einsum('bsd,edh->bseh', x, W3))
        expert_out = jnp.einsum('bseh,ehd->bsed', h, W2)
        out = jnp.einsum('bsed,bse->bsd', expert_out, w_full)
        hs = jnp.einsum('bsd,dh->bsh', x, Ws1) * jax.nn.silu(jnp.einsum('bsd,dh->bsh', x, Ws3))
        out = out + jnp.einsum('bsh,hd->bsd', hs, Ws2)
        return out

    def _L1_xattn_ref(c, q, w_cq, b_cq, w_c, b_c, w_q, b_q, W_l, b_l):
        import jax, jax.numpy as jnp
        import numpy as np
        B, C_LEN, Q_LEN, D = (8, 512, 128, 256)
        cq = jnp.einsum('bcd,bqd,d->bcq', c, q, w_cq) + b_cq
        s = (c @ w_c + b_c)[:, :, None] + (q @ w_q + b_q)[:, None, :] + cq
        a = jax.nn.softmax(s, axis=2)
        c2q_att = jnp.einsum('bcq,bqd->bcd', a, q)
        b_att = jax.nn.softmax(jnp.max(s, axis=2), axis=1)
        q2c_att = jnp.einsum('bc,bcd->bd', b_att, c)[:, None, :]
        x = jnp.concatenate([c, c2q_att, c * c2q_att, c * q2c_att], axis=-1)
        z = x @ W_l.T + b_l
        return z

    def _L1_ffn_ref(x, W_exp, b_exp, up_weights, up_bias, down_weights, W_con, b_con, down_bias):
        import jax, jax.numpy as jnp
        import numpy as np
        D_MODEL = 256
        EXPANSION = 4
        D_HIDDEN = D_MODEL * EXPANSION
        NUM_STAGES = int(np.log2(D_HIDDEN))

        def butterfly(y, weights, dim):
            lead = y.shape[:-1]
            for stage in range(weights.shape[0]):
                s = 2 ** stage
                nb = dim // (2 * s)
                yr = y.reshape(*lead, nb, 2, s)
                a = yr[..., 0, :]
                b = yr[..., 1, :]
                w = weights[stage].reshape(nb, s, 2, 2)
                na = w[..., 0, 0] * a + w[..., 0, 1] * b
                nb2 = w[..., 1, 0] * a + w[..., 1, 1] * b
                y = jnp.stack([na, nb2], axis=-2).reshape(*lead, dim)
            return y
        h = jnp.einsum('bsd,dh->bsh', x, W_exp) + b_exp
        h = butterfly(h, up_weights, D_HIDDEN)
        h = jax.nn.gelu(h + up_bias, approximate=False)
        h = butterfly(h, down_weights, D_HIDDEN)
        y = jnp.einsum('bsh,hd->bsd', h, W_con) + b_con
        return y + down_bias
    x = x + _L0_xattn_ref(_layernorm(x, axis=-1), ctx_1024, ctx_1024)
    x = x + _L0_ffn_ref(_layernorm(x, axis=-1), L0_ffn_Wr, L0_ffn_rb, L0_ffn_W1, L0_ffn_W2, L0_ffn_W3, L0_ffn_Ws1, L0_ffn_Ws2, L0_ffn_Ws3)
    x = x + _L1_xattn_ref(_layernorm(x, axis=-1), ctx_1024, L1_xattn_w_cq, L1_xattn_b_cq, L1_xattn_w_c, L1_xattn_b_c, L1_xattn_w_q, L1_xattn_b_q, L1_xattn_W_l, L1_xattn_b_l)
    x = x + _L1_ffn_ref(_layernorm(x, axis=-1), L1_ffn_W_exp, L1_ffn_b_exp, L1_ffn_up_weights, L1_ffn_up_bias, L1_ffn_down_weights, L1_ffn_W_con, L1_ffn_b_con, L1_ffn_down_bias)
    return x

_drawn_inputs = setup_inputs


def setup_inputs(seed=0):
    import zlib

    import numpy as np

    out = dict(_drawn_inputs(seed))
    spreads = {'L0_ffn_rb': (0.0, 0.546),
     'L1_ffn_b_exp': (0.0, 0.1),
     'L1_ffn_up_bias': (0.0, 0.1),
     'L1_ffn_b_con': (0.0, 0.1),
     'L1_ffn_down_bias': (0.0, 0.1)}
    factors = {'L0_ffn_Wr': 8.0,
     'L0_ffn_W1': 4.443,
     'L0_ffn_W2': 4.442,
     'L0_ffn_W3': 4.495,
     'L0_ffn_Ws1': 3.152,
     'L0_ffn_Ws2': 3.13,
     'L0_ffn_Ws3': 3.189,
     'L1_xattn_b_l': 4.445}
    for name, (base, spread) in spreads.items():
        noise = np.random.default_rng([zlib.crc32(name.encode()), seed]).standard_normal(out[name].shape)
        drawn = base * np.exp(spread * noise) if base else spread * noise
        out[name] = jnp.asarray(drawn.astype(out[name].dtype))
    for name, factor in factors.items():
        out[name] = (out[name] * factor).astype(out[name].dtype)
    return out
```

```python
import concourse.bass as bass
from concourse import mybir
from contextlib import ExitStack

F32 = mybir.dt.float32
I32 = mybir.dt.int32
ALU = mybir.AluOpType
ACT = mybir.ActivationFunctionType
AX = mybir.AxisListType
MASK_AT, GATE_AT = 16, 22

P = 128
D = 256
C = D // P
EPS = 1e-5


def wait(eng, sem, value):
    if isinstance(value, int) and value <= 0:
        return
    eng.wait_ge(sem, value)


def steps(eng, first, last, lo, hi, unroll, body):
    assert lo % unroll == 0 and hi % unroll == 0
    for t in range(first, lo):
        body(t, t % unroll)
    if hi > lo:
        with eng.Fori(lo // unroll, hi // unroll) as i:
            for u in range(unroll):
                body(i * unroll + u, u)
    for t in range(hi, last):
        body(t, t % unroll)


def stage_on(n):
    return lambda t: not isinstance(t, int) or 0 <= t < n


def upto(t, n):
    return min(t, n) if isinstance(t, int) else t


def build_program(nc, x, ctx_in, Wr, rb, W1, W2, W3, Ws1, Ws2, Ws3, w_cq, b_cq, w_c, b_c, w_q, b_q,
                  WlT, b_l, W_exp, b_exp, up_w, up_bias, dn_w, WconT, b_con, dn_bias, out):
    NB = x.shape[0]
    E = W1.shape[0]
    H = W1.shape[2]
    HC = H // P
    HS = Ws1.shape[1]
    HSC = HS // P
    NH = 16
    DH = D // NH
    HH = NH // C
    TOPK = 2
    NT = NB * TOPK + E
    F = W_exp.shape[1]
    FC = F // P
    NST = up_w.shape[0]
    ctx = ExitStack()
    sem = lambda name: ctx.enter_context(nc.semaphore(name))
    sems = lambda name, n: [sem(f"{name}{i}") for i in range(n)]
    per = lambda name, shape, dt=F32: ctx.enter_context(nc.sbuf_tensor(name, shape, dt))

    def dram(name, shape):
        return nc.dram_tensor(name, shape, F32, kind="Internal").ap()

    x1_d = dram("x1_d", (NB, P, D))
    h1_d = dram("h1_d", (NB, P, D))
    h1T_d = dram("h1T_d", (NB, P, C * P))
    acc_d = dram("acc_d", (NB, P, D))
    xs_d = dram("xs_d", (NT * P, D))
    ys_d = dram("ys_d", (NT * P, D))
    x3_d = dram("x3_d", (NB, P, D))
    bu_d = dram("bu_d", (1, F))

    with ctx:
        ident = per("ident", [P, P])
        mhalf = per("mhalf", [P, 1])
        epsc = per("epsc", [P, 1])
        spare = per("spare", [1, 2, 32])
        ones = per("ones", [P, P])
        logits = per("logits", [P, NB, E])
        gate = per("gate", [P, TOPK, NB])
        slot = per("slot", [P, TOPK, NB], I32)
        tile_expert = per("tile_expert", [1, NT], I32)
        w1m = per("w1m", [P, E, C, H])
        w3m = per("w3m", [P, E, C, H])
        w2m = per("w2m", [P, E, HC, D])

        turn = [0]

        def take_wait(eng):
            turn[0] = (turn[0] + 1) % 32
            if eng is nc.vector:
                eng.memset(spare[:, 0, turn[0]:turn[0] + 1], 0.0)
            else:
                eng.tensor_tensor(out=spare[:, 1, turn[0]:turn[0] + 1], in0=ones[0:1, 0:1], in1=ones[0:1, 0:1], op=ALU.mult)

        s_wm = sem("s_wm")
        s_c = sem("s_c")
        s_zero = sem("s_zero")

        with ExitStack() as ph:
            sb = lambda name, shape, dt=F32: ph.enter_context(nc.sbuf_tensor(name, shape, dt))
            xb = sb("xb", [P, 4, D])
            cb = sb("cb", [P, 4, D])
            xn = sb("xn", [P, 2, D])
            T0 = sb("T0", [P, 2, 2 * C, P])
            bd = sb("bd", [P, 2, C, HH, P])
            hmask = sb("hmask", [P, HH, P])
            pr = sb("pr", [P, C, HH, P])
            pT = sb("pT", [P, C, HH, P])
            va = sb("va", [P, 2, NH, DH + 1])
            mx = sb("mx", [P, C, HH])
            x1 = sb("x1", [P, 2, D])
            h1 = sb("h1", [P, 2, D])
            h1T = sb("h1T", [P, 2, C, P])
            rec = sb("rec", [P, 2, NH, 1])
            st1 = sb("st1", [P, 4, 6])
            mv1 = sb("mv1", [P, 4, 2])
            rs1 = sb("rs1", [P, 4, 2])
            st2 = sb("st2", [P, 4, 6])
            mv2 = sb("mv2", [P, 4, 2])
            rs2 = sb("rs2", [P, 4, 2])
            wr = sb("wr", [P, C, E])
            zeros = sb("zeros", [P, 2, D])
            S = [ph.enter_context(nc.psum_tensor(f"S{c}", [P, HH, P], F32)) for c in range(C)]
            PT = ph.enter_context(nc.psum_tensor("PT", [P, HH, P], F32))
            O = ph.enter_context(nc.psum_tensor("O", [P, 512], F32))
            M = ph.enter_context(nc.psum_tensor("M", [P, 512], F32))
            Ov = O[:, 0:NH * (DH + 1)].rearrange("p (h d) -> p h d", h=NH)

            s_wr = sem("s_wr")
            s_k0 = sem("s_k0")
            s_ld = sems("s_ld", 4)
            s_mv1, s_rs1, s_xn = (sem(n) for n in ("s_mv1", "s_rs1", "s_xn"))
            s_mv2, s_rs2, s_h1 = (sem(n) for n in ("s_mv2", "s_rs2", "s_h1"))
            s_tr1, s_ev1, s_bd, s_va = (sem(n) for n in ("s_tr1", "s_ev1", "s_bd", "s_va"))
            s_sc, s_mx, s_sub, s_exp = (sem(n) for n in ("s_sc", "s_mx", "s_sub", "s_exp"))
            s_pt, s_pte, s_pv = (sem(n) for n in ("s_pt", "s_pte", "s_pv"))
            s_rc, s_nm, s_x1 = (sem(n) for n in ("s_rc", "s_nm", "s_x1"))
            s_h1t, s_h1e, s_lg, s_lc = (sem(n) for n in ("s_h1t", "s_h1e", "s_lg", "s_lc"))
            s_x1st, s_h1st, s_h1Tst = sems("s_x1st", 2), sems("s_h1st", 2), sems("s_h1Tst", 2)
            on = stage_on(NB)
            RANGE = (-4, NB + 1, 4, NB - 4, 4)

            with nc.Block() as block:
                @block.sync
                def _(sp):
                    def load(t, k):
                        if not on(t):
                            return
                        wait(sp, s_x1, t - 3)
                        sp.dma_start(xb[:, k, :], x[t, :, :]).then_inc(s_ld[k], 16)
                        sp.dma_start(cb[:, k, :], ctx_in[t, :, :]).then_inc(s_ld[k], 16)

                    def body(t, k):
                        load(t + 4, k)
                        if on(t):
                            wait(sp, s_x1, t + 1)
                            sp.dma_start(x1_d[t, :, :], x1[:, k % 2, :]).then_inc(s_x1st[k % 2], 16)
                        if on(t - 1):
                            j = (k - 1) % 2
                            wait(sp, s_h1, t)
                            sp.dma_start(h1_d[t - 1, :, :], h1[:, j, :]).then_inc(s_h1st[j], 16)
                            wait(sp, s_h1e, t)
                            sp.dma_start(h1T_d[t - 1, :, :], h1T[:, j, :, :]).then_inc(s_h1Tst[j], 16)

                    sp.dma_start(wr[:, :, :], Wr.rearrange("(c p) e -> p c e", p=P)).then_inc(s_wr, 16)
                    for t in range(-4, 0):
                        body(t, t % 4)
                    for e in range(E):
                        sp.dma_start(w3m[:, e, :, :], W3[e].rearrange("(c p) h -> p c h", p=P)).then_inc(s_wm, 16)
                        sp.dma_start(w1m[:, e, :, :], W1[e].rearrange("(c p) h -> p c h", p=P)).then_inc(s_wm, 16)
                        sp.dma_start(w2m[:, e, :, :], W2[e].rearrange("(c p) d -> p c d", p=P)).then_inc(s_wm, 16)
                    steps(sp, 0, *RANGE[1:], body)
                    for j in range(2):
                        wait(sp, s_x1st[j], 16 * (NB // 2))
                        wait(sp, s_h1st[j], 16 * (NB // 2))
                        wait(sp, s_h1Tst[j], 16 * (NB // 2))

                @block.gpsimd
                def _(pool):
                    nc.gpsimd.memset(ident[:, :], 1.0).then_inc(s_k0, 1)
                    nc.gpsimd.memset(hmask[:, :, :], 1.0).then_inc(s_k0, 1)
                    nc.gpsimd.memset(ones[:, :], 1.0).then_inc(s_c, 1)
                    nc.gpsimd.memset(mhalf[:, :], -0.5).then_inc(s_c, 1)
                    nc.gpsimd.memset(epsc[:, :], EPS).then_inc(s_c, 1)
                    nc.gpsimd.memset(zeros[:, :, :], 0.0).then_inc(s_c, 1)
                    nc.gpsimd.memset(va[:, :, :, DH:DH + 1], 1.0).then_inc(s_c, 1)
                    pool.wait_ge(s_k0, 2)
                    nc.gpsimd.affine_select(out=ident[:, :], in_=ident[:, :], compare_op=ALU.is_equal, fill=0.0,
                                            base=0, pattern=[[-1, P]], channel_multiplier=1).then_inc(s_c, 1)
                    nc.gpsimd.affine_select(out=hmask[:, :, :], in_=hmask[:, :, :], compare_op=ALU.is_ge, fill=0.0,
                                            base=0, pattern=[[-DH, HH], [0, P]], channel_multiplier=1).then_inc(s_k0, 1)
                    pool.wait_ge(s_k0, 3)
                    nc.gpsimd.affine_select(out=hmask[:, :, :], in_=hmask[:, :, :], compare_op=ALU.is_ge, fill=0.0,
                                            base=DH - 1, pattern=[[DH, HH], [0, P]], channel_multiplier=-1).then_inc(s_c, 1)
                    pool.wait_ge(s_c, 7)

                    def rstd(t, s_mv, s_rs, mv, rs, k):
                        wait(pool, s_mv, 2 * t + 2)
                        nc.gpsimd.tensor_tensor(out=rs[:, k, 0:1], in0=mv[:, k, 1:2], in1=epsc[:, :], op=ALU.add).then_inc(s_rs, 1)
                        wait(pool, s_rs, 2 * t + 1)
                        nc.gpsimd.tensor_tensor(out=rs[:, k, 1:2], in0=rs[:, k, 0:1], in1=mhalf[:, :],
                                                op=ALU.pow).then_inc(s_rs, 1)

                    def body(t, k):
                        if on(t + 1):
                            a = (k + 1) % 4
                            wait(pool, s_ld[a], (t + 1 - a) * 8 + 32)
                            wait(pool, s_pv, 2 * t)
                            nc.gpsimd.tensor_tensor(out=va[:, a % 2, :, 0:DH],
                                                    in0=cb[:, a, :].rearrange("p (h d) -> p h d", h=NH),
                                                    in1=ones[:, 0:1].unsqueeze(1).broadcast_to([P, NH, DH]),
                                                    op=ALU.mult).then_inc(s_va, 1)
                        if on(t + 2):
                            a = k % 2
                            wait(pool, s_ev1, t + 3)
                            wait(pool, s_sc, 2 * t + 2)
                            for c in range(C):
                                nc.gpsimd.tensor_tensor(out=bd[:, a, c, :, :],
                                                        in0=T0[:, a, C + c:C + c + 1, :].broadcast_to([P, HH, P]),
                                                        in1=hmask[:, :, :], op=ALU.mult).then_inc(s_bd, 1)
                        if on(t + 3):
                            rstd(t + 3, s_mv1, s_rs1, mv1, rs1, (k + 3) % 4)
                        if on(t):
                            rstd(t, s_mv2, s_rs2, mv2, rs2, k)

                    steps(pool, *RANGE, body)

                @block.vector
                def _(dve):
                    def stats(t, k, src, st, mv, s_mv):
                        nc.vector.bn_stats(st[:, k, :], src).then_inc(s_mv, 1)
                        wait(dve, s_mv, 2 * t + 1)
                        take_wait(nc.vector)
                        nc.vector.bn_aggr(mv[:, k, :], st[:, k, :]).then_inc(s_mv, 1)

                    def body(t, k):
                        if on(t - 1):
                            a = (k - 1) % 4
                            wait(dve, s_rs2, 2 * t)
                            wait(dve, s_h1st[a % 2], (t - 1 - a % 2) * 8)
                            wait(dve, s_h1t, t - 2)
                            nc.vector.tensor_scalar(h1[:, a % 2, :], x1[:, a % 2, :], mv2[:, a, 0:1], rs2[:, a, 1:2],
                                                    ALU.subtract, ALU.mult).then_inc(s_h1, 1)
                        if on(t + 2):
                            a = (k + 2) % 4
                            wait(dve, s_rs1, 2 * t + 6)
                            wait(dve, s_tr1, t + 1)
                            nc.vector.tensor_scalar(xn[:, a % 2, :], xb[:, a, :], mv1[:, a, 0:1], rs1[:, a, 1:2],
                                                    ALU.subtract, ALU.mult).then_inc(s_xn, 1)
                        if on(t + 1):
                            for h in range(C):
                                wait(dve, s_sc, 2 * t + 3 + h)
                                nc.vector.tensor_reduce(mx[:, h, :], S[h][:, :, :], AX.X, ALU.max).then_inc(s_mx, 1)
                                wait(dve, s_mx, 2 * t + 3 + h)
                                nc.vector.tensor_tensor(S[h][:, :, :], S[h][:, :, :],
                                                        mx[:, h, :].unsqueeze(2).broadcast_to([P, HH, P]),
                                                        ALU.subtract).then_inc(s_sub, 1)
                        if on(t + 3):
                            a = (k + 3) % 4
                            wait(dve, s_ld[a], (t + 3 - a) * 8 + 32)
                            stats(t + 3, a, xb[:, a, :], st1, mv1, s_mv1)
                        if on(t):
                            a = k % 2
                            wait(dve, s_pv, 2 * t + 2)
                            wait(dve, s_x1st[a], (t - a) * 8)
                            nc.vector.reciprocal(rec[:, a, :, :], Ov[:, :, DH:DH + 1]).then_inc(s_rc, 1)
                            wait(dve, s_rc, t + 1)
                            nc.vector.tensor_tensor(x1[:, a, :].rearrange("p (h d) -> p h d", h=NH), Ov[:, :, 0:DH],
                                                    rec[:, a, :, :].broadcast_to([P, NH, DH]),
                                                    ALU.mult).then_inc(s_nm, 1)
                            wait(dve, s_nm, t + 1)
                            nc.vector.tensor_tensor(x1[:, a, :], x1[:, a, :], xb[:, k, :], ALU.add).then_inc(s_x1, 1)
                            wait(dve, s_x1, t + 1)
                            stats(t, k, x1[:, a, :], st2, mv2, s_mv2)
                        if on(t - 1):
                            wait(dve, s_lg, t)
                            nc.vector.tensor_scalar(logits[:, bass.ds(t - 1, 1), :].rearrange("p o e -> p (o e)"),
                                                    M[:, 0:E], 1.0 / 16.0, None, ALU.mult).then_inc(s_lc, 1)

                    steps(dve, *RANGE, body)

                @block.scalar
                def _(act):
                    act.wait_ge(s_c, 7)
                    for i in range(NT // 2):
                        act.dma_start(xs_d[2 * P * i:2 * P * (i + 1), :].rearrange("(a p) d -> p a d", p=P),
                                      zeros[:, :, :]).then_inc(s_zero, 16)

                    def body(t, k):
                        def weights_copy(h):
                            if on(t):
                                wait(act, s_pt, 2 * t + h + 1)
                                wait(act, s_pv, 2 * t + h - 1)
                                nc.scalar.copy(pT[:, h, :, :], PT[:, :, :]).then_inc(s_pte, 1)

                        def exps(h):
                            if on(t + 1):
                                wait(act, s_sub, 2 * t + 3 + h)
                                wait(act, s_pt, 2 * t + h + 1)
                                nc.scalar.activation(pr[:, h, :, :], S[h][:, :, :], ACT.Exp,
                                                     scale=DH ** -0.5).then_inc(s_exp, 1)

                        if on(t + 2):
                            wait(act, s_tr1, t + 3)
                            wait(act, s_sc, 2 * t + 2)
                            wait(act, s_bd, 2 * t + 2)
                            nc.scalar.copy(T0[:, k % 2, :, :],
                                           M[:, :].rearrange("p (c n) -> p c n", c=2 * C)).then_inc(s_ev1, 1)
                        weights_copy(0)
                        exps(0)
                        if on(t - 1):
                            wait(act, s_h1t, t)
                            wait(act, s_h1Tst[(k - 1) % 2], (t - 1 - (k - 1) % 2) * 8)
                            wait(act, s_lg, t - 2)
                            nc.scalar.copy(h1T[:, (k - 1) % 2, :, :],
                                           M[:, 0:C * P].rearrange("p (c n) -> p c n", c=C)).then_inc(s_h1e, 1)
                        weights_copy(1)
                        exps(1)

                    steps(act, *RANGE, body)

                @block.tensor
                def _(pe):
                    pe.wait_ge(s_c, 7)
                    pe.wait_ge(s_wr, 16)

                    def weights_transpose(t, h):
                        if on(t):
                            wait(pe, s_exp, 2 * t + h + 1)
                            wait(pe, s_pte, 2 * t + h)
                            for i in range(HH):
                                last = nc.tensor.transpose(PT[:, i, :], pr[:, h, i, :], ident[:, :])
                            last.then_inc(s_pt, 1)

                    def scores(t, k, h):
                        if on(t):
                            wait(pe, s_bd, 2 * t + 2)
                            wait(pe, s_exp, 2 * t - 1 + h)
                            for i in range(0, HH, 4):
                                last = nc.tensor.matmul(S[h][:, i:i + 4, :], T0[:, k % 2, h, :],
                                                        bd[:, k % 2, h, i:i + 4, :], start=True, stop=True)
                            last.then_inc(s_sc, 1)

                    def values(t, k, h):
                        if on(t):
                            wait(pe, s_pte, 2 * t + h + 1)
                            wait(pe, s_va, t + 1)
                            wait(pe, s_nm, t)
                            for i in range(HH):
                                last = nc.tensor.matmul(Ov[:, HH * h + i, :], pT[:, h, i, :],
                                                        va[:, k % 2, HH * h + i, :], start=True, stop=True)
                            last.then_inc(s_pv, 1)

                    def body(t, k):
                        if on(t + 2):
                            a = (k + 2) % 4
                            wait(pe, s_xn, t + 3)
                            wait(pe, s_ld[a], (t + 2 - a) * 8 + 32)
                            wait(pe, s_lc, t - 1)
                            for c in range(C):
                                nc.tensor.transpose(M[:, c * P:(c + 1) * P], xn[:, a % 2, c * P:(c + 1) * P], ident[:, :])
                            for c in range(C):
                                last = nc.tensor.transpose(M[:, (C + c) * P:(C + c + 1) * P],
                                                           cb[:, a, c * P:(c + 1) * P], ident[:, :])
                            last.then_inc(s_tr1, 1)
                        weights_transpose(t, 0)
                        scores(t + 1, k + 1, 0)
                        values(t, k, 0)
                        if on(t - 1):
                            a = (k - 1) % 2
                            wait(pe, s_h1, t)
                            wait(pe, s_ev1, upto(t + 3, NB))
                            wait(pe, s_lc, t - 1)
                            for c in range(C):
                                last = nc.tensor.transpose(M[:, c * P:(c + 1) * P], h1[:, a, c * P:(c + 1) * P],
                                                           ident[:, :])
                            last.then_inc(s_h1t, 1)
                        weights_transpose(t, 1)
                        scores(t + 1, k + 1, 1)
                        values(t, k, 1)
                        if on(t - 1):
                            wait(pe, s_h1e, t)
                            for c in range(C):
                                last = nc.tensor.matmul(M[:, 0:E], h1T[:, (k - 1) % 2, c, :], wr[:, c, :],
                                                        start=c == 0, stop=c == C - 1)
                            last.then_inc(s_lg, 1)

                    steps(pe, *RANGE, body)
        with ExitStack() as ph:
            sb = lambda name, shape, dt=F32: ph.enter_context(nc.sbuf_tensor(name, shape, dt))
            rbb = sb("rbb", [P, E])
            revi = sb("revi", [P, E])
            sel = sb("sel", [P, NB, E])
            t0 = sb("t0", [P, NB, E])
            oh = sb("oh", [P, TOPK, NB, E])
            top = sb("top", [P, NB])
            gl = sb("gl", [P, TOPK, NB])
            mask = sb("mask", [P, NB, E])
            upper = sb("upper", [P, P])
            cum = sb("cum", [P, E, NB])
            tot = sb("tot", [P, E, NB])
            zb = sb("zb", [P, E * NB])
            start = sb("start", [P, E])
            cnt = sb("cnt", [P, E])
            cnti = sb("cnti", [P, E], I32)
            tiles = sb("tiles", [P, E])
            ctile = sb("ctile", [P, E])
            off = sb("off", [P, E])
            slotf = sb("slotf", [P, TOPK, NB])
            tid = sb("tid", [1, NT])
            le = sb("le", [1, NT, E])
            tef = sb("tef", [1, NT])
            R = [ph.enter_context(nc.psum_tensor(f"R{i}", [P, NB, E], F32)) for i in range(2)]
            s_rb, s_i, s_i2, s_v, s_e, s_mm = (sem(n) for n in ("s_rb", "s_i", "s_i2", "s_v", "s_e", "s_mm"))
            with nc.Block() as block:
                @block.sync
                def _(sp):
                    sp.dma_start(rbb[:, :], rb.rearrange("(o e) -> o e", o=1).broadcast_to([P, E])).then_inc(s_rb, 16)

                @block.gpsimd
                def _(pool):
                    nc.gpsimd.iota(revi[:, :], pattern=[[-1, E]], base=E, channel_multiplier=0,
                                   allow_small_or_imprecise_dtypes=True).then_inc(s_i, 1)
                    nc.gpsimd.iota(tid[:, :], pattern=[[1, NT]], base=0, channel_multiplier=0,
                                   allow_small_or_imprecise_dtypes=True).then_inc(s_i, 1)
                    nc.gpsimd.memset(zb[:, :], 0.0).then_inc(s_i, 1)
                    nc.gpsimd.memset(upper[:, :], 1.0).then_inc(s_i2, 1)
                    pool.wait_ge(s_i2, 1)
                    nc.gpsimd.affine_select(out=upper[:, :], in_=upper[:, :], compare_op=ALU.is_gt, fill=0.0,
                                            base=0, pattern=[[1, P]], channel_multiplier=-1).then_inc(s_i, 1)

                @block.tensor
                def _(pe):
                    pe.wait_ge(s_i, 4)
                    pe.wait_ge(s_v, MASK_AT)
                    nc.tensor.matmul(R[0][:, :, :], upper[:, :], mask[:, :, :], start=True, stop=True)
                    nc.tensor.matmul(R[1][:, :, :], ones[:, :], mask[:, :, :], start=True, stop=True).then_inc(s_mm, 1)

                @block.scalar
                def _(act):
                    act.wait_ge(s_v, GATE_AT)
                    nc.scalar.activation(gl[:, :, :], gl[:, :, :], ACT.Exp).then_inc(s_e, 1)

                @block.vector
                def _(dve):
                    done = [0]

                    def link(ins):
                        done[0] += 1
                        ins.then_inc(s_v, 1)
                        dve.wait_ge(s_v, done[0])

                    TT, TS, RED = nc.vector.tensor_tensor, nc.vector.tensor_scalar, nc.vector.tensor_reduce
                    over_b = lambda a: a.unsqueeze(1).broadcast_to([P, NB, E])
                    over_e = lambda a: a.unsqueeze(2).broadcast_to([P, NB, E])
                    dve.wait_ge(s_rb, 16)
                    dve.wait_ge(s_i, 4)
                    link(TT(sel[:, :, :], logits[:, :, :], over_b(rbb[:, :]), ALU.add))
                    for j in range(TOPK):
                        link(RED(top[:, :], sel[:, :, :], AX.X, ALU.max))
                        link(TT(t0[:, :, :], sel[:, :, :], over_e(top[:, :]), ALU.is_ge))
                        link(TT(t0[:, :, :], t0[:, :, :], over_b(revi[:, :]), ALU.mult))
                        link(RED(top[:, :], t0[:, :, :], AX.X, ALU.max))
                        link(TT(oh[:, j, :, :], over_b(revi[:, :]), over_e(top[:, :]), ALU.is_equal))
                        if j + 1 < TOPK:
                            link(TS(t0[:, :, :], oh[:, j, :, :], -1.0, 1.0, ALU.mult, ALU.add))
                            link(TT(sel[:, :, :], sel[:, :, :], t0[:, :, :], ALU.mult))
                            link(TS(t0[:, :, :], oh[:, j, :, :], -3.0e38, None, ALU.mult))
                            link(TT(sel[:, :, :], sel[:, :, :], t0[:, :, :], ALU.add))
                    link(TT(mask[:, :, :], oh[:, 0, :, :], oh[:, 1, :, :], ALU.add))
                    assert done[0] == MASK_AT, done
                    for j in range(TOPK):
                        link(TT(t0[:, :, :], logits[:, :, :], oh[:, j, :, :], ALU.mult))
                        link(RED(gl[:, j, :], t0[:, :, :], AX.X, ALU.add))
                    link(TT(top[:, :], gl[:, 0, :], gl[:, 1, :], ALU.max))
                    link(TT(gl[:, :, :], gl[:, :, :], top[:, :].unsqueeze(1).broadcast_to([P, TOPK, NB]), ALU.subtract))
                    assert done[0] == GATE_AT, done
                    dve.wait_ge(s_e, 1)
                    link(TT(top[:, :], gl[:, 0, :], gl[:, 1, :], ALU.add))
                    link(nc.vector.reciprocal(top[:, :], top[:, :]))
                    link(TT(gate[:, :, :], gl[:, :, :], top[:, :].unsqueeze(1).broadcast_to([P, TOPK, NB]), ALU.mult))
                    dve.wait_ge(s_mm, 1)
                    link(nc.vector.tensor_copy(tot[:, :, :], R[1][:, :, :].rearrange("p b e -> p e b")))
                    link(nc.vector.tensor_tensor_scan(cum[:, :, :].rearrange("p e b -> p (e b)"),
                                                      tot[:, :, :].rearrange("p e b -> p (e b)"),
                                                      zb[:, :], 0.0, ALU.add, ALU.add))
                    link(nc.vector.memset(start[:, 0:1], 0.0))
                    link(nc.vector.tensor_copy(start[:, 1:E], cum[:, 0:E - 1, NB - 1]))
                    link(TT(cnt[:, :], cum[:, :, NB - 1], start[:, :], ALU.subtract))
                    link(TT(cum[:, :, :], cum[:, :, :], tot[:, :, :], ALU.subtract))
                    link(TS(cnti[:, :], cnt[:, :], float(P - 1), None, ALU.add))
                    link(TS(cnti[:, :], cnti[:, :], P.bit_length() - 1, None, ALU.logical_shift_right))
                    link(nc.vector.tensor_copy(tiles[:, :], cnti[:, :]))
                    link(nc.vector.tensor_tensor_scan(ctile[:, :], tiles[:, :], zb[:, 0:E], 0.0, ALU.add, ALU.add))
                    link(TT(off[:, :], ctile[:, :], tiles[:, :], ALU.subtract))
                    link(TS(off[:, :], off[:, :], float(P), None, ALU.mult))
                    link(TT(off[:, :], off[:, :], start[:, :], ALU.subtract))
                    link(TT(sel[:, :, :], R[0][:, :, :], cum[:, :, :].rearrange("p e b -> p b e"), ALU.add))
                    link(TT(sel[:, :, :], sel[:, :, :], over_b(off[:, :]), ALU.add))
                    for j in range(TOPK):
                        link(TT(t0[:, :, :], sel[:, :, :], oh[:, j, :, :], ALU.mult))
                        link(RED(slotf[:, j, :], t0[:, :, :], AX.X, ALU.add))
                    link(nc.vector.tensor_copy(slot[:, :, :], slotf[:, :, :]))
                    link(TT(le[:, :, :], ctile[0:1, :].unsqueeze(1).broadcast_to([1, NT, E]),
                            tid[:, :].unsqueeze(2).broadcast_to([1, NT, E]), ALU.is_le))
                    link(RED(tef[:, :], le[:, :, :], AX.X, ALU.add))
                    link(TS(tile_expert[:, :], tef[:, :], float(E - 1), None, ALU.min))

        with ExitStack() as ph:
            sb = lambda name, shape, dt=F32: ph.enter_context(nc.sbuf_tensor(name, shape, dt))
            ws1 = sb("ws1", [P, C, HS])
            ws3 = sb("ws3", [P, C, HS])
            ws2 = sb("ws2", [P, HSC, D])
            hs = sb("hs", [P, 4, 2, C, P])
            xr = sb("xr", [P, 4, 2, D])
            sg = sb("sg", [P, 2, 2, 2 * P])
            hh = sb("hh", [P, 2, HSC, 2 * P])
            ao = sb("ao", [P, 2, 2, D])
            ht = sb("ht", [P, 4, D])
            ix = sb("ix", [P, 4, TOPK, 1], I32)
            U = [ph.enter_context(nc.psum_tensor(f"U{i}", [P, 2, 2 * P], F32)) for i in range(2)]
            G = [ph.enter_context(nc.psum_tensor(f"G{i}", [P, 2, 2 * P], F32)) for i in range(2)]
            Y = [ph.enter_context(nc.psum_tensor(f"Y{i}", [P, D], F32)) for i in range(2)]
            s_ws = sem("s_ws")
            s_hl, s_ht = sems("s_hl", 4), sems("s_ht", 4)
            s_up, s_sl, s_ml, s_dn, s_ad, s_ix = (sem(n) for n in ("s_up", "s_sl", "s_ml", "s_dn", "s_ad", "s_ix"))
            s_ast, s_scat = sems("s_ast", 2), sems("s_scat", 4)
            NP = NB // 2
            onp, onb = stage_on(NP), stage_on(NB)
            RANGE3 = (-4, NP + 1, 4, NP - 4, 4)
            with nc.Block() as block:
                @block.sync
                def _(sp):
                    sp.dma_start(ws3[:, :, :], Ws3.rearrange("(c p) h -> p c h", p=P)).then_inc(s_ws, 16)
                    sp.dma_start(ws1[:, :, :], Ws1.rearrange("(c p) h -> p c h", p=P)).then_inc(s_ws, 16)

                    def body(t, k):
                        if onp(t + 4):
                            wait(sp, s_ad, 2 * t + 2)
                            sp.dma_start(hs[:, k, :, :, :].rearrange("p t c n -> p t (c n)"),
                                         h1T_d[bass.ds((t + 4) * 2, 2), :, :].rearrange("t p n -> p t n")
                                         ).then_inc(s_hl[k], 16)
                            sp.dma_start(xr[:, k, :, :],
                                         x1_d[bass.ds((t + 4) * 2, 2), :, :].rearrange("t p n -> p t n")
                                         ).then_inc(s_hl[k], 16)
                        if onp(t):
                            wait(sp, s_ad, 2 * t + 2)
                            sp.dma_start(acc_d[bass.ds(t * 2, 2), :, :].rearrange("t p n -> p t n"),
                                         ao[:, k % 2, :, :]).then_inc(s_ast[k % 2], 16)

                    steps(sp, *RANGE3, body)
                    for j in range(2):
                        wait(sp, s_ast[j], 16 * (NP // 2))

                @block.tensor
                def _(pe):
                    pe.wait_ge(s_ws, 48)

                    def up(t, k, h):
                        if onp(t):
                            wait(pe, s_hl[k], (t - k) * 8 + 32)
                            wait(pe, s_ml, 2 * t - 1 + h)
                            for w, bank in ((ws3, G[h]), (ws1, U[h])):
                                for i in range(2):
                                    for c in range(C):
                                        b = (2 * h + i) * P
                                        last = nc.tensor.matmul(bank[:, i, :], w[:, c, b:b + P], hs[:, k, :, c, :],
                                                                start=c == 0, stop=c == C - 1)
                            last.then_inc(s_up, 1)

                    def down(t, k, j):
                        if onp(t):
                            wait(pe, s_ml, 2 * t + 2)
                            wait(pe, s_ad, 2 * t - 1 + j)
                            for c in range(HSC):
                                last = nc.tensor.matmul(Y[j][:, :], hh[:, k % 2, c, j * P:(j + 1) * P], ws2[:, c, :],
                                                        start=c == 0, stop=c == HSC - 1)
                            last.then_inc(s_dn, 1)

                    def body(t, k):
                        up(t, k, 0)
                        down(t - 1, k + 1, 0)
                        up(t, k, 1)
                        down(t - 1, k + 1, 1)

                    steps(pe, 0, *RANGE3[1:], body)

                @block.scalar
                def _(act):
                    act.dma_start(ws2[:, :, :], Ws2.rearrange("(c p) d -> p c d", p=P)).then_inc(s_ws, 16)

                    def body(t, k):
                        if onp(t):
                            for h in range(2):
                                wait(act, s_up, 2 * t + h + 1)
                                wait(act, s_ml, 2 * t - 1 + h)
                                nc.scalar.activation(sg[:, h, :, :], G[h][:, :, :], ACT.Silu).then_inc(s_sl, 1)

                    steps(act, 0, *RANGE3[1:], body)

                @block.vector
                def _(dve):
                    def mul(t, k, h):
                        if onp(t):
                            wait(dve, s_sl, 2 * t + h + 1)
                            wait(dve, s_dn, 2 * t - 2)
                            nc.vector.tensor_tensor(hh[:, k % 2, 2 * h:2 * h + 2, :], U[h][:, :, :], sg[:, h, :, :],
                                                    ALU.mult).then_inc(s_ml, 1)

                    def add(t, k, j):
                        if onp(t):
                            wait(dve, s_dn, 2 * t + j + 1)
                            wait(dve, s_ast[k % 2], (t - k % 2) * 8)
                            nc.vector.tensor_tensor(ao[:, k % 2, j, :], Y[j][:, :], xr[:, k, j, :],
                                                    ALU.add).then_inc(s_ad, 1)

                    def body(t, k):
                        mul(t, k, 0)
                        add(t - 1, (k - 1) % 4, 0)
                        mul(t, k, 1)
                        add(t - 1, (k - 1) % 4, 1)

                    steps(dve, 0, *RANGE3[1:], body)

                @block.gpsimd
                def _(pool):
                    pool.wait_ge(s_zero, 16 * (NT // 2))

                    def body(t, k):
                        wait(pool, s_scat[k], (t - k) * 8)
                        take_wait(nc.gpsimd)
                        pool.dma_start(ht[:, k, :], h1_d[t, :, :]).then_inc(s_ht[k], 16)
                        take_wait(nc.gpsimd)
                        nc.gpsimd.tensor_copy(ix[:, k, :, :], slot[:, :, bass.ds(t, 1)]).then_inc(s_ix, 1)
                        wait(pool, s_ix, t + 1)
                        wait(pool, s_ht[k], (t - k) * 4 + 16)
                        for j in range(TOPK):
                            take_wait(nc.gpsimd)
                            nc.gpsimd.indirect_dma_start(
                                out=xs_d[:, :], out_offset=bass.IndirectOffsetOnAxis(ap=ix[:, k, j, :], axis=0),
                                in_=ht[:, k, :], in_offset=None).then_inc(s_scat[k], 16)

                    steps(pool, 0, NB, 4, NB, 4, body)
                    for k in range(4):
                        wait(pool, s_scat[k], 32 * (NB // 4))

        wup = per("wup", [P, C, F])
        wdT = per("wdT", [P, C, F])
        bup = per("bup", [P, FC])
        wl = per("wl", [P, 4 * C, D])
        with ExitStack() as ph:
            sb = lambda name, shape, dt=F32: ph.enter_context(nc.sbuf_tensor(name, shape, dt))
            xe = sb("xe", [P, 4, D])
            xT = sb("xT", [P, 2, C, P])
            sg4 = sb("sg4", [P, 2, H])
            he = sb("he", [P, 2, H])
            hT = sb("hT", [P, 2, HC, P])
            ye = sb("ye", [P, 2, D])
            bw = sb("bw", [P, 2, F // 2, 4])
            bt = sb("bt", [P, 2, F // 2])
            by = sb("by", [P, F])
            brow = sb("brow", [1, 3, F])
            Ue = [ph.enter_context(nc.psum_tensor(f"Ue{i}", [P, H], F32)) for i in range(2)]
            Ge = [ph.enter_context(nc.psum_tensor(f"Ge{i}", [P, H], F32)) for i in range(2)]
            XT = ph.enter_context(nc.psum_tensor("XT", [P, C, P], F32))
            HT = ph.enter_context(nc.psum_tensor("HT", [P, HC, P], F32))
            Ye = [ph.enter_context(nc.psum_tensor(f"Ye{i}", [P, D], F32)) for i in range(2)]
            s_xe = sems("s_xe", 4)
            s_xt, s_xte, s_g, s_u, s_sl4, s_he = (sem(n) for n in ("s_xt", "s_xte", "s_g", "s_u", "s_sl4", "s_he"))
            s_hT, s_hTe, s_ye, s_yc = (sem(n) for n in ("s_hT", "s_hTe", "s_ye", "s_yc"))
            s_yst = sems("s_yst", 2)
            s_bl, s_bo, s_bs = sem("s_bl"), sem("s_bo"), sem("s_bs")
            s_bw = sems("s_bw", 2)
            on4 = stage_on(NT)
            RANGE4 = (-4, NT + 2, 4, NT - 4, 4)
            with nc.Block() as block:
                @block.sync
                def _(sp):
                    def body(t, k):
                        if on4(t + 4):
                            wait(sp, s_xt, t + 1)
                            sp.dma_start(xe[:, k, :], xs_d[bass.ds((t + 4) * P, P), :]).then_inc(s_xe[k], 16)
                        if on4(t - 1):
                            j = (k - 1) % 2
                            wait(sp, s_yc, t)
                            sp.dma_start(ys_d[bass.ds((t - 1) * P, P), :], ye[:, j, :]).then_inc(s_yst[j], 16)

                    steps(sp, *RANGE4, body)
                    for j in range(2):
                        wait(sp, s_yst[j], 16 * (NT // 2))

                @block.tensor
                def _(pe):
                    pe.wait_ge(s_wm, 16 * 3 * E)

                    def xtr(t, k):
                        if on4(t):
                            wait(pe, s_xe[k % 4], (t - k % 4) * 4 + 16)
                            wait(pe, s_xte, t)
                            for c in range(C):
                                last = nc.tensor.transpose(XT[:, c, :], xe[:, k % 4, c * P:(c + 1) * P], ident[:, :])
                            last.then_inc(s_xt, 1)

                    def body(t, k):
                        if isinstance(t, int) and t < 0:
                            if t == -1:
                                xtr(0, 0)
                            return
                        a, b = k % 2, (k - 1) % 2
                        if on4(t):
                            e = pe.value_load(tile_expert[0:1, bass.ds(t, 1)], min_val=0, max_val=E - 1)
                            wait(pe, s_xte, t + 1)
                            wait(pe, s_sl4, t - 1)
                            for c in range(C):
                                last = nc.tensor.matmul(Ge[a][:, :], xT[:, a, c, :], w3m[:, bass.ds(e, 1), c, :],
                                                        start=c == 0, stop=c == C - 1)
                            last.then_inc(s_g, 1)
                        xtr(t + 1, k + 1)
                        if on4(t - 1):
                            wait(pe, s_he, t)
                            wait(pe, s_hTe, t - 1)
                            for c in range(HC):
                                last = nc.tensor.transpose(HT[:, c, :], he[:, b, c * P:(c + 1) * P], ident[:, :])
                            last.then_inc(s_hT, 1)
                        if on4(t):
                            wait(pe, s_he, t - 1)
                            for c in range(C):
                                last = nc.tensor.matmul(Ue[a][:, :], xT[:, a, c, :], w1m[:, bass.ds(e, 1), c, :],
                                                        start=c == 0, stop=c == C - 1)
                            last.then_inc(s_u, 1)
                        if on4(t - 1):
                            e = pe.value_load(tile_expert[0:1, bass.ds(t - 1, 1)], min_val=0, max_val=E - 1)
                            wait(pe, s_hTe, t)
                            wait(pe, s_yc, t - 2)
                            for c in range(HC):
                                last = nc.tensor.matmul(Ye[b][:, :], hT[:, b, c, :], w2m[:, bass.ds(e, 1), c, :],
                                                        start=c == 0, stop=c == HC - 1)
                            last.then_inc(s_ye, 1)

                    steps(pe, *RANGE4, body)

                @block.scalar
                def _(act):
                    def body(t, k):
                        if on4(t):
                            wait(act, s_g, t + 1)
                            wait(act, s_he, t - 1)
                            nc.scalar.activation(sg4[:, k % 2, :], Ge[k % 2][:, :], ACT.Silu).then_inc(s_sl4, 1)
                        if on4(t - 1):
                            wait(act, s_hT, t)
                            wait(act, s_ye, t - 2)
                            nc.scalar.copy(hT[:, (k - 1) % 2, :, :], HT[:, :, :]).then_inc(s_hTe, 1)

                    steps(act, *RANGE4, body)

                @block.vector
                def _(dve):
                    def body(t, k):
                        if on4(t + 1):
                            wait(dve, s_xt, t + 2)
                            wait(dve, s_u, t)
                            nc.vector.tensor_copy(xT[:, (k + 1) % 2, :, :], XT[:, :, :]).then_inc(s_xte, 1)
                        if on4(t):
                            wait(dve, s_sl4, t + 1)
                            wait(dve, s_u, t + 1)
                            wait(dve, s_hT, t - 1)
                            nc.vector.tensor_tensor(he[:, k % 2, :], Ue[k % 2][:, :], sg4[:, k % 2, :],
                                                    ALU.mult).then_inc(s_he, 1)
                        if on4(t - 1):
                            j = (k - 1) % 2
                            wait(dve, s_ye, t)
                            wait(dve, s_yst[j], (t - 1 - j) * 8)
                            nc.vector.tensor_copy(ye[:, j, :], Ye[j][:, :]).then_inc(s_yc, 1)

                    steps(dve, *RANGE4, body)

                @block.gpsimd
                def _(pool):
                    pool.dma_start(wup[:, :, :], W_exp.rearrange("(c p) h -> p c h", p=P)).then_inc(s_bl, 16)
                    pool.dma_start(brow[:, 0, :], b_exp.rearrange("(o h) -> o h", o=1)).then_inc(s_bl, 16)
                    pool.dma_start(brow[:, 1, :], up_bias.rearrange("(o h) -> o h", o=1)).then_inc(s_bl, 16)
                    pool.dma_start(wdT[:, :, :], WconT.rearrange("(c p) h -> p c h", p=P)).then_inc(s_bl, 16)
                    pool.dma_start(wl[:, :, :], WlT.rearrange("(c p) d -> p c d", p=P)).then_inc(s_bl, 16)
                    plan = [(up_w, s, False) for s in range(NST)] + [(dn_w, s, True) for s in reversed(range(NST))]
                    count = [0]

                    def load(n):
                        w, s, _ = plan[n]
                        pool.dma_start(bw[:, n % 2, :, :].rearrange("p k f -> p (k f)"),
                                       w[s].rearrange("k i j -> (k i j)").unsqueeze(0).broadcast_to([P, 2 * F])
                                       ).then_inc(s_bw[n % 2], 16)

                    def link(ins):
                        count[0] += 1
                        ins.then_inc(s_bo, 1)
                        pool.wait_ge(s_bo, count[0])

                    def stage(row, parts, n, flip):
                        s = plan[n][1]
                        st = 2 ** s
                        v = row.rearrange("p (k i s) -> p k i s", i=2, s=st)
                        a, b = v[:, :, 0, :], v[:, :, 1, :]
                        w = bw[0:parts, n % 2, :, :].rearrange("p (k s) f -> p k s f", s=st)
                        t = [bt[0:parts, j, :].rearrange("p (k s) -> p k s", s=st) for j in range(2)]
                        y = by[0:parts, 0:F // 2].rearrange("p (k s) -> p k s", s=st)
                        z = by[0:parts, F // 2:F].rearrange("p (k s) -> p k s", s=st)
                        aa, ab, ba, bb = (0, 2, 1, 3) if flip else (0, 1, 2, 3)
                        TT = nc.gpsimd.tensor_tensor
                        TT(out=t[0], in0=w[:, :, :, aa], in1=a, op=ALU.mult).then_inc(s_bo, 1)
                        TT(out=t[1], in0=w[:, :, :, ab], in1=b, op=ALU.mult).then_inc(s_bo, 1)
                        TT(out=y, in0=w[:, :, :, ba], in1=a, op=ALU.mult).then_inc(s_bo, 1)
                        count[0] += 3
                        link(TT(out=z, in0=w[:, :, :, bb], in1=b, op=ALU.mult))
                        TT(out=a, in0=t[0], in1=t[1], op=ALU.add).then_inc(s_bo, 1)
                        count[0] += 1
                        link(TT(out=b, in0=y, in1=z, op=ALU.add))

                    load(0)
                    load(1)
                    pool.wait_ge(s_bl, 80)
                    for n in range(2 * NST):
                        pool.wait_ge(s_bw[n % 2], 16 * (n // 2 + 1))
                        dst, flip = (wdT, True) if plan[n][2] else (wup, False)
                        for c in range(C):
                            stage(dst[:, c, :], P, n, flip)
                        if not flip:
                            stage(brow[:, 0, :], 1, n, False)
                        if n + 2 < 2 * NST:
                            load(n + 2)
                    link(nc.gpsimd.tensor_tensor(out=brow[:, 2, :], in0=brow[:, 0, :], in1=brow[:, 1, :], op=ALU.add))
                    pool.dma_start(bu_d[:, :], brow[:, 2, :]).then_inc(s_bs, 16)
                    pool.wait_ge(s_bs, 16)
                    pool.dma_start(bup[:, :], bu_d.rearrange("o (b p) -> p (o b)", p=P),
                                   allow_slow_non_contiguous=True).then_inc(s_bs, 16)
                    pool.wait_ge(s_bs, 32)

        with ExitStack() as ph:
            sb = lambda name, shape, dt=F32: ph.enter_context(nc.sbuf_tensor(name, shape, dt))
            ax = sb("ax", [P, 4, D])
            cx = sb("cx", [P, 4, D])
            yg = sb("yg", [P, 4, TOPK, D])
            ix5 = sb("ix5", [P, 4, TOPK, 1], I32)
            x2 = sb("x2", [P, 4, D])
            st5 = sb("st5", [P, 4, 6])
            mv5 = sb("mv5", [P, 4, 2])
            rs5 = sb("rs5", [P, 4, 2])
            c5 = sb("c5", [P, 4, D])
            cT = sb("cT", [P, 4, C, P])
            cw = sb("cw", [P, 2, C, P])
            qT = sb("qT", [P, 2, C, P])
            dots = sb("dots", [P, D])
            rr = sb("rr", [P, 4, 1])
            m5 = sb("m5", [P, 4, 2])
            nm5 = sb("nm5", [P, 4, 2])
            pa = sb("pa", [P, 2, P])
            ps = sb("ps", [P, 4, 2])
            aT = sb("aT", [P, 2, P])
            gmax = sb("gmax", [P, 4, 1])
            be = sb("be", [P, 4, 1])
            q2 = sb("q2", [P, 4, 4])
            wz = sb("wz", [P, 2, C, D])
            uT = sb("uT", [P, 2, C, P])
            vT = sb("vT", [P, 2, C, P])
            x3 = sb("x3", [P, 2, D])
            wcq = sb("wcq", [P, 2, C])
            wcb = sb("wcb", [P, D])
            bias3 = sb("bias3", [P, 4])
            blb = sb("blb", [P, D])
            T5 = ph.enter_context(nc.psum_tensor("T5", [P, 2 * C, P], F32))
            S5 = ph.enter_context(nc.psum_tensor("S5", [P, P], F32))
            A5 = ph.enter_context(nc.psum_tensor("A5", [P, P], F32))
            U5 = ph.enter_context(nc.psum_tensor("U5", [P, C, P], F32))
            Q5 = ph.enter_context(nc.psum_tensor("Q5", [P, 4], F32))
            Z5 = [ph.enter_context(nc.psum_tensor(f"Z5{i}", [P, D], F32)) for i in range(2)]
            s_w5, s_b5 = sem("s_w5"), sem("s_b5")
            s_l5, s_g5 = sems("s_l5", 4), sems("s_g5", 4)
            s_x3st = sems("s_x3st", 2)
            (s_ix5, s_y1, s_x2, s_mv5, s_rs5, s_c5, s_t5, s_q5, s_ct, s_cw, s_dt, s_rr, s_s5, s_m5, s_nm,
             s_M, s_gm, s_p5, s_pr5, s_an, s_a5, s_at, s_be, s_Q, s_qc, s_qr, s_qn, s_wz, s_u5, s_ut, s_vt, s_z, s_zc,
             s_x3) = (sem(f"s5_{i}") for i in range(34))
            RANGE5 = (-4, NB + 3, 4, NB - 4, 4)
            with nc.Block() as block:
                @block.sync
                def _(sp):
                    as_col = lambda a: a.rearrange("(c p) -> p c", p=P)
                    as_rows = lambda a, n: a.rearrange("(o d) -> o d", o=1).broadcast_to([P, n])
                    sp.dma_start(wcq[:, 0, :], as_col(w_cq), allow_slow_non_contiguous=True).then_inc(s_w5, 16)
                    sp.dma_start(wcq[:, 1, :], as_col(w_q), allow_slow_non_contiguous=True).then_inc(s_w5, 16)
                    sp.dma_start(wcb[:, :], as_rows(w_c, D)).then_inc(s_w5, 16)
                    sp.dma_start(blb[:, :], as_rows(b_l, D)).then_inc(s_w5, 16)
                    for i, b in enumerate((b_cq, b_c, b_q)):
                        sp.dma_start(bias3[:, i:i + 1], as_rows(b, 1)).then_inc(s_w5, 16)

                    def body(t, k):
                        if on(t + 4):
                            wait(sp, s_x3, t + 1)
                            sp.dma_start(ax[:, k, :], acc_d[t + 4, :, :]).then_inc(s_l5[k], 16)
                            sp.dma_start(cx[:, k, :], ctx_in[t + 4, :, :]).then_inc(s_l5[k], 16)
                        if on(t):
                            wait(sp, s_x3, t + 1)
                            sp.dma_start(x3_d[t, :, :], x3[:, k % 2, :]).then_inc(s_x3st[k % 2], 16)

                    steps(sp, *RANGE5, body)
                    for j in range(2):
                        wait(sp, s_x3st[j], 16 * (NB // 2))

                @block.gpsimd
                def _(pool):
                    pool.wait_ge(s_w5, 16 * 7)
                    nc.gpsimd.tensor_tensor(out=bias3[:, 3:4], in0=bias3[:, 0:1], in1=bias3[:, 1:2],
                                            op=ALU.add).then_inc(s_b5, 1)
                    pool.wait_ge(s_b5, 1)
                    nc.gpsimd.tensor_tensor(out=bias3[:, 0:1], in0=bias3[:, 3:4], in1=bias3[:, 2:3],
                                            op=ALU.add).then_inc(s_b5, 1)

                    def gather(t, k):
                        if on(t):
                            wait(pool, s_x2, t - 3)
                            take_wait(nc.gpsimd)
                            nc.gpsimd.tensor_copy(ix5[:, k, :, :], slot[:, :, bass.ds(t, 1)]).then_inc(s_ix5, 1)
                            wait(pool, s_ix5, t + 1)
                            for j in range(TOPK):
                                take_wait(nc.gpsimd)
                                nc.gpsimd.indirect_dma_start(
                                    out=yg[:, k, j, :], out_offset=None, in_=ys_d[:, :],
                                    in_offset=bass.IndirectOffsetOnAxis(ap=ix5[:, k, j, :], axis=0)
                                ).then_inc(s_g5[k], 16)

                    def body(t, k):
                        gather(t + 4, k)
                        a = (k + 2) % 4
                        if on(t + 2):
                            wait(pool, s_mv5, 2 * t + 6)
                            nc.gpsimd.tensor_tensor(out=rs5[:, a, 0:1], in0=mv5[:, a, 1:2], in1=epsc[:, :], op=ALU.add).then_inc(s_rs5, 1)
                            wait(pool, s_rs5, 2 * t + 5)
                            nc.gpsimd.tensor_tensor(out=rs5[:, a, 1:2], in0=rs5[:, a, 0:1], in1=mhalf[:, :],
                                                    op=ALU.pow).then_inc(s_rs5, 1)
                        if on(t + 1):
                            wait(pool, s_M, t + 2)
                            a = (k + 1) % 4
                            take_wait(nc.gpsimd)
                            nc.gpsimd.partition_all_reduce(gmax[:, a, :], m5[:, a, 1:2], P, bass.bass_isa.ReduceOp.max).then_inc(s_gm, 1)

                    steps(pool, *RANGE5, body)

                @block.vector
                def _(dve):
                    TT, TS, STT = nc.vector.tensor_tensor, nc.vector.tensor_scalar, nc.vector.scalar_tensor_tensor
                    dve.wait_ge(s_b5, 2)

                    def residual(t, k):
                        if on(t):
                            wait(dve, s_l5[k], (t - k) * 8 + 32)
                            wait(dve, s_g5[k], (t - k) * 8 + 32)
                            STT(ax[:, k, :], yg[:, k, 0, :], gate[:, 0, bass.ds(t, 1)], ax[:, k, :],
                                ALU.mult, ALU.add).then_inc(s_y1, 1)
                            wait(dve, s_y1, t + 1)
                            STT(x2[:, k, :], yg[:, k, 1, :], gate[:, 1, bass.ds(t, 1)], ax[:, k, :],
                                ALU.mult, ALU.add).then_inc(s_x2, 1)
                            wait(dve, s_x2, t + 1)
                            nc.vector.bn_stats(st5[:, k, :], x2[:, k, :]).then_inc(s_mv5, 1)
                            wait(dve, s_mv5, 2 * t + 1)
                            take_wait(nc.vector)
                            nc.vector.bn_aggr(mv5[:, k, :], st5[:, k, :]).then_inc(s_mv5, 1)

                    def normed(t, k):
                        if on(t):
                            wait(dve, s_rs5, 2 * t + 2)
                            wait(dve, s_z, t - 3)
                            TS(c5[:, k, :], x2[:, k, :], mv5[:, k, 0:1], rs5[:, k, 1:2],
                               ALU.subtract, ALU.mult).then_inc(s_c5, 1)
                            wait(dve, s_c5, t + 1)
                            wait(dve, s_dt, t)
                            STT(dots[:, :], c5[:, k, :], 1.0, wcb[:, :], ALU.mult, ALU.mult,
                                accum_out=rr[:, k, :]).then_inc(s_dt, 1)

                    def scaled(t, k):
                        if on(t):
                            wait(dve, s_ct, t + 1)
                            wait(dve, s_s5, t - 1)
                            for c in range(C):
                                TS(cw[:, k % 2, c, :], cT[:, k, c, :], wcq[:, 0, c:c + 1], wcq[:, 1, c:c + 1],
                                   ALU.mult, ALU.add).then_inc(s_cw, 1)

                    def row_max(t, k):
                        if on(t):
                            wait(dve, s_s5, t + 1)
                            wait(dve, s_dt, t + 1)
                            nc.vector.tensor_reduce(m5[:, k, 0:1], S5[:, :], AX.X, ALU.max).then_inc(s_m5, 1)
                            wait(dve, s_m5, t + 1)
                            TS(nm5[:, k, 0:1], m5[:, k, 0:1], -1.0, None, ALU.mult).then_inc(s_nm, 1)
                            STT(m5[:, k, 1:2], m5[:, k, 0:1], bias3[:, 0:1], rr[:, k, :],
                                ALU.add, ALU.add).then_inc(s_M, 1)

                    def weights(t, k):
                        if on(t):
                            wait(dve, s_p5, t + 1)
                            nc.vector.reciprocal(ps[:, k, 1:2], ps[:, k, 0:1]).then_inc(s_pr5, 1)
                            wait(dve, s_pr5, t + 1)
                            TS(pa[:, k % 2, :], pa[:, k % 2, :], ps[:, k, 1:2], None, ALU.mult).then_inc(s_an, 1)

                    def gmax_neg(t, k):
                        if on(t):
                            wait(dve, s_gm, t + 1)
                            TS(nm5[:, k, 1:2], gmax[:, k, :], -1.0, None, ALU.mult).then_inc(s_qn, 1)

                    def q2c(t, k):
                        if on(t):
                            wait(dve, s_Q, t + 1)
                            TS(q2[:, k, 0:3], Q5[:, 0:3], 1.0, None, ALU.mult).then_inc(s_qc, 1)
                            wait(dve, s_qc, t + 1)
                            nc.vector.reciprocal(q2[:, k, 3:4], q2[:, k, 2:3]).then_inc(s_qr, 1)
                            wait(dve, s_qr, 2 * t + 1)
                            TS(q2[:, k, 0:2], q2[:, k, 0:2], q2[:, k, 3:4], None, ALU.mult).then_inc(s_qr, 1)
                            wait(dve, s_qr, 2 * t + 2)
                            wait(dve, s_z, t - 1)
                            for c in range(C):
                                STT(wz[:, k % 2, c, :], wl[:, 3 * C + c, :], q2[:, k, c:c + 1], wl[:, c, :],
                                    ALU.mult, ALU.add).then_inc(s_wz, 1)

                    def attended(t, k):
                        if on(t):
                            wait(dve, s_ut, t + 1)
                            wait(dve, s_z, t - 1)
                            TT(vT[:, k % 2, :, :], cT[:, k, :, :], uT[:, k % 2, :, :], ALU.mult).then_inc(s_vt, 1)

                    def finish(t, k):
                        if on(t):
                            wait(dve, s_z, t + 1)
                            wait(dve, s_x3st[k % 2], (t - k % 2) * 8)
                            TT(x3[:, k % 2, :], Z5[k % 2][:, :], x2[:, k, :], ALU.add).then_inc(s_zc, 1)
                            wait(dve, s_zc, t + 1)
                            TT(x3[:, k % 2, :], x3[:, k % 2, :], blb[:, :], ALU.add).then_inc(s_x3, 1)

                    def body(t, k):
                        q = lambda n: (k + n) % 4
                        normed(t + 2, q(2))
                        scaled(t + 2, q(2))
                        weights(t + 1, q(1))
                        gmax_neg(t + 1, q(1))
                        attended(t + 1, q(1))
                        q2c(t + 1, q(1))
                        row_max(t + 2, q(2))
                        residual(t + 3, q(3))
                        finish(t, k)

                    steps(dve, *RANGE5, body)

                @block.scalar
                def _(act):
                    def body(t, k):
                        if on(t + 2):
                            a = (k + 2) % 4
                            wait(act, s_t5, t + 3)
                            wait(act, s_vt, t - 1)
                            wait(act, s_s5, t + 1)
                            nc.scalar.copy(cT[:, a, :, :], T5[:, 0:C, :]).then_inc(s_ct, 1)
                            nc.scalar.copy(qT[:, a % 2, :, :], T5[:, C:2 * C, :]).then_inc(s_q5, 1)
                        if on(t + 1):
                            a = (k + 1) % 4
                            wait(act, s_at, t)
                            wait(act, s_a5, t + 2)
                            nc.scalar.copy(aT[:, a % 2, :], A5[:, :]).then_inc(s_at, 1)
                            wait(act, s_qn, t + 2)
                            nc.scalar.activation(be[:, a, :], m5[:, a, 1:2], ACT.Exp, bias=nm5[:, a, 1:2]).then_inc(s_be, 1)
                            wait(act, s_u5, t + 2)
                            wait(act, s_z, t)
                            nc.scalar.copy(uT[:, a % 2, :, :], U5[:, :, :]).then_inc(s_ut, 1)
                        if on(t + 2):
                            a = (k + 2) % 4
                            wait(act, s_nm, t + 3)
                            wait(act, s_a5, t + 1)
                            nc.scalar.activation(pa[:, a % 2, :], S5[:, :], ACT.Exp, bias=nm5[:, a, 0:1],
                                                 accum_out=ps[:, a, 0:1]).then_inc(s_p5, 1)

                    steps(act, *RANGE5, body)

                @block.tensor
                def _(pe):
                    def body(t, k):
                        q = lambda n: (k + n) % 4
                        if on(t + 2):
                            a = q(2)
                            wait(pe, s_l5[a], (t + 2 - a) * 8 + 32)
                            wait(pe, s_c5, t + 3)
                            wait(pe, s_q5, t + 2)
                            for c in range(C):
                                nc.tensor.transpose(T5[:, c, :], c5[:, a, c * P:(c + 1) * P], ident[:, :])
                            for c in range(C):
                                last = nc.tensor.transpose(T5[:, C + c, :], cx[:, a, c * P:(c + 1) * P], ident[:, :])
                            last.then_inc(s_t5, 1)
                        if on(t + 1):
                            a = q(1)
                            wait(pe, s_an, t + 2)
                            wait(pe, s_at, t + 1)
                            nc.tensor.transpose(A5[:, :], pa[:, a % 2, :], ident[:, :]).then_inc(s_a5, 1)
                        if on(t):
                            wait(pe, s_wz, 2 * t + 2)
                            wait(pe, s_zc, t - 1)
                            for c in range(C):
                                nc.tensor.matmul(Z5[k % 2][:, :], cT[:, k, c, :], wz[:, k % 2, c, :],
                                                 start=c == 0, stop=False)
                            for c in range(C):
                                nc.tensor.matmul(Z5[k % 2][:, :], uT[:, k % 2, c, :], wl[:, C + c, :],
                                                 start=False, stop=False)
                        if on(t + 1):
                            a = q(1)
                            wait(pe, s_at, t + 2)
                            wait(pe, s_ut, t + 1)
                            for c in range(C):
                                last = nc.tensor.matmul(U5[:, c, :], cx[:, a, c * P:(c + 1) * P], aT[:, a % 2, :],
                                                        start=True, stop=True)
                            last.then_inc(s_u5, 1)
                        if on(t):
                            wait(pe, s_vt, t + 1)
                            for c in range(C):
                                last = nc.tensor.matmul(Z5[k % 2][:, :], vT[:, k % 2, c, :], wl[:, 2 * C + c, :],
                                                        start=False, stop=c == C - 1)
                            last.then_inc(s_z, 1)
                        if on(t + 1):
                            a = q(1)
                            wait(pe, s_be, t + 2)
                            wait(pe, s_qc, t + 1)
                            for c in range(C):
                                nc.tensor.matmul(Q5[:, c:c + 1], c5[:, a, c * P:(c + 1) * P], be[:, a, :],
                                                 start=True, stop=True)
                            nc.tensor.matmul(Q5[:, C:C + 1], ones[:, :], be[:, a, :], start=True, stop=True
                                             ).then_inc(s_Q, 1)
                        if on(t + 2):
                            a = q(2)
                            wait(pe, s_cw, 2 * t + 6)
                            wait(pe, s_q5, t + 3)
                            wait(pe, s_p5, t + 2)
                            for c in range(C):
                                last = nc.tensor.matmul(S5[:, :], cw[:, a % 2, c, :], qT[:, a % 2, c, :],
                                                        start=c == 0, stop=c == C - 1)
                            last.then_inc(s_s5, 1)

                    steps(pe, *RANGE5, body)

        with ExitStack() as ph:
            sb = lambda name, shape, dt=F32: ph.enter_context(nc.sbuf_tensor(name, shape, dt))
            wdn = sb("wdn", [P, FC, D])
            x6 = sb("x6", [P, 4, 2, D])
            st6 = sb("st6", [P, 4, 2, 6])
            mv6 = sb("mv6", [P, 4, 2, 2])
            rs6 = sb("rs6", [P, 4, 2, 2])
            n6 = sb("n6", [P, 2, 2, D])
            T6s = sb("T6s", [P, 2, C, 2, P])
            g6 = sb("g6", [P, 2, FC, 2 * P])
            o6 = sb("o6", [P, 2, 2, D])
            bo6 = sb("bo6", [P, 3, D])
            T6 = [ph.enter_context(nc.psum_tensor(f"T6{i}", [P, C, P], F32)) for i in range(2)]
            H6 = [ph.enter_context(nc.psum_tensor(f"H6{i}", [P, 2 * P], F32)) for i in range(4)]
            Y6 = [ph.enter_context(nc.psum_tensor(f"Y6{i}", [P, D], F32)) for i in range(2)]
            s_w6, s_wt6, s_we6, s_b6 = sem("s_w6"), sem("s_wt6"), sem("s_we6"), sem("s_b6")
            s_l6, BASE_L = s_ld, 32 * (NB // 4)
            s_mv6, s_rs6, s_n6, s_t6, s_e6, s_h6, s_g6, s_y6, s_a6, s_o6 = (
                sem(f"s6_{i}") for i in range(10))
            s_ost, BASE_S = s_x1st, 16 * (NB // 2)
            RANGE6 = (-4, NP + 1, 4, NP - 4, 4)
            with nc.Block() as block:
                @block.sync
                def _(sp):
                    sp.dma_start(bo6[:, 0, :], b_con.rearrange("(o d) -> o d", o=1).broadcast_to([P, D])).then_inc(s_w6, 16)
                    sp.dma_start(bo6[:, 1, :], dn_bias.rearrange("(o d) -> o d", o=1).broadcast_to([P, D])).then_inc(s_w6, 16)

                    def body(t, k):
                        if onp(t + 4):
                            wait(sp, s_o6, 2 * t + 2)
                            sp.dma_start(x6[:, k, :, :], x3_d[bass.ds((t + 4) * 2, 2), :, :].rearrange("t p n -> p t n")
                                         ).then_inc(s_l6[k], 16)
                        if onp(t):
                            wait(sp, s_o6, 2 * t + 2)
                            sp.dma_start(out[bass.ds(t * 2, 2), :, :].rearrange("t p n -> p t n"),
                                         o6[:, k % 2, :, :]).then_inc(s_ost[k % 2], 16)

                    steps(sp, *RANGE6, body)
                    for j in range(2):
                        wait(sp, s_ost[j], 16 * (NP // 2) + BASE_S)

                @block.gpsimd
                def _(pool):
                    pool.wait_ge(s_w6, 32)
                    nc.gpsimd.tensor_tensor(out=bo6[:, 2, :], in0=bo6[:, 0, :], in1=bo6[:, 1, :], op=ALU.add).then_inc(s_b6, 1)

                    def body(t, k):
                        if onp(t + 2):
                            a = (k + 2) % 4
                            wait(pool, s_mv6, 4 * t + 12)
                            nc.gpsimd.tensor_tensor(out=rs6[:, a, :, 0:1], in0=mv6[:, a, :, 1:2],
                                                    in1=epsc[:, :].unsqueeze(1).broadcast_to([P, 2, 1]), op=ALU.add).then_inc(s_rs6, 1)
                            wait(pool, s_rs6, 2 * t + 5)
                            nc.gpsimd.tensor_tensor(out=rs6[:, a, :, 1:2], in0=rs6[:, a, :, 0:1],
                                                    in1=mhalf[:, :].unsqueeze(1).broadcast_to([P, 2, 1]),
                                                    op=ALU.pow).then_inc(s_rs6, 1)

                    steps(pool, *RANGE6, body)

                @block.vector
                def _(dve):
                    for i in range(2 * FC):
                        c, b = i // FC, i % FC
                        wait(dve, s_wt6, i + 1)
                        nc.vector.tensor_copy(wdn[:, b, c * P:(c + 1) * P], T6[i % 2][:, 0, :]).then_inc(s_we6, 1)
                    dve.wait_ge(s_b6, 1)

                    def body(t, k):
                        q = lambda n: (k + n) % 4
                        if onp(t + 2):
                            a = q(2)
                            wait(dve, s_l6[a], (t + 2 - a) * 4 + 16 + BASE_L)
                            for j in range(2):
                                nc.vector.bn_stats(st6[:, a, j, :], x6[:, a, j, :]).then_inc(s_mv6, 1)
                            for j in range(2):
                                wait(dve, s_mv6, 4 * t + 9 + j)
                                take_wait(nc.vector)
                                nc.vector.bn_aggr(mv6[:, a, j, :], st6[:, a, j, :]).then_inc(s_mv6, 1)
                        if onp(t + 1):
                            a = q(1)
                            wait(dve, s_rs6, 2 * t + 4)
                            wait(dve, s_t6, 2 * t)
                            for j in range(2):
                                nc.vector.tensor_scalar(n6[:, a % 2, j, :], x6[:, a, j, :], mv6[:, a, j, 0:1],
                                                        rs6[:, a, j, 1:2], ALU.subtract, ALU.mult).then_inc(s_n6, 1)
                            for j in range(2):
                                wait(dve, s_t6, 2 * t + 3 + j)
                                wait(dve, s_h6, FC * t)
                                nc.vector.tensor_copy(T6s[:, a % 2, :, j, :], T6[j][:, :, :]).then_inc(s_e6, 1)
                        if onp(t - 1):
                            a = q(-1)
                            for j in range(2):
                                wait(dve, s_y6, 2 * t - 1 + j)
                                wait(dve, s_ost[a % 2], (t - 1 - a % 2) * 8 + BASE_S)
                                nc.vector.tensor_tensor(o6[:, a % 2, j, :], Y6[j][:, :], x6[:, a, j, :],
                                                        ALU.add).then_inc(s_a6, 1)
                                wait(dve, s_a6, 2 * t - 1 + j)
                                nc.vector.tensor_tensor(o6[:, a % 2, j, :], o6[:, a % 2, j, :], bo6[:, 2, :],
                                                        ALU.add).then_inc(s_o6, 1)

                    steps(dve, *RANGE6, body)

                @block.scalar
                def _(act):
                    def body(t, k):
                        if onp(t):
                            for b in range(FC):
                                wait(act, s_h6, FC * t + b + 1)
                                wait(act, s_y6, 2 * t - 2)
                                nc.scalar.activation(g6[:, k % 2, b, :], H6[b % 4][:, :], ACT.Gelu,
                                                     bias=bup[:, b:b + 1]).then_inc(s_g6, 1)

                    steps(act, *RANGE6, body)

                @block.tensor
                def _(pe):
                    for i in range(2 * FC):
                        c, b = i // FC, i % FC
                        wait(pe, s_we6, i - 1)
                        nc.tensor.transpose(T6[i % 2][:, 0, :], wdT[:, c, b * P:(b + 1) * P], ident[:, :]).then_inc(s_wt6, 1)
                    pe.wait_ge(s_we6, 2 * FC)

                    def tr(t, k):
                        if onp(t):
                            wait(pe, s_n6, 2 * t + 2)
                            wait(pe, s_e6, 2 * t)
                            for j in range(2):
                                for c in range(C):
                                    last = nc.tensor.transpose(T6[j][:, c, :], n6[:, k % 2, j, c * P:(c + 1) * P], ident[:, :])
                                last.then_inc(s_t6, 1)

                    def up(t, k, b):
                        if onp(t):
                            wait(pe, s_e6, 2 * t + 2)
                            wait(pe, s_g6, FC * t + b - 3)
                            for c in range(C):
                                last = nc.tensor.matmul(H6[b % 4][:, :], wup[:, c, b * P:(b + 1) * P],
                                                        T6s[:, k % 2, c, :, :], start=c == 0, stop=c == C - 1)
                            last.then_inc(s_h6, 1)

                    def down(t, k, j, half):
                        if onp(t):
                            wait(pe, s_g6, FC * t + FC)
                            wait(pe, s_a6, 2 * t - 1 + j)
                            for b in range(half * FC // 2, (half + 1) * FC // 2):
                                last = nc.tensor.matmul(Y6[j][:, :], g6[:, k % 2, b, j * P:(j + 1) * P], wdn[:, b, :],
                                                        start=b == 0, stop=b == FC - 1)
                            if half:
                                last.then_inc(s_y6, 1)

                    def body(t, k):
                        tr(t + 1, k + 1)
                        up(t, k, 0)
                        up(t, k, 1)
                        down(t - 1, k + 1, 0, 0)
                        up(t, k, 2)
                        up(t, k, 3)
                        down(t - 1, k + 1, 0, 1)
                        up(t, k, 4)
                        up(t, k, 5)
                        down(t - 1, k + 1, 1, 0)
                        up(t, k, 6)
                        up(t, k, 7)
                        down(t - 1, k + 1, 1, 1)

                    steps(pe, *RANGE6, body)


_INS = ['x', 'ctx_1024', 'L0_ffn_Wr', 'L0_ffn_rb', 'L0_ffn_W1', 'L0_ffn_W2', 'L0_ffn_W3', 'L0_ffn_Ws1', 'L0_ffn_Ws2',
        'L0_ffn_Ws3', 'L1_xattn_w_cq', 'L1_xattn_b_cq', 'L1_xattn_w_c', 'L1_xattn_b_c', 'L1_xattn_w_q', 'L1_xattn_b_q',
        'L1_xattn_W_l', 'L1_xattn_b_l', 'L1_ffn_W_exp', 'L1_ffn_b_exp', 'L1_ffn_up_weights', 'L1_ffn_up_bias',
        'L1_ffn_down_weights', 'L1_ffn_W_con', 'L1_ffn_b_con', 'L1_ffn_down_bias']
_TRANSPOSED = ('L1_xattn_W_l', 'L1_ffn_W_con')


def kernel(**inputs):
    import numpy as _np
    import concourse.bacc as _bacc
    from concourse import mybir as _mybir
    from concourse.bass_utils import run_bass_kernel_spmd as _run

    nc = _bacc.Bacc("TRN2", target_bir_lowering=False, num_devices=1)
    arrays, args = {}, []
    for name in _INS:
        a = _np.asarray(inputs[name])
        a = _np.ascontiguousarray(a.T if name in _TRANSPOSED else a)
        if a.ndim == 0:
            a = a.reshape(1)
        arrays[f"in_{name}_dram"] = a
        args.append(nc.dram_tensor(f"in_{name}_dram", a.shape, _mybir.dt.from_np(a.dtype), kind="ExternalInput").ap())
    shape = tuple(inputs['x'].shape)
    args.append(nc.dram_tensor("out_dram", shape, _mybir.dt.float32, kind="ExternalOutput").ap())
    build_program(nc, *args)
    r = _run(nc, [arrays], core_ids=[0])
    return r.results[0]["out_dram"]
```

```python
import concourse.bass as bass
from concourse import mybir
from contextlib import ExitStack

F32 = mybir.dt.float32
I32 = mybir.dt.int32
ALU = mybir.AluOpType
ACT = mybir.ActivationFunctionType
AX = mybir.AxisListType
MASK_AT, GATE_AT = 16, 22

P = 128
D = 256
C = D // P
EPS = 1e-5


def due(count):
    return not isinstance(count, int) or count > 0


def steps(eng, first, last, lo, hi, unroll, body):
    assert lo % unroll == 0 and hi % unroll == 0
    for t in range(first, lo):
        body(t, t % unroll)
    if hi > lo:
        with eng.Fori(lo // unroll, hi // unroll) as i:
            for u in range(unroll):
                body(i * unroll + u, u)
    for t in range(hi, last):
        body(t, t % unroll)


def stage_on(n):
    return lambda t: not isinstance(t, int) or 0 <= t < n


def upto(t, n):
    return min(t, n) if isinstance(t, int) else t


def build_program(nc, x, ctx_in, Wr, rb, W1, W2, W3, Ws1, Ws2, Ws3, w_cq, b_cq, w_c, b_c, w_q, b_q,
                  WlT, b_l, W_exp, b_exp, up_w, up_bias, dn_w, WconT, b_con, dn_bias, out):
    NB = x.shape[0]
    E = W1.shape[0]
    H = W1.shape[2]
    HC = H // P
    HS = Ws1.shape[1]
    HSC = HS // P
    NH = 16
    DH = D // NH
    HH = NH // C
    TOPK = 2
    NT = NB * TOPK + E
    F = W_exp.shape[1]
    FC = F // P
    NST = up_w.shape[0]
    ctx = ExitStack()
    sem = lambda name: ctx.enter_context(nc.semaphore(name))
    sems = lambda name, n: [sem(f"{name}{i}") for i in range(n)]
    per = lambda name, shape, dt=F32: ctx.enter_context(nc.sbuf_tensor(name, shape, dt))

    def dram(name, shape):
        return nc.dram_tensor(name, shape, F32, kind="Internal").ap()

    x1_d = dram("x1_d", (NB, P, D))
    h1_d = dram("h1_d", (NB, P, D))
    h1T_d = dram("h1T_d", (NB, P, C * P))
    acc_d = dram("acc_d", (NB, P, D))
    xs_d = dram("xs_d", (NT * P, D))
    ys_d = dram("ys_d", (NT * P, D))
    x3_d = dram("x3_d", (NB, P, D))
    bu_d = dram("bu_d", (1, F))

    with ctx:
        ident = per("ident", [P, P])
        mhalf = per("mhalf", [P, 1])
        epsc = per("epsc", [P, 1])
        spare = per("spare", [1, 2, 32])
        ones = per("ones", [P, P])
        logits = per("logits", [P, NB, E])
        gate = per("gate", [P, TOPK, NB])
        slot = per("slot", [P, TOPK, NB], I32)
        tile_expert = per("tile_expert", [1, NT], I32)
        w1m = per("w1m", [P, E, C, H])
        w3m = per("w3m", [P, E, C, H])
        w2m = per("w2m", [P, E, HC, D])
        ws1 = per("ws1", [P, C, HS])
        ws3 = per("ws3", [P, C, HS])
        ws2 = per("ws2", [P, HSC, D])

        turn = [0]

        def take_wait(eng):
            turn[0] = (turn[0] + 1) % 32
            if eng is nc.vector:
                eng.memset(spare[:, 0, turn[0]:turn[0] + 1], 0.0)
            else:
                eng.tensor_tensor(out=spare[:, 1, turn[0]:turn[0] + 1], in0=ones[0:1, 0:1], in1=ones[0:1, 0:1], op=ALU.mult)

        s_ws = sem("s_ws")
        s_wm = sem("s_wm")
        s_c = sem("s_c")
        s_zero = sem("s_zero")

        with ExitStack() as ph:
            sb = lambda name, shape, dt=F32: ph.enter_context(nc.sbuf_tensor(name, shape, dt))
            xb = sb("xb", [P, 4, D])
            cb = sb("cb", [P, 4, D])
            xn = sb("xn", [P, 2, D])
            T0 = sb("T0", [P, 2, 2 * C, P])
            bd = sb("bd", [P, 2, C, HH, P])
            hmask = sb("hmask", [P, HH, P])
            pr = sb("pr", [P, C, HH, P])
            pT = sb("pT", [P, C, HH, P])
            va = sb("va", [P, 2, NH, DH + 1])
            mx = sb("mx", [P, C, HH])
            x1 = sb("x1", [P, 2, D])
            h1 = sb("h1", [P, 2, D])
            h1T = sb("h1T", [P, 2, C, P])
            rec = sb("rec", [P, 2, NH, 1])
            st1 = sb("st1", [P, 4, 6])
            mv1 = sb("mv1", [P, 4, 2])
            rs1 = sb("rs1", [P, 4, 2])
            st2 = sb("st2", [P, 4, 6])
            mv2 = sb("mv2", [P, 4, 2])
            rs2 = sb("rs2", [P, 4, 2])
            wr = sb("wr", [P, C, E])
            zeros = sb("zeros", [P, 2, D])
            S = [ph.enter_context(nc.psum_tensor(f"S{c}", [P, HH, P], F32)) for c in range(C)]
            PT = ph.enter_context(nc.psum_tensor("PT", [P, HH, P], F32))
            O = ph.enter_context(nc.psum_tensor("O", [P, 512], F32))
            M = ph.enter_context(nc.psum_tensor("M", [P, 512], F32))
            Ov = O[:, 0:NH * (DH + 1)].rearrange("p (h d) -> p h d", h=NH)

            s_wr = sem("s_wr")
            s_k0 = sem("s_k0")
            s_ld = sems("s_ld", 4)
            s_mv1, s_rs1, s_xn = (sem(n) for n in ("s_mv1", "s_rs1", "s_xn"))
            s_mv2, s_rs2, s_h1 = (sem(n) for n in ("s_mv2", "s_rs2", "s_h1"))
            s_tr1, s_ev1, s_bd, s_va = (sem(n) for n in ("s_tr1", "s_ev1", "s_bd", "s_va"))
            s_sc, s_mx, s_sub, s_exp = (sem(n) for n in ("s_sc", "s_mx", "s_sub", "s_exp"))
            s_pt, s_pte, s_pv = (sem(n) for n in ("s_pt", "s_pte", "s_pv"))
            s_rc, s_nm, s_x1 = (sem(n) for n in ("s_rc", "s_nm", "s_x1"))
            s_h1t, s_h1e, s_lg, s_lc = (sem(n) for n in ("s_h1t", "s_h1e", "s_lg", "s_lc"))
            s_x1st, s_h1st, s_h1Tst = sems("s_x1st", 2), sems("s_h1st", 2), sems("s_h1Tst", 2)
            on = stage_on(NB)
            RANGE = (-4, NB + 1, 4, NB - 4, 4)

            with nc.Block() as block:
                @block.sync
                def _(sp):
                    def load(t, k):
                        if not on(t):
                            return
                        if due(t - 3):
                            sp.wait_ge(s_x1, t - 3)
                        sp.dma_start(xb[:, k, :], x[t, :, :]).then_inc(s_ld[k], 16)
                        sp.dma_start(cb[:, k, :], ctx_in[t, :, :]).then_inc(s_ld[k], 16)

                    def fill(t, k):
                        if on(t):
                            sp.dma_start(xs_d[bass.ds(t * (2 * P), 2 * P), :].rearrange("(a p) d -> p a d", p=P),
                                         zeros[:, :, :]).then_inc(s_zero, 16)
                            if k < 3:
                                e = t // 4 if isinstance(t, int) else bass.ds((t - k) // 4, 1)
                                dst, src, n = ((w3m, W3, C), (w1m, W1, C), (w2m, W2, HC))[k]
                                d, r = dst[:, e, :, :], src[e]
                                if not isinstance(t, int):
                                    d, r = d.rearrange("p o c h -> p (o c) h"), r.rearrange("o k h -> (o k) h")
                                sp.dma_start(d, r.rearrange("(c p) h -> p c h", p=P)).then_inc(s_wm, 16)

                    def body(t, k):
                        load(t + 4, k)
                        fill(t, k)
                        if on(t):
                            sp.wait_ge(s_x1, t + 1)
                            sp.dma_start(x1_d[t, :, :], x1[:, k % 2, :]).then_inc(s_x1st[k % 2], 16)
                        if on(t - 1):
                            j = (k - 1) % 2
                            sp.wait_ge(s_h1, t)
                            sp.dma_start(h1_d[t - 1, :, :], h1[:, j, :]).then_inc(s_h1st[j], 16)
                            sp.wait_ge(s_h1e, t)
                            sp.dma_start(h1T_d[t - 1, :, :], h1T[:, j, :, :]).then_inc(s_h1Tst[j], 16)

                    sp.wait_ge(s_c, 7)
                    sp.dma_start(ws3[:, :, :], Ws3.rearrange("(c p) h -> p c h", p=P)).then_inc(s_ws, 16)
                    sp.dma_start(ws1[:, :, :], Ws1.rearrange("(c p) h -> p c h", p=P)).then_inc(s_ws, 16)
                    sp.dma_start(ws2[:, :, :], Ws2.rearrange("(c p) d -> p c d", p=P)).then_inc(s_ws, 16)
                    sp.dma_start(wr[:, :, :], Wr.rearrange("(c p) e -> p c e", p=P)).then_inc(s_wr, 16)
                    steps(sp, *RANGE, body)
                    for i in range(NB, NT // 2):
                        sp.dma_start(xs_d[2 * P * i:2 * P * (i + 1), :].rearrange("(a p) d -> p a d", p=P),
                                     zeros[:, :, :]).then_inc(s_zero, 16)
                    for j in range(2):
                        sp.wait_ge(s_x1st[j], 16 * (NB // 2))
                        sp.wait_ge(s_h1st[j], 16 * (NB // 2))
                        sp.wait_ge(s_h1Tst[j], 16 * (NB // 2))

                @block.gpsimd
                def _(pool):
                    nc.gpsimd.memset(ident[:, :], 1.0).then_inc(s_k0, 1)
                    nc.gpsimd.memset(hmask[:, :, :], 1.0).then_inc(s_k0, 1)
                    nc.gpsimd.memset(ones[:, :], 1.0).then_inc(s_c, 1)
                    nc.gpsimd.memset(mhalf[:, :], -0.5).then_inc(s_c, 1)
                    nc.gpsimd.memset(epsc[:, :], EPS).then_inc(s_c, 1)
                    nc.gpsimd.memset(zeros[:, :, :], 0.0).then_inc(s_c, 1)
                    nc.gpsimd.memset(va[:, :, :, DH:DH + 1], 1.0).then_inc(s_c, 1)
                    pool.wait_ge(s_k0, 2)
                    nc.gpsimd.affine_select(out=ident[:, :], in_=ident[:, :], compare_op=ALU.is_equal, fill=0.0,
                                            base=0, pattern=[[-1, P]], channel_multiplier=1).then_inc(s_c, 1)
                    nc.gpsimd.affine_select(out=hmask[:, :, :], in_=hmask[:, :, :], compare_op=ALU.is_ge, fill=0.0,
                                            base=0, pattern=[[-DH, HH], [0, P]], channel_multiplier=1).then_inc(s_k0, 1)
                    pool.wait_ge(s_k0, 3)
                    nc.gpsimd.affine_select(out=hmask[:, :, :], in_=hmask[:, :, :], compare_op=ALU.is_ge, fill=0.0,
                                            base=DH - 1, pattern=[[DH, HH], [0, P]], channel_multiplier=-1).then_inc(s_c, 1)
                    pool.wait_ge(s_c, 7)

                    def rstd(t, s_mv, s_rs, mv, rs, k):
                        pool.wait_ge(s_mv, 2 * t + 2)
                        nc.gpsimd.tensor_tensor(out=rs[:, k, 0:1], in0=mv[:, k, 1:2], in1=epsc[:, :], op=ALU.add).then_inc(s_rs, 1)
                        pool.wait_ge(s_rs, 2 * t + 1)
                        nc.gpsimd.tensor_tensor(out=rs[:, k, 1:2], in0=rs[:, k, 0:1], in1=mhalf[:, :],
                                                op=ALU.pow).then_inc(s_rs, 1)

                    def body(t, k):
                        if on(t - 1):
                            rstd(t - 1, s_mv2, s_rs2, mv2, rs2, (k - 1) % 4)
                        if on(t + 2):
                            a = k % 2
                            pool.wait_ge(s_ev1, t + 3)
                            if due(2 * t + 2):
                                pool.wait_ge(s_sc, 2 * t + 2)
                            for c in range(C):
                                nc.gpsimd.tensor_tensor(out=bd[:, a, c, :, :],
                                                        in0=T0[:, a, C + c:C + c + 1, :].broadcast_to([P, HH, P]),
                                                        in1=hmask[:, :, :], op=ALU.mult).then_inc(s_bd, 1)
                        if on(t + 3):
                            rstd(t + 3, s_mv1, s_rs1, mv1, rs1, (k + 3) % 4)
                        if on(t + 1):
                            a = (k + 1) % 4
                            pool.wait_ge(s_ld[a], (t + 1 - a) * 8 + 32)
                            if due(2 * t):
                                pool.wait_ge(s_pv, 2 * t)
                            nc.gpsimd.tensor_tensor(out=va[:, a % 2, :, 0:DH],
                                                    in0=cb[:, a, :].rearrange("p (h d) -> p h d", h=NH),
                                                    in1=ones[:, 0:1].unsqueeze(1).broadcast_to([P, NH, DH]),
                                                    op=ALU.mult).then_inc(s_va, 1)

                    steps(pool, *RANGE, body)

                @block.vector
                def _(dve):
                    def stats(t, k, src, st, mv, s_mv):
                        nc.vector.bn_stats(st[:, k, :], src).then_inc(s_mv, 1)
                        dve.wait_ge(s_mv, 2 * t + 1)
                        take_wait(nc.vector)
                        nc.vector.bn_aggr(mv[:, k, :], st[:, k, :]).then_inc(s_mv, 1)

                    def soft_max(t, h):
                        if on(t):
                            dve.wait_ge(s_sc, 2 * t + 1 + h)
                            nc.vector.tensor_reduce(mx[:, h, :], S[h][:, :, :], AX.X, ALU.max).then_inc(s_mx, 1)
                            dve.wait_ge(s_mx, 2 * t + 1 + h)
                            nc.vector.tensor_tensor(S[h][:, :, :], S[h][:, :, :],
                                                    mx[:, h, :].unsqueeze(2).broadcast_to([P, HH, P]),
                                                    ALU.subtract).then_inc(s_sub, 1)

                    def body(t, k):
                        if on(t - 1):
                            a = (k - 1) % 4
                            dve.wait_ge(s_rs2, 2 * t)
                            if due((t - 1 - a % 2) * 8):
                                dve.wait_ge(s_h1st[a % 2], (t - 1 - a % 2) * 8)
                            if due(t - 2):
                                dve.wait_ge(s_h1t, t - 2)
                            nc.vector.tensor_scalar(h1[:, a % 2, :], x1[:, a % 2, :], mv2[:, a, 0:1], rs2[:, a, 1:2],
                                                    ALU.subtract, ALU.mult).then_inc(s_h1, 1)
                        soft_max(t + 1, 0)
                        if on(t + 3):
                            a = (k + 3) % 4
                            dve.wait_ge(s_ld[a], (t + 3 - a) * 8 + 32)
                            stats(t + 3, a, xb[:, a, :], st1, mv1, s_mv1)
                        soft_max(t + 1, 1)
                        if on(t - 1):
                            dve.wait_ge(s_lg, t)
                            nc.vector.tensor_scalar(logits[:, bass.ds(t - 1, 1), :].rearrange("p o e -> p (o e)"),
                                                    M[:, 0:E], 1.0 / 16.0, None, ALU.mult).then_inc(s_lc, 1)
                        if on(t + 3):
                            a = (k + 3) % 4
                            dve.wait_ge(s_rs1, 2 * t + 8)
                            if due(t + 2):
                                dve.wait_ge(s_tr1, t + 2)
                            nc.vector.tensor_scalar(xn[:, a % 2, :], xb[:, a, :], mv1[:, a, 0:1], rs1[:, a, 1:2],
                                                    ALU.subtract, ALU.mult).then_inc(s_xn, 1)
                        if on(t):
                            a = k % 2
                            dve.wait_ge(s_pv, 2 * t + 2)
                            if due((t - a) * 8):
                                dve.wait_ge(s_x1st[a], (t - a) * 8)
                            nc.vector.reciprocal(rec[:, a, :, :], Ov[:, :, DH:DH + 1]).then_inc(s_rc, 1)
                            dve.wait_ge(s_rc, t + 1)
                            nc.vector.tensor_tensor(x1[:, a, :].rearrange("p (h d) -> p h d", h=NH), Ov[:, :, 0:DH],
                                                    rec[:, a, :, :].broadcast_to([P, NH, DH]),
                                                    ALU.mult).then_inc(s_nm, 1)
                            dve.wait_ge(s_nm, t + 1)
                            nc.vector.tensor_tensor(x1[:, a, :], x1[:, a, :], xb[:, k, :], ALU.add).then_inc(s_x1, 1)
                            dve.wait_ge(s_x1, t + 1)
                            stats(t, k, x1[:, a, :], st2, mv2, s_mv2)

                    steps(dve, *RANGE, body)

                @block.scalar
                def _(act):
                    def body(t, k):
                        def weights_copy(h):
                            if on(t):
                                act.wait_ge(s_pt, 2 * t + h + 1)
                                if due(2 * t + h - 1):
                                    act.wait_ge(s_pv, 2 * t + h - 1)
                                nc.scalar.copy(pT[:, h, :, :], PT[:, :, :]).then_inc(s_pte, 1)

                        def exps(h):
                            if on(t + 1):
                                act.wait_ge(s_sub, 2 * t + 3 + h)
                                if due(2 * t + h + 1):
                                    act.wait_ge(s_pt, 2 * t + h + 1)
                                nc.scalar.activation(pr[:, h, :, :], S[h][:, :, :], ACT.Exp,
                                                     scale=DH ** -0.5).then_inc(s_exp, 1)

                        if on(t + 2):
                            act.wait_ge(s_tr1, t + 3)
                            if due(2 * t + 2):
                                act.wait_ge(s_sc, 2 * t + 2)
                            if due(2 * t + 2):
                                act.wait_ge(s_bd, 2 * t + 2)
                            nc.scalar.copy(T0[:, k % 2, :, :],
                                           M[:, :].rearrange("p (c n) -> p c n", c=2 * C)).then_inc(s_ev1, 1)
                        weights_copy(0)
                        if on(t - 1):
                            act.wait_ge(s_h1t, t)
                            if due((t - 1 - (k - 1) % 2) * 8):
                                act.wait_ge(s_h1Tst[(k - 1) % 2], (t - 1 - (k - 1) % 2) * 8)
                            if due(t - 2):
                                act.wait_ge(s_lg, t - 2)
                            nc.scalar.copy(h1T[:, (k - 1) % 2, :, :],
                                           M[:, 0:C * P].rearrange("p (c n) -> p c n", c=C)).then_inc(s_h1e, 1)
                        weights_copy(1)
                        exps(0)
                        exps(1)

                    steps(act, *RANGE, body)

                @block.tensor
                def _(pe):
                    pe.wait_ge(s_c, 7)
                    pe.wait_ge(s_wr, 16)

                    def weights_transpose(t, h):
                        if on(t):
                            pe.wait_ge(s_exp, 2 * t + h + 1)
                            if due(2 * t + h):
                                pe.wait_ge(s_pte, 2 * t + h)
                            for i in range(HH):
                                last = nc.tensor.transpose(PT[:, i, :], pr[:, h, i, :], ident[:, :])
                            last.then_inc(s_pt, 1)

                    def scores(t, k, h):
                        if on(t):
                            pe.wait_ge(s_bd, 2 * t + 2)
                            if due(2 * t - 1 + h):
                                pe.wait_ge(s_exp, 2 * t - 1 + h)
                            for i in range(0, HH, 4):
                                last = nc.tensor.matmul(S[h][:, i:i + 4, :], T0[:, k % 2, h, :],
                                                        bd[:, k % 2, h, i:i + 4, :], start=True, stop=True)
                            last.then_inc(s_sc, 1)

                    def values(t, k, h):
                        if on(t):
                            pe.wait_ge(s_pte, 2 * t + h + 1)
                            pe.wait_ge(s_va, t + 1)
                            if due(t):
                                pe.wait_ge(s_nm, t)
                            for i in range(HH):
                                last = nc.tensor.matmul(Ov[:, HH * h + i, :], pT[:, h, i, :],
                                                        va[:, k % 2, HH * h + i, :], start=True, stop=True)
                            last.then_inc(s_pv, 1)

                    def body(t, k):
                        weights_transpose(t, 0)
                        if on(t + 2):
                            a = (k + 2) % 4
                            pe.wait_ge(s_xn, t + 3)
                            pe.wait_ge(s_ld[a], (t + 2 - a) * 8 + 32)
                            if due(t - 1):
                                pe.wait_ge(s_lc, t - 1)
                            for c in range(C):
                                nc.tensor.transpose(M[:, c * P:(c + 1) * P], xn[:, a % 2, c * P:(c + 1) * P], ident[:, :])
                            for c in range(C):
                                last = nc.tensor.transpose(M[:, (C + c) * P:(C + c + 1) * P],
                                                           cb[:, a, c * P:(c + 1) * P], ident[:, :])
                            last.then_inc(s_tr1, 1)
                        scores(t + 1, k + 1, 0)
                        values(t, k, 0)
                        if on(t - 1):
                            a = (k - 1) % 2
                            pe.wait_ge(s_h1, t)
                            pe.wait_ge(s_ev1, upto(t + 3, NB))
                            if due(t - 1):
                                pe.wait_ge(s_lc, t - 1)
                            for c in range(C):
                                last = nc.tensor.transpose(M[:, c * P:(c + 1) * P], h1[:, a, c * P:(c + 1) * P],
                                                           ident[:, :])
                            last.then_inc(s_h1t, 1)
                        weights_transpose(t, 1)
                        scores(t + 1, k + 1, 1)
                        if on(t - 1):
                            pe.wait_ge(s_h1e, t)
                            for c in range(C):
                                last = nc.tensor.matmul(M[:, 0:E], h1T[:, (k - 1) % 2, c, :], wr[:, c, :],
                                                        start=c == 0, stop=c == C - 1)
                            last.then_inc(s_lg, 1)
                        values(t, k, 1)

                    steps(pe, *RANGE, body)
        with ExitStack() as ph:
            sb = lambda name, shape, dt=F32: ph.enter_context(nc.sbuf_tensor(name, shape, dt))
            rbb = sb("rbb", [P, E])
            revi = sb("revi", [P, E])
            sel = sb("sel", [P, NB, E])
            t0 = sb("t0", [P, NB, E])
            oh = sb("oh", [P, TOPK, NB, E])
            top = sb("top", [P, NB])
            gl = sb("gl", [P, TOPK, NB])
            mask = sb("mask", [P, NB, E])
            upper = sb("upper", [P, P])
            cum = sb("cum", [P, E, NB])
            tot = sb("tot", [P, E, NB])
            zb = sb("zb", [P, E * NB])
            start = sb("start", [P, E])
            cnt = sb("cnt", [P, E])
            cnti = sb("cnti", [P, E], I32)
            tiles = sb("tiles", [P, E])
            ctile = sb("ctile", [P, E])
            off = sb("off", [P, E])
            slotf = sb("slotf", [P, TOPK, NB])
            tid = sb("tid", [1, NT])
            le = sb("le", [1, NT, E])
            tef = sb("tef", [1, NT])
            R = [ph.enter_context(nc.psum_tensor(f"R{i}", [P, NB, E], F32)) for i in range(2)]
            s_rb, s_i, s_i2, s_v, s_e, s_mm = (sem(n) for n in ("s_rb", "s_i", "s_i2", "s_v", "s_e", "s_mm"))
            with nc.Block() as block:
                @block.sync
                def _(sp):
                    sp.dma_start(rbb[:, :], rb.rearrange("(o e) -> o e", o=1).broadcast_to([P, E])).then_inc(s_rb, 16)

                @block.gpsimd
                def _(pool):
                    nc.gpsimd.iota(revi[:, :], pattern=[[-1, E]], base=E, channel_multiplier=0,
                                   allow_small_or_imprecise_dtypes=True).then_inc(s_i, 1)
                    nc.gpsimd.iota(tid[:, :], pattern=[[1, NT]], base=0, channel_multiplier=0,
                                   allow_small_or_imprecise_dtypes=True).then_inc(s_i, 1)
                    nc.gpsimd.memset(zb[:, :], 0.0).then_inc(s_i, 1)
                    nc.gpsimd.memset(upper[:, :], 1.0).then_inc(s_i2, 1)
                    pool.wait_ge(s_i2, 1)
                    nc.gpsimd.affine_select(out=upper[:, :], in_=upper[:, :], compare_op=ALU.is_gt, fill=0.0,
                                            base=0, pattern=[[1, P]], channel_multiplier=-1).then_inc(s_i, 1)

                @block.tensor
                def _(pe):
                    pe.wait_ge(s_i, 4)
                    pe.wait_ge(s_v, MASK_AT)
                    nc.tensor.matmul(R[0][:, :, :], upper[:, :], mask[:, :, :], start=True, stop=True)
                    nc.tensor.matmul(R[1][:, :, :], ones[:, :], mask[:, :, :], start=True, stop=True).then_inc(s_mm, 1)

                @block.scalar
                def _(act):
                    act.wait_ge(s_v, GATE_AT)
                    nc.scalar.activation(gl[:, :, :], gl[:, :, :], ACT.Exp).then_inc(s_e, 1)

                @block.vector
                def _(dve):
                    done = [0]

                    def link(ins):
                        done[0] += 1
                        ins.then_inc(s_v, 1)
                        dve.wait_ge(s_v, done[0])

                    TT, TS, RED = nc.vector.tensor_tensor, nc.vector.tensor_scalar, nc.vector.tensor_reduce
                    over_b = lambda a: a.unsqueeze(1).broadcast_to([P, NB, E])
                    over_e = lambda a: a.unsqueeze(2).broadcast_to([P, NB, E])
                    dve.wait_ge(s_rb, 16)
                    dve.wait_ge(s_i, 4)
                    link(TT(sel[:, :, :], logits[:, :, :], over_b(rbb[:, :]), ALU.add))
                    for j in range(TOPK):
                        link(RED(top[:, :], sel[:, :, :], AX.X, ALU.max))
                        link(TT(t0[:, :, :], sel[:, :, :], over_e(top[:, :]), ALU.is_ge))
                        link(TT(t0[:, :, :], t0[:, :, :], over_b(revi[:, :]), ALU.mult))
                        link(RED(top[:, :], t0[:, :, :], AX.X, ALU.max))
                        link(TT(oh[:, j, :, :], over_b(revi[:, :]), over_e(top[:, :]), ALU.is_equal))
                        if j + 1 < TOPK:
                            link(TS(t0[:, :, :], oh[:, j, :, :], -1.0, 1.0, ALU.mult, ALU.add))
                            link(TT(sel[:, :, :], sel[:, :, :], t0[:, :, :], ALU.mult))
                            link(TS(t0[:, :, :], oh[:, j, :, :], -3.0e38, None, ALU.mult))
                            link(TT(sel[:, :, :], sel[:, :, :], t0[:, :, :], ALU.add))
                    link(TT(mask[:, :, :], oh[:, 0, :, :], oh[:, 1, :, :], ALU.add))
                    assert done[0] == MASK_AT, done
                    for j in range(TOPK):
                        link(TT(t0[:, :, :], logits[:, :, :], oh[:, j, :, :], ALU.mult))
                        link(RED(gl[:, j, :], t0[:, :, :], AX.X, ALU.add))
                    link(TT(top[:, :], gl[:, 0, :], gl[:, 1, :], ALU.max))
                    link(TT(gl[:, :, :], gl[:, :, :], top[:, :].unsqueeze(1).broadcast_to([P, TOPK, NB]), ALU.subtract))
                    assert done[0] == GATE_AT, done
                    dve.wait_ge(s_e, 1)
                    link(TT(top[:, :], gl[:, 0, :], gl[:, 1, :], ALU.add))
                    link(nc.vector.reciprocal(top[:, :], top[:, :]))
                    link(TT(gate[:, :, :], gl[:, :, :], top[:, :].unsqueeze(1).broadcast_to([P, TOPK, NB]), ALU.mult))
                    dve.wait_ge(s_mm, 1)
                    link(nc.vector.tensor_copy(tot[:, :, :], R[1][:, :, :].rearrange("p b e -> p e b")))
                    link(nc.vector.tensor_tensor_scan(cum[:, :, :].rearrange("p e b -> p (e b)"),
                                                      tot[:, :, :].rearrange("p e b -> p (e b)"),
                                                      zb[:, :], 0.0, ALU.add, ALU.add))
                    link(nc.vector.memset(start[:, 0:1], 0.0))
                    link(nc.vector.tensor_copy(start[:, 1:E], cum[:, 0:E - 1, NB - 1]))
                    link(TT(cnt[:, :], cum[:, :, NB - 1], start[:, :], ALU.subtract))
                    link(TT(cum[:, :, :], cum[:, :, :], tot[:, :, :], ALU.subtract))
                    link(TS(cnti[:, :], cnt[:, :], float(P - 1), None, ALU.add))
                    link(TS(cnti[:, :], cnti[:, :], P.bit_length() - 1, None, ALU.logical_shift_right))
                    link(nc.vector.tensor_copy(tiles[:, :], cnti[:, :]))
                    link(nc.vector.tensor_tensor_scan(ctile[:, :], tiles[:, :], zb[:, 0:E], 0.0, ALU.add, ALU.add))
                    link(TT(off[:, :], ctile[:, :], tiles[:, :], ALU.subtract))
                    link(TS(off[:, :], off[:, :], float(P), None, ALU.mult))
                    link(TT(off[:, :], off[:, :], start[:, :], ALU.subtract))
                    link(TT(sel[:, :, :], R[0][:, :, :], cum[:, :, :].rearrange("p e b -> p b e"), ALU.add))
                    link(TT(sel[:, :, :], sel[:, :, :], over_b(off[:, :]), ALU.add))
                    for j in range(TOPK):
                        link(TT(t0[:, :, :], sel[:, :, :], oh[:, j, :, :], ALU.mult))
                        link(RED(slotf[:, j, :], t0[:, :, :], AX.X, ALU.add))
                    link(nc.vector.tensor_copy(slot[:, :, :], slotf[:, :, :]))
                    link(TT(le[:, :, :], ctile[0:1, :].unsqueeze(1).broadcast_to([1, NT, E]),
                            tid[:, :].unsqueeze(2).broadcast_to([1, NT, E]), ALU.is_le))
                    link(RED(tef[:, :], le[:, :, :], AX.X, ALU.add))
                    link(TS(tile_expert[:, :], tef[:, :], float(E - 1), None, ALU.min))

        with ExitStack() as ph:
            sb = lambda name, shape, dt=F32: ph.enter_context(nc.sbuf_tensor(name, shape, dt))
            hs = sb("hs", [P, 4, 2, C, P])
            xr = sb("xr", [P, 4, 2, D])
            sg = sb("sg", [P, 2, 2, 2 * P])
            hh = sb("hh", [P, 2, HSC, 2 * P])
            ao = sb("ao", [P, 2, 2, D])
            ht = sb("ht", [P, 4, D])
            ix = sb("ix", [P, 4, TOPK, 1], I32)
            U = [ph.enter_context(nc.psum_tensor(f"U{i}", [P, 2, 2 * P], F32)) for i in range(2)]
            G = [ph.enter_context(nc.psum_tensor(f"G{i}", [P, 2, 2 * P], F32)) for i in range(2)]
            Y = [ph.enter_context(nc.psum_tensor(f"Y{i}", [P, D], F32)) for i in range(2)]
            s_hl, s_ht = sems("s_hl", 4), sems("s_ht", 4)
            s_up, s_sl, s_ml, s_dn, s_ad, s_ix = (sem(n) for n in ("s_up", "s_sl", "s_ml", "s_dn", "s_ad", "s_ix"))
            s_ast, s_scat = sems("s_ast", 2), sems("s_scat", 4)
            NP = NB // 2
            onp, onb = stage_on(NP), stage_on(NB)
            RANGE3 = (-4, NP + 1, 4, NP - 4, 4)
            with nc.Block() as block:
                @block.sync
                def _(sp):
                    def body(t, k):
                        if onp(t + 4):
                            if due(2 * t + 2):
                                sp.wait_ge(s_ad, 2 * t + 2)
                            sp.dma_start(hs[:, k, :, :, :].rearrange("p t c n -> p t (c n)"),
                                         h1T_d[bass.ds((t + 4) * 2, 2), :, :].rearrange("t p n -> p t n")
                                         ).then_inc(s_hl[k], 16)
                            sp.dma_start(xr[:, k, :, :],
                                         x1_d[bass.ds((t + 4) * 2, 2), :, :].rearrange("t p n -> p t n")
                                         ).then_inc(s_hl[k], 16)
                        if onp(t):
                            sp.wait_ge(s_ad, 2 * t + 2)
                            sp.dma_start(acc_d[bass.ds(t * 2, 2), :, :].rearrange("t p n -> p t n"),
                                         ao[:, k % 2, :, :]).then_inc(s_ast[k % 2], 16)

                    steps(sp, *RANGE3, body)
                    for j in range(2):
                        sp.wait_ge(s_ast[j], 16 * (NP // 2))

                @block.tensor
                def _(pe):
                    pe.wait_ge(s_ws, 48)

                    def up(t, k, h):
                        if onp(t):
                            pe.wait_ge(s_hl[k], (t - k) * 8 + 32)
                            if due(2 * t - 1 + h):
                                pe.wait_ge(s_ml, 2 * t - 1 + h)
                            for w, bank in ((ws3, G[h]), (ws1, U[h])):
                                for i in range(2):
                                    for c in range(C):
                                        b = (2 * h + i) * P
                                        last = nc.tensor.matmul(bank[:, i, :], w[:, c, b:b + P], hs[:, k, :, c, :],
                                                                start=c == 0, stop=c == C - 1)
                            last.then_inc(s_up, 1)

                    def down(t, k, j):
                        if onp(t):
                            pe.wait_ge(s_ml, 2 * t + 2)
                            if due(2 * t - 1 + j):
                                pe.wait_ge(s_ad, 2 * t - 1 + j)
                            for c in range(HSC):
                                last = nc.tensor.matmul(Y[j][:, :], hh[:, k % 2, c, j * P:(j + 1) * P], ws2[:, c, :],
                                                        start=c == 0, stop=c == HSC - 1)
                            last.then_inc(s_dn, 1)

                    def body(t, k):
                        up(t, k, 0)
                        down(t - 1, k + 1, 0)
                        up(t, k, 1)
                        down(t - 1, k + 1, 1)

                    steps(pe, 0, *RANGE3[1:], body)

                @block.scalar
                def _(act):
                    def body(t, k):
                        if onp(t):
                            for h in range(2):
                                act.wait_ge(s_up, 2 * t + h + 1)
                                if due(2 * t - 1 + h):
                                    act.wait_ge(s_ml, 2 * t - 1 + h)
                                nc.scalar.activation(sg[:, h, :, :], G[h][:, :, :], ACT.Silu).then_inc(s_sl, 1)

                    steps(act, 0, *RANGE3[1:], body)

                @block.vector
                def _(dve):
                    def mul(t, k, h):
                        if onp(t):
                            dve.wait_ge(s_sl, 2 * t + h + 1)
                            if due(2 * t - 2):
                                dve.wait_ge(s_dn, 2 * t - 2)
                            nc.vector.tensor_tensor(hh[:, k % 2, 2 * h:2 * h + 2, :], U[h][:, :, :], sg[:, h, :, :],
                                                    ALU.mult).then_inc(s_ml, 1)

                    def add(t, k, j):
                        if onp(t):
                            dve.wait_ge(s_dn, 2 * t + j + 1)
                            if due((t - k % 2) * 8):
                                dve.wait_ge(s_ast[k % 2], (t - k % 2) * 8)
                            nc.vector.tensor_tensor(ao[:, k % 2, j, :], Y[j][:, :], xr[:, k, j, :],
                                                    ALU.add).then_inc(s_ad, 1)

                    def body(t, k):
                        mul(t, k, 0)
                        add(t - 1, (k - 1) % 4, 0)
                        mul(t, k, 1)
                        add(t - 1, (k - 1) % 4, 1)

                    steps(dve, 0, *RANGE3[1:], body)

                @block.gpsimd
                def _(pool):
                    pool.wait_ge(s_zero, 16 * (NT // 2))

                    def body(t, k):
                        if due((t - k) * 8):
                            pool.wait_ge(s_scat[k], (t - k) * 8)
                        take_wait(nc.gpsimd)
                        pool.dma_start(ht[:, k, :], h1_d[t, :, :]).then_inc(s_ht[k], 16)
                        take_wait(nc.gpsimd)
                        nc.gpsimd.tensor_copy(ix[:, k, :, :], slot[:, :, bass.ds(t, 1)]).then_inc(s_ix, 1)
                        pool.wait_ge(s_ix, t + 1)
                        pool.wait_ge(s_ht[k], (t - k) * 4 + 16)
                        for j in range(TOPK):
                            take_wait(nc.gpsimd)
                            nc.gpsimd.indirect_dma_start(
                                out=xs_d[:, :], out_offset=bass.IndirectOffsetOnAxis(ap=ix[:, k, j, :], axis=0),
                                in_=ht[:, k, :], in_offset=None).then_inc(s_scat[k], 16)

                    steps(pool, 0, NB, 4, NB, 4, body)
                    for k in range(4):
                        pool.wait_ge(s_scat[k], 32 * (NB // 4))

        wup = per("wup", [P, C, F])
        wdT = per("wdT", [P, C, F])
        bup = per("bup", [P, FC])
        wl = per("wl", [P, 4 * C, D])
        with ExitStack() as ph:
            sb = lambda name, shape, dt=F32: ph.enter_context(nc.sbuf_tensor(name, shape, dt))
            xe = sb("xe", [P, 4, D])
            xT = sb("xT", [P, 2, C, P])
            sg4 = sb("sg4", [P, 2, H])
            he = sb("he", [P, 2, H])
            hT = sb("hT", [P, 2, HC, P])
            ye = sb("ye", [P, 2, D])
            bw = sb("bw", [P, 2, F // 2, 4])
            bt = sb("bt", [P, 2, F // 2])
            by = sb("by", [P, F])
            brow = sb("brow", [1, 3, F])
            Ue = [ph.enter_context(nc.psum_tensor(f"Ue{i}", [P, H], F32)) for i in range(2)]
            Ge = [ph.enter_context(nc.psum_tensor(f"Ge{i}", [P, H], F32)) for i in range(2)]
            XT = ph.enter_context(nc.psum_tensor("XT", [P, C, P], F32))
            HT = ph.enter_context(nc.psum_tensor("HT", [P, HC, P], F32))
            Ye = [ph.enter_context(nc.psum_tensor(f"Ye{i}", [P, D], F32)) for i in range(2)]
            s_xe = sems("s_xe", 4)
            s_xt, s_xte, s_g, s_u, s_sl4, s_he = (sem(n) for n in ("s_xt", "s_xte", "s_g", "s_u", "s_sl4", "s_he"))
            s_hT, s_hTe, s_ye, s_yc = (sem(n) for n in ("s_hT", "s_hTe", "s_ye", "s_yc"))
            s_yst = sems("s_yst", 2)
            s_bl, s_bo, s_bs = sem("s_bl"), sem("s_bo"), sem("s_bs")
            s_bw = sems("s_bw", 2)
            on4 = stage_on(NT)
            RANGE4 = (-4, NT + 2, 4, NT - 4, 4)
            with nc.Block() as block:
                @block.sync
                def _(sp):
                    def body(t, k):
                        if on4(t + 4):
                            if due(t + 1):
                                sp.wait_ge(s_xt, t + 1)
                            sp.dma_start(xe[:, k, :], xs_d[bass.ds((t + 4) * P, P), :]).then_inc(s_xe[k], 16)
                        if on4(t - 1):
                            j = (k - 1) % 2
                            sp.wait_ge(s_yc, t)
                            sp.dma_start(ys_d[bass.ds((t - 1) * P, P), :], ye[:, j, :]).then_inc(s_yst[j], 16)

                    steps(sp, *RANGE4, body)
                    for j in range(2):
                        sp.wait_ge(s_yst[j], 16 * (NT // 2))

                @block.tensor
                def _(pe):
                    pe.wait_ge(s_wm, 16 * 3 * E)

                    def xtr(t, k):
                        if on4(t):
                            pe.wait_ge(s_xe[k % 4], (t - k % 4) * 4 + 16)
                            if due(t):
                                pe.wait_ge(s_xte, t)
                            for c in range(C):
                                last = nc.tensor.transpose(XT[:, c, :], xe[:, k % 4, c * P:(c + 1) * P], ident[:, :])
                            last.then_inc(s_xt, 1)

                    def body(t, k):
                        if isinstance(t, int) and t < 0:
                            if t == -1:
                                xtr(0, 0)
                            return
                        a, b = k % 2, (k - 1) % 2
                        if on4(t):
                            e = pe.value_load(tile_expert[0:1, bass.ds(t, 1)], min_val=0, max_val=E - 1)
                            pe.wait_ge(s_xte, t + 1)
                            if due(t - 1):
                                pe.wait_ge(s_sl4, t - 1)
                            for c in range(C):
                                last = nc.tensor.matmul(Ge[a][:, :], xT[:, a, c, :], w3m[:, bass.ds(e, 1), c, :],
                                                        start=c == 0, stop=c == C - 1)
                            last.then_inc(s_g, 1)
                        xtr(t + 1, k + 1)
                        if on4(t - 1):
                            pe.wait_ge(s_he, t)
                            if due(t - 1):
                                pe.wait_ge(s_hTe, t - 1)
                            for c in range(HC):
                                last = nc.tensor.transpose(HT[:, c, :], he[:, b, c * P:(c + 1) * P], ident[:, :])
                            last.then_inc(s_hT, 1)
                        if on4(t):
                            if due(t - 1):
                                pe.wait_ge(s_he, t - 1)
                            for c in range(C):
                                last = nc.tensor.matmul(Ue[a][:, :], xT[:, a, c, :], w1m[:, bass.ds(e, 1), c, :],
                                                        start=c == 0, stop=c == C - 1)
                            last.then_inc(s_u, 1)
                        if on4(t - 1):
                            e = pe.value_load(tile_expert[0:1, bass.ds(t - 1, 1)], min_val=0, max_val=E - 1)
                            pe.wait_ge(s_hTe, t)
                            if due(t - 2):
                                pe.wait_ge(s_yc, t - 2)
                            for c in range(HC):
                                last = nc.tensor.matmul(Ye[b][:, :], hT[:, b, c, :], w2m[:, bass.ds(e, 1), c, :],
                                                        start=c == 0, stop=c == HC - 1)
                            last.then_inc(s_ye, 1)

                    steps(pe, *RANGE4, body)

                @block.scalar
                def _(act):
                    def body(t, k):
                        if on4(t):
                            act.wait_ge(s_g, t + 1)
                            if due(t - 1):
                                act.wait_ge(s_he, t - 1)
                            nc.scalar.activation(sg4[:, k % 2, :], Ge[k % 2][:, :], ACT.Silu).then_inc(s_sl4, 1)
                        if on4(t - 1):
                            act.wait_ge(s_hT, t)
                            if due(t - 2):
                                act.wait_ge(s_ye, t - 2)
                            nc.scalar.copy(hT[:, (k - 1) % 2, :, :], HT[:, :, :]).then_inc(s_hTe, 1)

                    steps(act, *RANGE4, body)

                @block.vector
                def _(dve):
                    def body(t, k):
                        if on4(t + 1):
                            dve.wait_ge(s_xt, t + 2)
                            if due(t):
                                dve.wait_ge(s_u, t)
                            nc.vector.tensor_copy(xT[:, (k + 1) % 2, :, :], XT[:, :, :]).then_inc(s_xte, 1)
                        if on4(t):
                            dve.wait_ge(s_sl4, t + 1)
                            dve.wait_ge(s_u, t + 1)
                            if due(t - 1):
                                dve.wait_ge(s_hT, t - 1)
                            nc.vector.tensor_tensor(he[:, k % 2, :], Ue[k % 2][:, :], sg4[:, k % 2, :],
                                                    ALU.mult).then_inc(s_he, 1)
                        if on4(t - 1):
                            j = (k - 1) % 2
                            dve.wait_ge(s_ye, t)
                            if due((t - 1 - j) * 8):
                                dve.wait_ge(s_yst[j], (t - 1 - j) * 8)
                            nc.vector.tensor_copy(ye[:, j, :], Ye[j][:, :]).then_inc(s_yc, 1)

                    steps(dve, *RANGE4, body)

                @block.gpsimd
                def _(pool):
                    pool.dma_start(wup[:, :, :], W_exp.rearrange("(c p) h -> p c h", p=P)).then_inc(s_bl, 16)
                    pool.dma_start(brow[:, 0, :], b_exp.rearrange("(o h) -> o h", o=1)).then_inc(s_bl, 16)
                    pool.dma_start(brow[:, 1, :], up_bias.rearrange("(o h) -> o h", o=1)).then_inc(s_bl, 16)
                    pool.dma_start(wdT[:, :, :], WconT.rearrange("(c p) h -> p c h", p=P)).then_inc(s_bl, 16)
                    pool.dma_start(wl[:, :, :], WlT.rearrange("(c p) d -> p c d", p=P)).then_inc(s_bl, 16)
                    plan = [(up_w, s, False) for s in range(NST)] + [(dn_w, s, True) for s in reversed(range(NST))]
                    count = [0]

                    def load(n):
                        w, s, _ = plan[n]
                        pool.dma_start(bw[:, n % 2, :, :].rearrange("p k f -> p (k f)"),
                                       w[s].rearrange("k i j -> (k i j)").unsqueeze(0).broadcast_to([P, 2 * F])
                                       ).then_inc(s_bw[n % 2], 16)

                    def link(ins):
                        count[0] += 1
                        ins.then_inc(s_bo, 1)
                        pool.wait_ge(s_bo, count[0])

                    def stage(row, parts, n, flip):
                        s = plan[n][1]
                        st = 2 ** s
                        v = row.rearrange("p (k i s) -> p k i s", i=2, s=st)
                        a, b = v[:, :, 0, :], v[:, :, 1, :]
                        w = bw[0:parts, n % 2, :, :].rearrange("p (k s) f -> p k s f", s=st)
                        t = [bt[0:parts, j, :].rearrange("p (k s) -> p k s", s=st) for j in range(2)]
                        y = by[0:parts, 0:F // 2].rearrange("p (k s) -> p k s", s=st)
                        z = by[0:parts, F // 2:F].rearrange("p (k s) -> p k s", s=st)
                        aa, ab, ba, bb = (0, 2, 1, 3) if flip else (0, 1, 2, 3)
                        TT = nc.gpsimd.tensor_tensor
                        TT(out=t[0], in0=w[:, :, :, aa], in1=a, op=ALU.mult).then_inc(s_bo, 1)
                        TT(out=t[1], in0=w[:, :, :, ab], in1=b, op=ALU.mult).then_inc(s_bo, 1)
                        TT(out=y, in0=w[:, :, :, ba], in1=a, op=ALU.mult).then_inc(s_bo, 1)
                        count[0] += 3
                        link(TT(out=z, in0=w[:, :, :, bb], in1=b, op=ALU.mult))
                        TT(out=a, in0=t[0], in1=t[1], op=ALU.add).then_inc(s_bo, 1)
                        count[0] += 1
                        link(TT(out=b, in0=y, in1=z, op=ALU.add))

                    load(0)
                    load(1)
                    pool.wait_ge(s_bl, 80)
                    for n in range(2 * NST):
                        pool.wait_ge(s_bw[n % 2], 16 * (n // 2 + 1))
                        dst, flip = (wdT, True) if plan[n][2] else (wup, False)
                        for c in range(C):
                            stage(dst[:, c, :], P, n, flip)
                        if not flip:
                            stage(brow[:, 0, :], 1, n, False)
                        if n + 2 < 2 * NST:
                            load(n + 2)
                    link(nc.gpsimd.tensor_tensor(out=brow[:, 2, :], in0=brow[:, 0, :], in1=brow[:, 1, :], op=ALU.add))
                    pool.dma_start(bu_d[:, :], brow[:, 2, :]).then_inc(s_bs, 16)
                    pool.wait_ge(s_bs, 16)
                    pool.dma_start(bup[:, :], bu_d.rearrange("o (b p) -> p (o b)", p=P),
                                   allow_slow_non_contiguous=True).then_inc(s_bs, 16)
                    pool.wait_ge(s_bs, 32)

        with ExitStack() as ph:
            sb = lambda name, shape, dt=F32: ph.enter_context(nc.sbuf_tensor(name, shape, dt))
            ax = sb("ax", [P, 4, D])
            cx = sb("cx", [P, 4, D])
            yg = sb("yg", [P, 4, TOPK, D])
            ix5 = sb("ix5", [P, 4, TOPK, 1], I32)
            x2 = sb("x2", [P, 4, D])
            st5 = sb("st5", [P, 4, 6])
            mv5 = sb("mv5", [P, 4, 2])
            rs5 = sb("rs5", [P, 4, 2])
            c5 = sb("c5", [P, 4, D])
            cT = sb("cT", [P, 4, C, P])
            cw = sb("cw", [P, 2, C, P])
            qT = sb("qT", [P, 2, C, P])
            dots = sb("dots", [P, D])
            rr = sb("rr", [P, 4, 1])
            m5 = sb("m5", [P, 4, 1])
            xbl = sb("xbl", [P, 2, D])
            nm5 = sb("nm5", [P, 4, 2])
            pa = sb("pa", [P, 2, P])
            ps = sb("ps", [P, 4, 2])
            aT = sb("aT", [P, 2, P])
            gmax = sb("gmax", [P, 4, 1])
            be = sb("be", [P, 4, 1])
            q2 = sb("q2", [P, 4, 4])
            wz = sb("wz", [P, 2, C, D])
            uT = sb("uT", [P, 2, C, P])
            vT = sb("vT", [P, 2, C, P])
            x3 = sb("x3", [P, 2, D])
            wcq = sb("wcq", [P, 2, C])
            wcb = sb("wcb", [P, D])
            bias3 = sb("bias3", [P, 4])
            blb = sb("blb", [P, D])
            T5 = ph.enter_context(nc.psum_tensor("T5", [P, 2 * C, P], F32))
            S5 = ph.enter_context(nc.psum_tensor("S5", [P, P], F32))
            A5 = ph.enter_context(nc.psum_tensor("A5", [P, P], F32))
            U5 = ph.enter_context(nc.psum_tensor("U5", [P, C, P], F32))
            Q5 = ph.enter_context(nc.psum_tensor("Q5", [P, 4], F32))
            Z5 = [ph.enter_context(nc.psum_tensor(f"Z5{i}", [P, D], F32)) for i in range(2)]
            s_w5, s_b5 = sem("s_w5"), sem("s_b5")
            s_l5, s_g5 = sems("s_l5", 4), sems("s_g5", 4)
            s_x3st = sems("s_x3st", 2)
            (s_ix5, s_y1, s_x2, s_mv5, s_rs5, s_c5, s_t5, s_q5, s_ct, s_cw, s_dt, s_rr, s_s5, s_nm,
             s_M, s_gm, s_p5, s_pr5, s_an, s_a5, s_at, s_be, s_Q, s_qc, s_qr, s_qn, s_wz, s_u5, s_ut, s_vt, s_z, s_xb,
             s_x3) = (sem(f"s5_{i}") for i in range(33))
            RANGE5 = (-4, NB + 3, 4, NB - 4, 4)
            with nc.Block() as block:
                @block.sync
                def _(sp):
                    as_col = lambda a: a.rearrange("(c p) -> p c", p=P)
                    as_rows = lambda a, n: a.rearrange("(o d) -> o d", o=1).broadcast_to([P, n])
                    sp.dma_start(wcq[:, 0, :], as_col(w_cq), allow_slow_non_contiguous=True).then_inc(s_w5, 16)
                    sp.dma_start(wcq[:, 1, :], as_col(w_q), allow_slow_non_contiguous=True).then_inc(s_w5, 16)
                    sp.dma_start(wcb[:, :], as_rows(w_c, D)).then_inc(s_w5, 16)
                    sp.dma_start(blb[:, :], as_rows(b_l, D)).then_inc(s_w5, 16)
                    for i, b in enumerate((b_cq, b_c, b_q)):
                        sp.dma_start(bias3[:, i:i + 1], as_rows(b, 1)).then_inc(s_w5, 16)

                    def body(t, k):
                        if on(t + 4):
                            if due(t + 1):
                                sp.wait_ge(s_x2, t + 1)
                            if due(t + 1):
                                sp.wait_ge(s_u5, t + 1)
                            sp.dma_start(ax[:, k, :], acc_d[t + 4, :, :]).then_inc(s_l5[k], 16)
                            sp.dma_start(cx[:, k, :], ctx_in[t + 4, :, :]).then_inc(s_l5[k], 16)
                        if on(t):
                            sp.wait_ge(s_x3, t + 1)
                            sp.dma_start(x3_d[t, :, :], x3[:, k % 2, :]).then_inc(s_x3st[k % 2], 16)

                    steps(sp, *RANGE5, body)
                    for j in range(2):
                        sp.wait_ge(s_x3st[j], 16 * (NB // 2))

                @block.gpsimd
                def _(pool):
                    pool.wait_ge(s_w5, 16 * 7)
                    nc.gpsimd.tensor_tensor(out=bias3[:, 3:4], in0=bias3[:, 0:1], in1=bias3[:, 1:2],
                                            op=ALU.add).then_inc(s_b5, 1)
                    pool.wait_ge(s_b5, 1)
                    nc.gpsimd.tensor_tensor(out=bias3[:, 0:1], in0=bias3[:, 3:4], in1=bias3[:, 2:3],
                                            op=ALU.add).then_inc(s_b5, 1)

                    def gather(t, k):
                        if on(t):
                            if due(t - 3):
                                pool.wait_ge(s_x2, t - 3)
                            take_wait(nc.gpsimd)
                            nc.gpsimd.tensor_copy(ix5[:, k, :, :], slot[:, :, bass.ds(t, 1)]).then_inc(s_ix5, 1)
                            pool.wait_ge(s_ix5, t + 1)
                            for j in range(TOPK):
                                take_wait(nc.gpsimd)
                                nc.gpsimd.indirect_dma_start(
                                    out=yg[:, k, j, :], out_offset=None, in_=ys_d[:, :],
                                    in_offset=bass.IndirectOffsetOnAxis(ap=ix5[:, k, j, :], axis=0)
                                ).then_inc(s_g5[k], 16)

                    def body(t, k):
                        gather(t + 4, k)
                        if on(t + 3):
                            a = (k + 3) % 4
                            pool.wait_ge(s_mv5, 2 * t + 8)
                            nc.gpsimd.tensor_tensor(out=rs5[:, a, 0:1], in0=mv5[:, a, 1:2], in1=epsc[:, :],
                                                    op=ALU.add).then_inc(s_rs5, 1)
                            pool.wait_ge(s_rs5, 2 * t + 7)
                            nc.gpsimd.tensor_tensor(out=rs5[:, a, 1:2], in0=rs5[:, a, 0:1], in1=mhalf[:, :],
                                                    op=ALU.pow).then_inc(s_rs5, 1)
                        if on(t):
                            if due(t - 1):
                                pool.wait_ge(s_x3, t - 1)
                            nc.gpsimd.tensor_tensor(out=xbl[:, k % 2, :], in0=x2[:, k, :], in1=blb[:, :],
                                                    op=ALU.add).then_inc(s_xb, 1)
                        if on(t + 2):
                            pool.wait_ge(s_M, t + 3)
                            a = (k + 2) % 4
                            take_wait(nc.gpsimd)
                            nc.gpsimd.partition_all_reduce(gmax[:, a, :], m5[:, a, :], P,
                                                           bass.bass_isa.ReduceOp.max).then_inc(s_gm, 1)
                    steps(pool, *RANGE5, body)

                @block.vector
                def _(dve):
                    TT, TS, STT = nc.vector.tensor_tensor, nc.vector.tensor_scalar, nc.vector.scalar_tensor_tensor
                    dve.wait_ge(s_b5, 2)

                    def residual(t, k):
                        if on(t):
                            dve.wait_ge(s_l5[k], (t - k) * 8 + 32)
                            dve.wait_ge(s_g5[k], (t - k) * 8 + 32)
                            STT(ax[:, k, :], yg[:, k, 0, :], gate[:, 0, bass.ds(t, 1)], ax[:, k, :],
                                ALU.mult, ALU.add).then_inc(s_y1, 1)
                            dve.wait_ge(s_y1, t + 1)
                            STT(x2[:, k, :], yg[:, k, 1, :], gate[:, 1, bass.ds(t, 1)], ax[:, k, :],
                                ALU.mult, ALU.add).then_inc(s_x2, 1)
                            dve.wait_ge(s_x2, t + 1)
                            nc.vector.bn_stats(st5[:, k, :], x2[:, k, :]).then_inc(s_mv5, 1)
                            dve.wait_ge(s_mv5, 2 * t + 1)
                            take_wait(nc.vector)
                            nc.vector.bn_aggr(mv5[:, k, :], st5[:, k, :]).then_inc(s_mv5, 1)

                    def normed(t, k):
                        if on(t):
                            dve.wait_ge(s_rs5, 2 * t + 2)
                            if due(t - 3):
                                dve.wait_ge(s_z, t - 3)
                            TS(c5[:, k, :], x2[:, k, :], mv5[:, k, 0:1], rs5[:, k, 1:2],
                               ALU.subtract, ALU.mult).then_inc(s_c5, 1)
                            dve.wait_ge(s_c5, t + 1)
                            if due(t):
                                dve.wait_ge(s_dt, t)
                            STT(dots[:, :], c5[:, k, :], 1.0, wcb[:, :], ALU.mult, ALU.mult,
                                accum_out=rr[:, k, :]).then_inc(s_dt, 1)

                    def row_max(t, k):
                        if on(t):
                            dve.wait_ge(s_s5, t + 1)
                            dve.wait_ge(s_dt, t + 1)
                            nc.vector.tensor_reduce(nm5[:, k, 0:1], S5[:, :], AX.X, ALU.max,
                                                    negate=True).then_inc(s_nm, 1)
                            dve.wait_ge(s_nm, t + 1)
                            STT(m5[:, k, :], rr[:, k, :], bias3[:, 0:1], nm5[:, k, 0:1],
                                ALU.add, ALU.subtract).then_inc(s_M, 1)

                    def weights(t, k):
                        if on(t):
                            dve.wait_ge(s_p5, t + 1)
                            nc.vector.reciprocal(ps[:, k, 1:2], ps[:, k, 0:1]).then_inc(s_pr5, 1)

                    def gmax_neg(t, k):
                        if on(t):
                            dve.wait_ge(s_gm, t + 1)
                            TS(nm5[:, k, 1:2], gmax[:, k, :], -1.0, None, ALU.mult).then_inc(s_qn, 1)

                    def q2c(t, k):
                        if on(t):
                            dve.wait_ge(s_Q, t + 1)
                            nc.vector.reciprocal(q2[:, k, 3:4], Q5[:, 2:3]).then_inc(s_qr, 1)
                            dve.wait_ge(s_qr, t + 1)
                            TS(q2[:, k, 0:2], Q5[:, 0:2], q2[:, k, 3:4], None, ALU.mult).then_inc(s_qc, 1)
                            dve.wait_ge(s_qc, t + 1)
                            if due(t - 1):
                                dve.wait_ge(s_z, t - 1)
                            for c in range(C):
                                STT(wz[:, k % 2, c, :], wl[:, 3 * C + c, :], q2[:, k, c:c + 1], wl[:, c, :],
                                    ALU.mult, ALU.add).then_inc(s_wz, 1)

                    def attended(t, k):
                        if on(t):
                            dve.wait_ge(s_ut, t + 1)
                            if due(t - 1):
                                dve.wait_ge(s_z, t - 1)
                            TT(vT[:, k % 2, :, :], cT[:, k, :, :], uT[:, k % 2, :, :], ALU.mult).then_inc(s_vt, 1)

                    def finish(t, k):
                        if on(t):
                            dve.wait_ge(s_z, t + 1)
                            if due((t - k % 2) * 8):
                                dve.wait_ge(s_x3st[k % 2], (t - k % 2) * 8)
                            dve.wait_ge(s_xb, t + 1)
                            TT(x3[:, k % 2, :], Z5[k % 2][:, :], xbl[:, k % 2, :], ALU.add).then_inc(s_x3, 1)

                    def body(t, k):
                        q = lambda n: (k + n) % 4
                        residual(t + 3, q(3))
                        q2c(t, k)
                        row_max(t + 2, q(2))
                        normed(t + 3, q(3))
                        attended(t + 1, q(1))
                        weights(t + 2, q(2))
                        gmax_neg(t + 2, q(2))
                        finish(t, k)

                    steps(dve, *RANGE5, body)

                @block.scalar
                def _(act):
                    def body(t, k):
                        q = lambda n: (k + n) % 4
                        if on(t + 1):
                            a = q(1)
                            act.wait_ge(s_a5, t + 2)
                            if due(t):
                                act.wait_ge(s_u5, t)
                            nc.scalar.copy(aT[:, a % 2, :], A5[:, :]).then_inc(s_at, 1)
                        if on(t + 2):
                            a = q(2)
                            act.wait_ge(s_nm, t + 3)
                            if due(t + 1):
                                act.wait_ge(s_a5, t + 1)
                            nc.scalar.activation(pa[:, a % 2, :], S5[:, :], ACT.Exp, bias=nm5[:, a, 0:1],
                                                 accum_out=ps[:, a, 0:1]).then_inc(s_p5, 1)
                        if on(t + 1):
                            a = q(1)
                            act.wait_ge(s_u5, t + 2)
                            if due(t):
                                act.wait_ge(s_z, t)
                            if due(t):
                                act.wait_ge(s_vt, t)
                            nc.scalar.copy(uT[:, a % 2, :, :], U5[:, :, :]).then_inc(s_ut, 1)
                        if on(t + 3):
                            a = q(3)
                            act.wait_ge(s_t5, t + 4)
                            if due(t + 2):
                                act.wait_ge(s_s5, t + 2)
                            if due(t):
                                act.wait_ge(s_z, t)
                            for c in range(C):
                                nc.scalar.activation(cw[:, a % 2, c, :], T5[:, c, :], ACT.Identity,
                                                     scale=wcq[:, 0, c:c + 1], bias=wcq[:, 1, c:c + 1]).then_inc(s_cw, 1)
                            nc.scalar.copy(cT[:, a, :, :], T5[:, 0:C, :]).then_inc(s_ct, 1)
                            nc.scalar.copy(qT[:, a % 2, :, :], T5[:, C:2 * C, :]).then_inc(s_q5, 1)
                        if on(t + 2):
                            a = q(2)
                            act.wait_ge(s_pr5, t + 3)
                            nc.scalar.mul(pa[:, a % 2, :], pa[:, a % 2, :], ps[:, a, 1:2]).then_inc(s_an, 1)
                            act.wait_ge(s_qn, t + 3)
                            nc.scalar.activation(be[:, a, :], m5[:, a, :], ACT.Exp, bias=nm5[:, a, 1:2]).then_inc(s_be, 1)

                    steps(act, *RANGE5, body)

                @block.tensor
                def _(pe):
                    def project(t, k, operand, chunk, first=False, final=False):
                        for c in range(C):
                            last = nc.tensor.matmul(Z5[k % 2][:, :], operand[c], chunk[c],
                                                    start=first and c == 0, stop=final and c == C - 1)
                        return last

                    def body(t, k):
                        q = lambda n: (k + n) % 4
                        if on(t + 2):
                            a = q(2)
                            pe.wait_ge(s_cw, 2 * t + 6)
                            pe.wait_ge(s_q5, t + 3)
                            if due(t + 2):
                                pe.wait_ge(s_p5, t + 2)
                            for c in range(C):
                                last = nc.tensor.matmul(S5[:, :], cw[:, a % 2, c, :], qT[:, a % 2, c, :],
                                                        start=c == 0, stop=c == C - 1)
                            last.then_inc(s_s5, 1)
                        if on(t + 1):
                            a = q(1)
                            pe.wait_ge(s_an, t + 2)
                            if due(t + 1):
                                pe.wait_ge(s_at, t + 1)
                            nc.tensor.transpose(A5[:, :], pa[:, a % 2, :], ident[:, :]).then_inc(s_a5, 1)
                        if on(t):
                            if due(t - 1):
                                pe.wait_ge(s_x3, t - 1)
                            pe.wait_ge(s_ut, t + 1)
                            project(t, k, [uT[:, k % 2, c, :] for c in range(C)], [wl[:, C + c, :] for c in range(C)],
                                    first=True)
                            pe.wait_ge(s_vt, t + 1)
                            project(t, k, [vT[:, k % 2, c, :] for c in range(C)], [wl[:, 2 * C + c, :] for c in range(C)])
                        if on(t + 1):
                            a = q(1)
                            pe.wait_ge(s_at, t + 2)
                            if due(t + 1):
                                pe.wait_ge(s_ut, t + 1)
                            for c in range(C):
                                last = nc.tensor.matmul(U5[:, c, :], cx[:, a, c * P:(c + 1) * P], aT[:, a % 2, :],
                                                        start=True, stop=True)
                            last.then_inc(s_u5, 1)
                        if on(t + 3):
                            a = q(3)
                            pe.wait_ge(s_l5[a], (t + 3 - a) * 8 + 32)
                            pe.wait_ge(s_c5, t + 4)
                            if due(t + 3):
                                pe.wait_ge(s_q5, t + 3)
                            for c in range(C):
                                nc.tensor.transpose(T5[:, c, :], c5[:, a, c * P:(c + 1) * P], ident[:, :])
                            for c in range(C):
                                last = nc.tensor.transpose(T5[:, C + c, :], cx[:, a, c * P:(c + 1) * P], ident[:, :])
                            last.then_inc(s_t5, 1)
                        if on(t):
                            pe.wait_ge(s_wz, 2 * t + 2)
                            project(t, k, [cT[:, k, c, :] for c in range(C)], [wz[:, k % 2, c, :] for c in range(C)],
                                    final=True).then_inc(s_z, 1)
                        if on(t + 1):
                            a = q(1)
                            pe.wait_ge(s_be, t + 2)
                            if due(t + 1):
                                pe.wait_ge(s_qc, t + 1)
                            for c in range(C):
                                nc.tensor.matmul(Q5[:, c:c + 1], c5[:, a, c * P:(c + 1) * P], be[:, a, :],
                                                 start=True, stop=True)
                            nc.tensor.matmul(Q5[:, C:C + 1], ones[:, :], be[:, a, :], start=True, stop=True
                                             ).then_inc(s_Q, 1)

                    steps(pe, *RANGE5, body)

        with ExitStack() as ph:
            sb = lambda name, shape, dt=F32: ph.enter_context(nc.sbuf_tensor(name, shape, dt))
            wdn = sb("wdn", [P, FC, D])
            x6 = sb("x6", [P, 4, 2, D])
            st6 = sb("st6", [P, 4, 2, 6])
            mv6 = sb("mv6", [P, 4, 2, 2])
            rs6 = sb("rs6", [P, 4, 2, 2])
            n6 = sb("n6", [P, 2, 2, D])
            T6s = sb("T6s", [P, 2, C, 2, P])
            g6 = sb("g6", [P, 2, FC, 2 * P])
            o6 = sb("o6", [P, 2, 2, D])
            bo6 = sb("bo6", [P, 3, D])
            T6 = [ph.enter_context(nc.psum_tensor(f"T6{i}", [P, C, P], F32)) for i in range(2)]
            H6 = [ph.enter_context(nc.psum_tensor(f"H6{i}", [P, 2 * P], F32)) for i in range(4)]
            Y6 = [ph.enter_context(nc.psum_tensor(f"Y6{i}", [P, D], F32)) for i in range(2)]
            s_w6, s_wt6, s_we6, s_b6 = sem("s_w6"), sem("s_wt6"), sem("s_we6"), sem("s_b6")
            s_l6, BASE_L = s_ld, 32 * (NB // 4)
            s_mv6, s_rs6, s_n6, s_t6, s_e6, s_h6, s_g6, s_y6, s_a6, s_o6 = (
                sem(f"s6_{i}") for i in range(10))
            s_ost, BASE_S = s_x1st, 16 * (NB // 2)
            RANGE6 = (-4, NP + 1, 4, NP - 4, 4)
            with nc.Block() as block:
                @block.sync
                def _(sp):
                    sp.dma_start(bo6[:, 0, :], b_con.rearrange("(o d) -> o d", o=1).broadcast_to([P, D])).then_inc(s_w6, 16)
                    sp.dma_start(bo6[:, 1, :], dn_bias.rearrange("(o d) -> o d", o=1).broadcast_to([P, D])).then_inc(s_w6, 16)

                    def body(t, k):
                        if onp(t + 4):
                            if due(2 * t + 2):
                                sp.wait_ge(s_o6, 2 * t + 2)
                            sp.dma_start(x6[:, k, :, :], x3_d[bass.ds((t + 4) * 2, 2), :, :].rearrange("t p n -> p t n")
                                         ).then_inc(s_l6[k], 16)
                        if onp(t):
                            sp.wait_ge(s_o6, 2 * t + 2)
                            sp.dma_start(out[bass.ds(t * 2, 2), :, :].rearrange("t p n -> p t n"),
                                         o6[:, k % 2, :, :]).then_inc(s_ost[k % 2], 16)

                    steps(sp, *RANGE6, body)
                    for j in range(2):
                        sp.wait_ge(s_ost[j], 16 * (NP // 2) + BASE_S)

                @block.gpsimd
                def _(pool):
                    pool.wait_ge(s_w6, 32)
                    nc.gpsimd.tensor_tensor(out=bo6[:, 2, :], in0=bo6[:, 0, :], in1=bo6[:, 1, :], op=ALU.add).then_inc(s_b6, 1)

                    def body(t, k):
                        if onp(t + 2):
                            a = (k + 2) % 4
                            pool.wait_ge(s_mv6, 4 * t + 12)
                            nc.gpsimd.tensor_tensor(out=rs6[:, a, :, 0:1], in0=mv6[:, a, :, 1:2],
                                                    in1=epsc[:, :].unsqueeze(1).broadcast_to([P, 2, 1]), op=ALU.add).then_inc(s_rs6, 1)
                            pool.wait_ge(s_rs6, 2 * t + 5)
                            nc.gpsimd.tensor_tensor(out=rs6[:, a, :, 1:2], in0=rs6[:, a, :, 0:1],
                                                    in1=mhalf[:, :].unsqueeze(1).broadcast_to([P, 2, 1]),
                                                    op=ALU.pow).then_inc(s_rs6, 1)

                    steps(pool, *RANGE6, body)

                @block.vector
                def _(dve):
                    for i in range(2 * FC):
                        c, b = i // FC, i % FC
                        dve.wait_ge(s_wt6, i + 1)
                        nc.vector.tensor_copy(wdn[:, b, c * P:(c + 1) * P], T6[i % 2][:, 0, :]).then_inc(s_we6, 1)
                    dve.wait_ge(s_b6, 1)

                    def stats(t, a):
                        if onp(t):
                            dve.wait_ge(s_l6[a], (t - a) * 4 + 16 + BASE_L)
                            for j in range(2):
                                nc.vector.bn_stats(st6[:, a, j, :], x6[:, a, j, :]).then_inc(s_mv6, 1)
                            for j in range(2):
                                dve.wait_ge(s_mv6, 4 * t + 1 + j)
                                take_wait(nc.vector)
                                nc.vector.bn_aggr(mv6[:, a, j, :], st6[:, a, j, :]).then_inc(s_mv6, 1)

                    def finish(t, a, j):
                        if onp(t):
                            dve.wait_ge(s_y6, 2 * t + 1 + j)
                            dve.wait_ge(s_ost[a % 2], (t - a % 2) * 8 + BASE_S)
                            nc.vector.tensor_tensor(o6[:, a % 2, j, :], Y6[j][:, :], x6[:, a, j, :],
                                                    ALU.add).then_inc(s_a6, 1)
                            dve.wait_ge(s_a6, 2 * t + 1 + j)
                            nc.vector.tensor_tensor(o6[:, a % 2, j, :], o6[:, a % 2, j, :], bo6[:, 2, :],
                                                    ALU.add).then_inc(s_o6, 1)

                    def body(t, k):
                        q = lambda n: (k + n) % 4
                        if onp(t + 1):
                            a = q(1)
                            dve.wait_ge(s_rs6, 2 * t + 4)
                            if due(2 * t):
                                dve.wait_ge(s_t6, 2 * t)
                            for j in range(2):
                                nc.vector.tensor_scalar(n6[:, a % 2, j, :], x6[:, a, j, :], mv6[:, a, j, 0:1],
                                                        rs6[:, a, j, 1:2], ALU.subtract, ALU.mult).then_inc(s_n6, 1)
                            for j in range(2):
                                dve.wait_ge(s_t6, 2 * t + 3 + j)
                                if due(FC * t):
                                    dve.wait_ge(s_h6, FC * t)
                                nc.vector.tensor_copy(T6s[:, a % 2, :, j, :], T6[j][:, :, :]).then_inc(s_e6, 1)
                        for j in range(2):
                            finish(t - 1, q(-1), j)
                            if j == 0:
                                stats(t + 2, q(2))

                    steps(dve, *RANGE6, body)

                @block.scalar
                def _(act):
                    def body(t, k):
                        if onp(t):
                            for b in range(FC):
                                act.wait_ge(s_h6, FC * t + b + 1)
                                if due(2 * t - 2):
                                    act.wait_ge(s_y6, 2 * t - 2)
                                nc.scalar.activation(g6[:, k % 2, b, :], H6[b % 4][:, :], ACT.Gelu,
                                                     bias=bup[:, b:b + 1]).then_inc(s_g6, 1)

                    steps(act, *RANGE6, body)

                @block.tensor
                def _(pe):
                    for i in range(2 * FC):
                        c, b = i // FC, i % FC
                        if due(i - 1):
                            pe.wait_ge(s_we6, i - 1)
                        nc.tensor.transpose(T6[i % 2][:, 0, :], wdT[:, c, b * P:(b + 1) * P], ident[:, :]).then_inc(s_wt6, 1)
                    pe.wait_ge(s_we6, 2 * FC)

                    def tr(t, k):
                        if onp(t):
                            pe.wait_ge(s_n6, 2 * t + 2)
                            if due(2 * t):
                                pe.wait_ge(s_e6, 2 * t)
                            for j in range(2):
                                for c in range(C):
                                    last = nc.tensor.transpose(T6[j][:, c, :], n6[:, k % 2, j, c * P:(c + 1) * P], ident[:, :])
                                last.then_inc(s_t6, 1)

                    def up(t, k, b):
                        if onp(t):
                            pe.wait_ge(s_e6, 2 * t + 2)
                            if due(FC * t + b - 3):
                                pe.wait_ge(s_g6, FC * t + b - 3)
                            for c in range(C):
                                last = nc.tensor.matmul(H6[b % 4][:, :], wup[:, c, b * P:(b + 1) * P],
                                                        T6s[:, k % 2, c, :, :], start=c == 0, stop=c == C - 1)
                            last.then_inc(s_h6, 1)

                    def down(t, k, j, half):
                        if onp(t):
                            pe.wait_ge(s_g6, FC * t + FC)
                            if due(2 * t - 1 + j):
                                pe.wait_ge(s_a6, 2 * t - 1 + j)
                            for b in range(half * FC // 2, (half + 1) * FC // 2):
                                last = nc.tensor.matmul(Y6[j][:, :], g6[:, k % 2, b, j * P:(j + 1) * P], wdn[:, b, :],
                                                        start=b == 0, stop=b == FC - 1)
                            if half:
                                last.then_inc(s_y6, 1)

                    def body(t, k):
                        up(t, k, 0)
                        up(t, k, 1)
                        down(t - 1, k + 1, 0, 0)
                        up(t, k, 2)
                        up(t, k, 3)
                        tr(t + 1, k + 1)
                        down(t - 1, k + 1, 0, 1)
                        up(t, k, 4)
                        up(t, k, 5)
                        down(t - 1, k + 1, 1, 0)
                        up(t, k, 6)
                        up(t, k, 7)
                        down(t - 1, k + 1, 1, 1)

                    steps(pe, *RANGE6, body)


_INS = ['x', 'ctx_1024', 'L0_ffn_Wr', 'L0_ffn_rb', 'L0_ffn_W1', 'L0_ffn_W2', 'L0_ffn_W3', 'L0_ffn_Ws1', 'L0_ffn_Ws2',
        'L0_ffn_Ws3', 'L1_xattn_w_cq', 'L1_xattn_b_cq', 'L1_xattn_w_c', 'L1_xattn_b_c', 'L1_xattn_w_q', 'L1_xattn_b_q',
        'L1_xattn_W_l', 'L1_xattn_b_l', 'L1_ffn_W_exp', 'L1_ffn_b_exp', 'L1_ffn_up_weights', 'L1_ffn_up_bias',
        'L1_ffn_down_weights', 'L1_ffn_W_con', 'L1_ffn_b_con', 'L1_ffn_down_bias']
_TRANSPOSED = ('L1_xattn_W_l', 'L1_ffn_W_con')


def kernel(**inputs):
    import numpy as _np
    import concourse.bacc as _bacc
    from concourse import mybir as _mybir
    from concourse.bass_utils import run_bass_kernel_spmd as _run

    nc = _bacc.Bacc("TRN2", target_bir_lowering=False, num_devices=1)
    arrays, args = {}, []
    for name in _INS:
        a = _np.asarray(inputs[name])
        a = _np.ascontiguousarray(a.T if name in _TRANSPOSED else a)
        if a.ndim == 0:
            a = a.reshape(1)
        arrays[f"in_{name}_dram"] = a
        args.append(nc.dram_tensor(f"in_{name}_dram", a.shape, _mybir.dt.from_np(a.dtype), kind="ExternalInput").ap())
    shape = tuple(inputs['x'].shape)
    args.append(nc.dram_tensor("out_dram", shape, _mybir.dt.float32, kind="ExternalOutput").ap())
    build_program(nc, *args)
    r = _run(nc, [arrays], core_ids=[0])
    return r.results[0]["out_dram"]
```

```python
import concourse.bass as bass
from concourse import mybir
from contextlib import ExitStack

F32 = mybir.dt.float32
F16 = mybir.dt.float16
I32 = mybir.dt.int32
ALU = mybir.AluOpType
ACT = mybir.ActivationFunctionType
AX = mybir.AxisListType
MASK_AT, GATE_AT, ROUTED_AT = 16, 22, 48

P = 128
D = 256
C = D // P
EPS = 1e-5
HI, LO = 0, 1
PARTS = ((HI, HI), (HI, LO), (LO, HI))
PS = 4096.0
XS = 64.0
WS = 256.0
ES = 4.0
GS = 16.0


def due(count):
    return not isinstance(count, int) or count > 0


def steps(eng, first, last, lo, hi, unroll, body):
    assert lo % unroll == 0 and hi % unroll == 0
    for t in range(first, lo):
        body(t, t % unroll)
    if hi > lo:
        with eng.Fori(lo // unroll, hi // unroll) as i:
            for u in range(unroll):
                body(i * unroll + u, u)
    for t in range(hi, last):
        body(t, t % unroll)


def stage_on(n):
    return lambda t: not isinstance(t, int) or 0 <= t < n


def upto(t, n):
    return min(t, n) if isinstance(t, int) else t


def build_program(nc, x, ctx_in, Wr, rb, W1, W2, W3, Ws1, Ws2, Ws3, w_cq, b_cq, w_c, b_c, w_q, b_q,
                  WlT, b_l, WexpT, b_exp, up_w, up_bias, dn_w, W_con, b_con, dn_bias, out):
    NB = x.shape[0]
    E = W1.shape[0]
    H = W1.shape[2]
    HC = H // P
    HS = Ws1.shape[1]
    HSC = HS // P
    NH = 16
    DH = D // NH
    HH = NH // C
    TOPK = 2
    NT = NB * TOPK + E
    F = WexpT.shape[0]
    FC = F // P
    ctx = ExitStack()
    sem = lambda name: ctx.enter_context(nc.semaphore(name))
    sems = lambda name, n: [sem(f"{name}{i}") for i in range(n)]
    per = lambda name, shape, dt=F32: ctx.enter_context(nc.sbuf_tensor(name, shape, dt))

    def dram(name, shape):
        return nc.dram_tensor(name, shape, F32, kind="Internal").ap()

    x1_d = dram("x1_d", (NB, P, D))
    h1_d = dram("h1_d", (NB, P, D))
    h1T_d = dram("h1T_d", (NB, P, C * P))
    acc_d = dram("acc_d", (NB, P, D))
    xs_d = dram("xs_d", (NT * P, D))
    ys_d = dram("ys_d", (NT * P, D))
    x3_d = dram("x3_d", (NB, P, D))

    with ctx:
        ident = per("ident", [P, P])
        mhalf = per("mhalf", [P, 1])
        epsc = per("epsc", [P, 1])
        spare = per("spare", [1, 3, 32])
        ones = per("ones", [P, P])
        logits = per("logits", [P, NB, E])
        gate = per("gate", [P, TOPK, NB])
        slot = per("slot", [P, TOPK, NB], I32)
        tile_expert = per("tile_expert", [1, NT], I32)
        wm = per("wm", [P, 3, E, 2, C * H], F16)
        shared = ctx.enter_context(ExitStack())
        per = lambda name, shape, dt=F32, scope=shared: scope.enter_context(nc.sbuf_tensor(name, shape, dt))
        stage = per("stage", [P, 3, C * H])
        wsm = per("wsm", [P, 3, 2, C * H], F16)

        turn = [0]

        def take_wait(eng):
            turn[0] = (turn[0] + 1) % 32
            if eng is nc.vector:
                eng.memset(spare[:, 0, turn[0]:turn[0] + 1], 0.0)
            elif eng is nc.scalar:
                eng.copy(spare[:, 2, turn[0]:turn[0] + 1], ones[0:1, 0:1])
            else:
                eng.tensor_tensor(out=spare[:, 1, turn[0]:turn[0] + 1], in0=ones[0:1, 0:1], in1=ones[0:1, 0:1], op=ALU.mult)

        s_ws = sem("s_ws")
        s_wsh = sem("s_wsh")
        s_c = sem("s_c")
        s_zero = sem("s_zero")

        with ExitStack() as ph:
            sb = lambda name, shape, dt=F32: ph.enter_context(nc.sbuf_tensor(name, shape, dt))
            xb = sb("xb", [P, 4, D])
            cb = sb("cb", [P, 4, D])
            xn = sb("xn", [P, 2, D])
            T0 = sb("T0", [P, 2, 2 * C, P])
            bd = sb("bd", [P, 2, C, HH, P])
            hmask = sb("hmask", [P, HH, P])
            pr = sb("pr", [P, C, HH, P])
            pT = sb("pT", [P, C, 2, HH, P], F16)
            va = sb("va", [P, 2, 2, NH, DH + 1], F16)
            nmx = sb("nmx", [P, C, HH])
            x1 = sb("x1", [P, 2, D])
            h1 = sb("h1", [P, 2, D])
            h1T = sb("h1T", [P, 2, C, P])
            rec = sb("rec", [P, 2, NH, 1])
            st1 = sb("st1", [P, 4, 6])
            mv1 = sb("mv1", [P, 4, 2])
            rs1 = sb("rs1", [P, 4, 2])
            st2 = sb("st2", [P, 4, 6])
            mv2 = sb("mv2", [P, 4, 2])
            rs2 = sb("rs2", [P, 4, 2])
            wr = sb("wr", [P, C, E])
            zeros = sb("zeros", [P, 2, D])
            S = [ph.enter_context(nc.psum_tensor(f"S{c}", [P, HH, P], F32)) for c in range(C)]
            PT = ph.enter_context(nc.psum_tensor("PT", [P, HH, P], F32))
            O = ph.enter_context(nc.psum_tensor("O", [P, 512], F32))
            M = ph.enter_context(nc.psum_tensor("M", [P, 512], F32))
            Ov = O[:, 0:NH * (DH + 1)].rearrange("p (h d) -> p h d", h=NH)

            s_wr = sem("s_wr")
            s_k0 = sem("s_k0")
            s_ld = sems("s_ld", 4)
            s_mv1, s_rs1, s_xn = (sem(n) for n in ("s_mv1", "s_rs1", "s_xn"))
            s_mv2, s_rs2, s_h1 = (sem(n) for n in ("s_mv2", "s_rs2", "s_h1"))
            s_tr1, s_ev1, s_bd, s_va = (sem(n) for n in ("s_tr1", "s_ev1", "s_bd", "s_va"))
            s_sc, s_mx, s_exp = (sem(n) for n in ("s_sc", "s_mx", "s_exp"))
            s_pt, s_pth, s_ptl, s_pv = (sem(n) for n in ("s_pt", "s_pth", "s_ptl", "s_pv"))
            s_rc, s_nm, s_x1 = (sem(n) for n in ("s_rc", "s_nm", "s_x1"))
            s_h1t, s_h1e, s_lg, s_lc = (sem(n) for n in ("s_h1t", "s_h1e", "s_lg", "s_lc"))
            s_x1st, s_h1st, s_h1Tst = sems("s_x1st", 2), sems("s_h1st", 2), sems("s_h1Tst", 2)
            on = stage_on(NB)
            RANGE = (-4, NB + 1, 4, NB - 4, 4)

            with nc.Block() as block:
                @block.sync
                def _(sp):
                    def load(t, k):
                        if not on(t):
                            return
                        if due(t - 3):
                            sp.wait_ge(s_x1, t - 3)
                        sp.dma_start(xb[:, k, :], x[t, :, :]).then_inc(s_ld[k], 16)
                        sp.dma_start(cb[:, k, :], ctx_in[t, :, :]).then_inc(s_ld[k], 16)

                    def fill(t, k):
                        if isinstance(t, int) and t == 0:
                            sp.wait_ge(s_c, 8)
                            for i, w in enumerate((Ws3, Ws1, Ws2)):
                                sp.dma_start(stage[:, i, :].rearrange("p (c n) -> p c n", n=w.shape[1]),
                                             w.rearrange("(c p) n -> p c n", p=P)).then_inc(s_ws, 16)
                        if on(t):
                            sp.dma_start(xs_d[bass.ds(t * (2 * P), 2 * P), :].rearrange("(a p) d -> p a d", p=P),
                                         zeros[:, :, :]).then_inc(s_zero, 16)

                    def body(t, k):
                        load(t + 4, k)
                        fill(t, k)
                        if on(t):
                            sp.wait_ge(s_x1, t + 1)
                            sp.dma_start(x1_d[t, :, :], x1[:, k % 2, :]).then_inc(s_x1st[k % 2], 16)
                        if on(t - 1):
                            j = (k - 1) % 2
                            sp.wait_ge(s_h1, t)
                            sp.dma_start(h1_d[t - 1, :, :], h1[:, j, :]).then_inc(s_h1st[j], 16)
                            sp.wait_ge(s_h1e, t)
                            sp.dma_start(h1T_d[t - 1, :, :], h1T[:, j, :, :]).then_inc(s_h1Tst[j], 16)

                    sp.dma_start(wr[:, :, :], Wr.rearrange("(c p) e -> p c e", p=P)).then_inc(s_wr, 16)
                    steps(sp, *RANGE, body)
                    for i in range(NB, NT // 2):
                        sp.dma_start(xs_d[2 * P * i:2 * P * (i + 1), :].rearrange("(a p) d -> p a d", p=P),
                                     zeros[:, :, :]).then_inc(s_zero, 16)
                    for j in range(2):
                        sp.wait_ge(s_x1st[j], 16 * (NB // 2))
                        sp.wait_ge(s_h1st[j], 16 * (NB // 2))
                        sp.wait_ge(s_h1Tst[j], 16 * (NB // 2))

                @block.gpsimd
                def _(pool):
                    nc.gpsimd.memset(ident[:, :], 1.0).then_inc(s_k0, 1)
                    nc.gpsimd.memset(hmask[:, :, :], DH ** -0.5).then_inc(s_k0, 1)
                    nc.gpsimd.memset(ones[:, :], 1.0).then_inc(s_c, 1)
                    nc.gpsimd.memset(mhalf[:, :], -0.5).then_inc(s_c, 1)
                    nc.gpsimd.memset(epsc[:, :], EPS).then_inc(s_c, 1)
                    nc.gpsimd.memset(zeros[:, :, :], 0.0).then_inc(s_c, 1)
                    nc.gpsimd.memset(va[:, :, HI, :, DH:DH + 1], 1.0).then_inc(s_c, 1)
                    nc.gpsimd.memset(va[:, :, LO, :, DH:DH + 1], 0.0).then_inc(s_c, 1)
                    pool.wait_ge(s_k0, 2)
                    nc.gpsimd.affine_select(out=ident[:, :], in_=ident[:, :], compare_op=ALU.is_equal, fill=0.0,
                                            base=0, pattern=[[-1, P]], channel_multiplier=1).then_inc(s_c, 1)
                    nc.gpsimd.affine_select(out=hmask[:, :, :], in_=hmask[:, :, :], compare_op=ALU.is_ge, fill=0.0,
                                            base=0, pattern=[[-DH, HH], [0, P]], channel_multiplier=1).then_inc(s_k0, 1)
                    pool.wait_ge(s_k0, 3)
                    nc.gpsimd.affine_select(out=hmask[:, :, :], in_=hmask[:, :, :], compare_op=ALU.is_ge, fill=0.0,
                                            base=DH - 1, pattern=[[DH, HH], [0, P]], channel_multiplier=-1).then_inc(s_c, 1)
                    pool.wait_ge(s_c, 8)

                    def rstd(t, s_mv, s_rs, mv, rs, k):
                        pool.wait_ge(s_mv, 2 * t + 2)
                        nc.gpsimd.tensor_tensor(out=rs[:, k, 0:1], in0=mv[:, k, 1:2], in1=epsc[:, :], op=ALU.add).then_inc(s_rs, 1)
                        pool.wait_ge(s_rs, 2 * t + 1)
                        nc.gpsimd.tensor_tensor(out=rs[:, k, 1:2], in0=rs[:, k, 0:1], in1=mhalf[:, :],
                                                op=ALU.pow).then_inc(s_rs, 1)

                    def body(t, k):
                        if on(t - 1):
                            rstd(t - 1, s_mv2, s_rs2, mv2, rs2, (k - 1) % 4)
                        if on(t + 2):
                            a = k % 2
                            pool.wait_ge(s_ev1, t + 3)
                            if due(2 * t + 2):
                                pool.wait_ge(s_sc, 2 * t + 2)
                            for c in range(C):
                                nc.gpsimd.tensor_tensor(out=bd[:, a, c, :, :],
                                                        in0=T0[:, a, C + c:C + c + 1, :].broadcast_to([P, HH, P]),
                                                        in1=hmask[:, :, :], op=ALU.mult).then_inc(s_bd, 1)
                        if on(t + 3):
                            rstd(t + 3, s_mv1, s_rs1, mv1, rs1, (k + 3) % 4)
                        if on(t + 1):
                            a = (k + 1) % 4
                            pool.wait_ge(s_ld[a], (t + 1 - a) * 8 + 32)
                            if due(2 * t):
                                pool.wait_ge(s_pv, 2 * t)
                            ctx_h = cb[:, a, :].rearrange("p (h d) -> p h d", h=NH)
                            nc.gpsimd.tensor_tensor(out=va[:, a % 2, HI, :, 0:DH], in0=ctx_h,
                                                    in1=ones[:, 0:1].unsqueeze(1).broadcast_to([P, NH, DH]),
                                                    op=ALU.mult).then_inc(s_va, 1)
                            pool.wait_ge(s_va, 2 * t + 3)
                            nc.gpsimd.tensor_tensor(out=va[:, a % 2, LO, :, 0:DH], in0=ctx_h,
                                                    in1=va[:, a % 2, HI, :, 0:DH], op=ALU.subtract).then_inc(s_va, 1)

                    steps(pool, *RANGE, body)

                @block.vector
                def _(dve):
                    def stats(t, k, src, st, mv, s_mv):
                        nc.vector.bn_stats(st[:, k, :], src).then_inc(s_mv, 1)
                        dve.wait_ge(s_mv, 2 * t + 1)
                        take_wait(nc.vector)
                        nc.vector.bn_aggr(mv[:, k, :], st[:, k, :]).then_inc(s_mv, 1)

                    def maxima(t, h):
                        if on(t):
                            dve.wait_ge(s_sc, 2 * t + 1 + h)
                            nc.vector.tensor_reduce(nmx[:, h, :], S[h][:, :, :], AX.X, ALU.max,
                                                    negate=True).then_inc(s_mx, 1)

                    def weights_rest(t, h):
                        if on(t):
                            dve.wait_ge(s_pth, 2 * t + h + 1)
                            nc.vector.scalar_tensor_tensor(pT[:, h, LO, :, :], PT[:, :, :], PS, pT[:, h, HI, :, :],
                                                           ALU.mult, ALU.subtract).then_inc(s_ptl, 1)

                    def body(t, k):
                        if isinstance(t, int) and t == NB - 1:
                            dve.wait_ge(s_wsh, 3)
                            for i in range(3):
                                nc.vector.scalar_tensor_tensor(wsm[:, i, LO, :], stage[:, i, :], WS, wsm[:, i, HI, :],
                                                               ALU.mult, ALU.subtract)
                        weights_rest(t, 0)
                        if on(t - 1):
                            a = (k - 1) % 4
                            dve.wait_ge(s_rs2, 2 * t)
                            if due((t - 1 - a % 2) * 8):
                                dve.wait_ge(s_h1st[a % 2], (t - 1 - a % 2) * 8)
                            if due(t - 2):
                                dve.wait_ge(s_h1t, t - 2)
                            nc.vector.tensor_scalar(h1[:, a % 2, :], x1[:, a % 2, :], mv2[:, a, 0:1], rs2[:, a, 1:2],
                                                    ALU.subtract, ALU.mult).then_inc(s_h1, 1)
                        maxima(t + 1, 0)
                        if on(t + 3):
                            a = (k + 3) % 4
                            dve.wait_ge(s_ld[a], (t + 3 - a) * 8 + 32)
                            stats(t + 3, a, xb[:, a, :], st1, mv1, s_mv1)
                        weights_rest(t, 1)
                        maxima(t + 1, 1)
                        if on(t - 1):
                            dve.wait_ge(s_lg, t)
                            nc.vector.tensor_scalar(logits[:, bass.ds(t - 1, 1), :].rearrange("p o e -> p (o e)"),
                                                    M[:, 0:E], 1.0 / 16.0, None, ALU.mult).then_inc(s_lc, 1)
                        if on(t + 3):
                            a = (k + 3) % 4
                            dve.wait_ge(s_rs1, 2 * t + 8)
                            if due(t + 2):
                                dve.wait_ge(s_tr1, t + 2)
                            nc.vector.tensor_scalar(xn[:, a % 2, :], xb[:, a, :], mv1[:, a, 0:1], rs1[:, a, 1:2],
                                                    ALU.subtract, ALU.mult).then_inc(s_xn, 1)
                        if on(t):
                            a = k % 2
                            dve.wait_ge(s_pv, 2 * t + 2)
                            if due((t - a) * 8):
                                dve.wait_ge(s_x1st[a], (t - a) * 8)
                            nc.vector.reciprocal(rec[:, a, :, :], Ov[:, :, DH:DH + 1]).then_inc(s_rc, 1)
                            dve.wait_ge(s_rc, t + 1)
                            nc.vector.tensor_tensor(x1[:, a, :].rearrange("p (h d) -> p h d", h=NH), Ov[:, :, 0:DH],
                                                    rec[:, a, :, :].broadcast_to([P, NH, DH]),
                                                    ALU.mult).then_inc(s_nm, 1)
                            dve.wait_ge(s_nm, t + 1)
                            nc.vector.tensor_tensor(x1[:, a, :], x1[:, a, :], xb[:, k, :], ALU.add).then_inc(s_x1, 1)
                            dve.wait_ge(s_x1, t + 1)
                            stats(t, k, x1[:, a, :], st2, mv2, s_mv2)

                    steps(dve, *RANGE, body)

                @block.scalar
                def _(act):
                    def body(t, k):
                        def weights_hi(h):
                            if on(t):
                                act.wait_ge(s_pt, 2 * t + h + 1)
                                if due(2 * t + h - 1):
                                    act.wait_ge(s_pv, 2 * t + h - 1)
                                nc.scalar.mul(pT[:, h, HI, :, :], PT[:, :, :], PS).then_inc(s_pth, 1)

                        def exps(t, h):
                            if on(t):
                                act.wait_ge(s_mx, 2 * t + 1 + h)
                                if due(2 * t + h - 1):
                                    act.wait_ge(s_pt, 2 * t + h - 1)
                                for i in range(HH):
                                    last = nc.scalar.activation(pr[:, h, i, :], S[h][:, i, :], ACT.Exp,
                                                                bias=nmx[:, h, i:i + 1])
                                last.then_inc(s_exp, 1)

                        weights_hi(0)
                        if on(t + 2):
                            act.wait_ge(s_tr1, t + 3)
                            if due(2 * t + 2):
                                act.wait_ge(s_sc, 2 * t + 2)
                            if due(2 * t + 2):
                                act.wait_ge(s_bd, 2 * t + 2)
                            nc.scalar.copy(T0[:, k % 2, :, :],
                                           M[:, :].rearrange("p (c n) -> p c n", c=2 * C)).then_inc(s_ev1, 1)
                        exps(t, 1)
                        if on(t - 1):
                            act.wait_ge(s_h1t, t)
                            if due((t - 1 - (k - 1) % 2) * 8):
                                act.wait_ge(s_h1Tst[(k - 1) % 2], (t - 1 - (k - 1) % 2) * 8)
                            if due(t - 2):
                                act.wait_ge(s_lg, t - 2)
                            nc.scalar.copy(h1T[:, (k - 1) % 2, :, :],
                                           M[:, 0:C * P].rearrange("p (c n) -> p c n", c=C)).then_inc(s_h1e, 1)
                        weights_hi(1)
                        exps(t + 1, 0)
                        if isinstance(t, int) and 0 <= t - (NB - 4) < 3:
                            i = t - (NB - 4)
                            act.wait_ge(s_ws, 48)
                            nc.scalar.mul(wsm[:, i, HI, :], stage[:, i, :], WS).then_inc(s_wsh, 1)

                    steps(act, *RANGE, body)

                @block.tensor
                def _(pe):
                    pe.wait_ge(s_c, 8)
                    pe.wait_ge(s_wr, 16)

                    def weights_transpose(t, h):
                        if on(t):
                            pe.wait_ge(s_exp, 2 * t + h + 1)
                            if due(2 * t + h):
                                pe.wait_ge(s_ptl, 2 * t + h)
                            for i in range(HH):
                                last = nc.tensor.transpose(PT[:, i, :], pr[:, h, i, :], ident[:, :])
                            last.then_inc(s_pt, 1)

                    def scores(t, k, h):
                        if on(t):
                            pe.wait_ge(s_bd, 2 * t + 2)
                            if due(2 * t - 1 + h):
                                pe.wait_ge(s_exp, 2 * t - 1 + h)
                            for i in range(0, HH, 4):
                                last = nc.tensor.matmul(S[h][:, i:i + 4, :], T0[:, k % 2, h, :],
                                                        bd[:, k % 2, h, i:i + 4, :], start=True, stop=True)
                            last.then_inc(s_sc, 1)

                    def values(t, k, h):
                        if on(t):
                            pe.wait_ge(s_ptl, 2 * t + h + 1)
                            pe.wait_ge(s_va, 2 * t + 2)
                            if due(t):
                                pe.wait_ge(s_nm, t)
                            for i in range(HH):
                                for j, (wp, vp) in enumerate(PARTS):
                                    last = nc.tensor.matmul(Ov[:, HH * h + i, :], pT[:, h, wp, i, :],
                                                            va[:, k % 2, vp, HH * h + i, :], start=j == 0, stop=j == 2)
                            last.then_inc(s_pv, 1)

                    def body(t, k):
                        weights_transpose(t, 0)
                        if on(t + 2):
                            a = (k + 2) % 4
                            pe.wait_ge(s_xn, t + 3)
                            pe.wait_ge(s_ld[a], (t + 2 - a) * 8 + 32)
                            if due(t - 1):
                                pe.wait_ge(s_lc, t - 1)
                            for c in range(C):
                                nc.tensor.transpose(M[:, c * P:(c + 1) * P], xn[:, a % 2, c * P:(c + 1) * P], ident[:, :])
                            for c in range(C):
                                last = nc.tensor.transpose(M[:, (C + c) * P:(C + c + 1) * P],
                                                           cb[:, a, c * P:(c + 1) * P], ident[:, :])
                            last.then_inc(s_tr1, 1)
                        scores(t + 1, k + 1, 0)
                        values(t, k, 0)
                        if on(t - 1):
                            a = (k - 1) % 2
                            pe.wait_ge(s_h1, t)
                            pe.wait_ge(s_ev1, upto(t + 3, NB))
                            if due(t - 1):
                                pe.wait_ge(s_lc, t - 1)
                            for c in range(C):
                                last = nc.tensor.transpose(M[:, c * P:(c + 1) * P], h1[:, a, c * P:(c + 1) * P],
                                                           ident[:, :])
                            last.then_inc(s_h1t, 1)
                        weights_transpose(t, 1)
                        scores(t + 1, k + 1, 1)
                        if on(t - 1):
                            pe.wait_ge(s_h1e, t)
                            for c in range(C):
                                last = nc.tensor.matmul(M[:, 0:E], h1T[:, (k - 1) % 2, c, :], wr[:, c, :],
                                                        start=c == 0, stop=c == C - 1)
                            last.then_inc(s_lg, 1)
                        values(t, k, 1)

                    steps(pe, *RANGE, body)
        with ExitStack() as ph:
            sb = lambda name, shape, dt=F32: ph.enter_context(nc.sbuf_tensor(name, shape, dt))
            rbb = sb("rbb", [P, E])
            revi = sb("revi", [P, E])
            sel = sb("sel", [P, NB, E])
            t0 = sb("t0", [P, NB, E])
            oh = sb("oh", [P, TOPK, NB, E])
            top = sb("top", [P, NB])
            gl = sb("gl", [P, TOPK, NB])
            mask = sb("mask", [P, NB, E])
            upper = sb("upper", [P, P])
            cum = sb("cum", [P, E, NB])
            tot = sb("tot", [P, E, NB])
            zb = sb("zb", [P, E * NB])
            start = sb("start", [P, E])
            cnt = sb("cnt", [P, E])
            cnti = sb("cnti", [P, E], I32)
            tiles = sb("tiles", [P, E])
            ctile = sb("ctile", [P, E])
            off = sb("off", [P, E])
            slotf = sb("slotf", [P, TOPK, NB])
            tid = sb("tid", [1, NT])
            le = sb("le", [1, NT, E])
            tef = sb("tef", [1, NT])
            R = ph.enter_context(nc.psum_tensor("R", [P, 2, NB, E], F32))
            s_rb, s_i, s_v, s_e, s_mm = (sem(n) for n in ("s_rb", "s_i", "s_v", "s_e", "s_mm"))
            hs = sb("hs", [P, 4, 2, C, P])
            hp = sb("hp", [P, 2, 2, 2, C, P], F16)
            xr = sb("xr", [P, 4, 2, D])
            sg = sb("sg", [P, 2, 2, 2 * P])
            hf = sb("hf", [P, 2, 2, 2 * P])
            hh = sb("hh", [P, 2, 2, HSC, 2 * P], F16)
            ao = sb("ao", [P, 2, 2, D])
            ht = sb("ht", [P, 4, 2, D])
            ix = sb("ix", [P, 4, TOPK, 2], I32)
            U = [ph.enter_context(nc.psum_tensor(f"U{i}", [P, 2, 2 * P], F32)) for i in range(2)]
            G = [ph.enter_context(nc.psum_tensor(f"G{i}", [P, 2, 2 * P], F32)) for i in range(2)]
            Y = [ph.enter_context(nc.psum_tensor(f"Y{i}", [P, D], F32)) for i in range(2)]
            s_hl, s_ht, s_st = sems("s_hl", 4), sems("s_ht", 4), sems("s_st", 3)
            s_up, s_sl, s_ml, s_dn, s_ad, s_ix = (sem(n) for n in ("s_up", "s_sl", "s_ml", "s_dn", "s_ad", "s_ix"))
            s_xh3, s_xl3, s_fh, s_fl, s_wh, s_wl = (sem(n) for n in ("s_xh3", "s_xl3", "s_fh", "s_fl", "s_wh", "s_wl"))
            s_ast, s_scat = sems("s_ast", 2), sems("s_scat", 4)
            NP = NB // 2
            onp = stage_on(NP)
            RANGE3 = (-4, NP + 1, 4, NP - 4, 4)

            def matrices(t, k):
                return [((t - k) * 3 + 2 * i, i % 3, (t - k) // 2 + k // 2) for i in ((0, 1), (2,), (3, 4), (5,))[k]]

            def loads(t, k):
                return (t - k) * 8 + k // 2 * 16 + 16

            one = lambda e: bass.ds(e, 1)
            with nc.Block() as block:
                @block.sync
                def _(sp):
                    sp.dma_start(rbb[:, :], rb.rearrange("(o e) -> o e", o=1).broadcast_to([P, E])).then_inc(s_rb, 16)

                    def body(t, k):
                        if onp(t + 1):
                            for n2, kind, e in matrices(t + 1, (k + 1) % 4):
                                if due(n2 - 4):
                                    sp.wait_ge(s_wl, n2 - 4)
                                w = (W3, W1, W2)[kind]
                                sp.dma_start(stage[:, kind, :].rearrange("p (c n) -> p c n", n=w.shape[2]),
                                             w[one(e), :, :].rearrange("o k n -> (o k) n").rearrange(
                                                 "(c p) n -> p c n", p=P)).then_inc(s_st[kind], 16)
                        if onp(t + 4):
                            if due(2 * t + 2):
                                sp.wait_ge(s_ad, 2 * t + 2)
                            sp.dma_start(hs[:, k, :, :, :].rearrange("p t c n -> p t (c n)"),
                                         h1T_d[bass.ds((t + 4) * 2, 2), :, :].rearrange("t p n -> p t n")
                                         ).then_inc(s_hl[k], 16)
                            sp.dma_start(xr[:, k, :, :],
                                         x1_d[bass.ds((t + 4) * 2, 2), :, :].rearrange("t p n -> p t n")
                                         ).then_inc(s_hl[k], 16)
                        if onp(t):
                            sp.wait_ge(s_ad, 2 * t + 2)
                            sp.dma_start(acc_d[bass.ds(t * 2, 2), :, :].rearrange("t p n -> p t n"),
                                         ao[:, k % 2, :, :]).then_inc(s_ast[k % 2], 16)
                        if onp(t + 3):
                            a = (k + 3) % 4
                            if due((t + 3 - a) * 16):
                                sp.wait_ge(s_scat[a], (t + 3 - a) * 16)
                            sp.dma_start(ht[:, a, :, :], h1_d[bass.ds((t + 3) * 2, 2), :, :].rearrange("t p n -> p t n")
                                         ).then_inc(s_ht[a], 16)

                    steps(sp, *RANGE3, body)
                    for j in range(2):
                        sp.wait_ge(s_ast[j], 16 * (NP // 2))

                @block.tensor
                def _(pe):
                    def up(t, k, h):
                        if onp(t):
                            pe.wait_ge(s_xl3, t + 1)
                            if due(2 * t - 1 + h):
                                pe.wait_ge(s_ml, 2 * t - 1 + h)
                            for kind, bank in ((0, G[h]), (1, U[h])):
                                for i in range(2):
                                    b = (2 * h + i) * P
                                    for j, (wp, xp) in enumerate(PARTS):
                                        for c in range(C):
                                            last = nc.tensor.matmul(
                                                bank[:, i, :], wsm[:, kind, wp, c * HS + b:c * HS + b + P],
                                                hp[:, k % 2, xp, :, c, :], start=j == 0 and c == 0,
                                                stop=j == 2 and c == C - 1)
                            last.then_inc(s_up, 1)

                    def down(t, k, j):
                        if onp(t):
                            pe.wait_ge(s_fl, 2 * t + 2)
                            if due(2 * t - 1 + j):
                                pe.wait_ge(s_ad, 2 * t - 1 + j)
                            for i, (xp, wp) in enumerate(PARTS):
                                for c in range(HSC):
                                    last = nc.tensor.matmul(Y[j][:, :], hh[:, k % 2, xp, c, j * P:(j + 1) * P],
                                                            wsm[:, 2, wp, c * D:(c + 1) * D], start=i == 0 and c == 0,
                                                            stop=i == 2 and c == HSC - 1)
                            last.then_inc(s_dn, 1)

                    def body(t, k):
                        up(t, k, 0)
                        down(t - 1, k + 1, 0)
                        up(t, k, 1)
                        down(t - 1, k + 1, 1)
                        if isinstance(t, int) and t == 0:
                            pe.wait_ge(s_i, 5)
                            pe.wait_ge(s_v, MASK_AT)
                            nc.tensor.matmul(R[:, 0, :, :], upper[:, :], mask[:, :, :], start=True, stop=True)
                            nc.tensor.matmul(R[:, 1, :, :], ones[:, :], mask[:, :, :], start=True,
                                             stop=True).then_inc(s_mm, 1)

                    steps(pe, 0, *RANGE3[1:], body)

                @block.scalar
                def _(act):
                    def body(t, k):
                        if isinstance(t, int) and t == 0:
                            act.wait_ge(s_v, GATE_AT)
                            nc.scalar.activation(gl[:, :, :], gl[:, :, :], ACT.Exp).then_inc(s_e, 1)
                        if onp(t + 1):
                            a = (k + 1) % 4
                            act.wait_ge(s_hl[a], (t + 1 - a) * 8 + 32)
                            if due(2 * t):
                                act.wait_ge(s_up, 2 * t)
                            nc.scalar.mul(hp[:, a % 2, HI, :, :, :], hs[:, a, :, :, :], XS).then_inc(s_xh3, 1)
                        if onp(t - 1):
                            for n2, kind, e in matrices(t - 1, (k - 1) % 4):
                                act.wait_ge(s_st[kind], loads(t - 1, (k - 1) % 4))
                                take_wait(nc.scalar)
                                nc.scalar.mul(wm[:, kind, one(e), HI, :].rearrange("p o n -> p (o n)"),
                                              stage[:, kind, :], WS).then_inc(s_wh, 2)
                        if onp(t):
                            for h in range(2):
                                act.wait_ge(s_up, 2 * t + h + 1)
                                if due(2 * t - 1 + h):
                                    act.wait_ge(s_ml, 2 * t - 1 + h)
                                nc.scalar.activation(sg[:, h, :, :], G[h][:, :, :], ACT.Silu,
                                                     scale=1 / (XS * WS)).then_inc(s_sl, 1)
                                act.wait_ge(s_ml, 2 * t + h + 1)
                                if due(2 * t - 2):
                                    act.wait_ge(s_dn, 2 * t - 2)
                                nc.scalar.copy(hh[:, k % 2, HI, 2 * h:2 * h + 2, :], hf[:, h, :, :]).then_inc(s_fh, 1)

                    steps(act, -4, *RANGE3[1:], body)

                @block.vector
                def _(dve):
                    done = [0]

                    def link(ins):
                        done[0] += 1
                        ins.then_inc(s_v, 1)
                        dve.wait_ge(s_v, done[0])

                    TT, TS, RED = nc.vector.tensor_tensor, nc.vector.tensor_scalar, nc.vector.tensor_reduce
                    over_b = lambda a: a.unsqueeze(1).broadcast_to([P, NB, E])
                    over_e = lambda a: a.unsqueeze(2).broadcast_to([P, NB, E])

                    def choose():
                        dve.wait_ge(s_rb, 16)
                        dve.wait_ge(s_i, 5)
                        link(TT(sel[:, :, :], logits[:, :, :], over_b(rbb[:, :]), ALU.add))
                        for j in range(TOPK):
                            link(RED(top[:, :], sel[:, :, :], AX.X, ALU.max))
                            link(TT(t0[:, :, :], sel[:, :, :], over_e(top[:, :]), ALU.is_ge))
                            link(TT(t0[:, :, :], t0[:, :, :], over_b(revi[:, :]), ALU.mult))
                            link(RED(top[:, :], t0[:, :, :], AX.X, ALU.max))
                            link(TT(oh[:, j, :, :], over_b(revi[:, :]), over_e(top[:, :]), ALU.is_equal))
                            if j + 1 < TOPK:
                                link(TS(t0[:, :, :], oh[:, j, :, :], -1.0, 1.0, ALU.mult, ALU.add))
                                link(TT(sel[:, :, :], sel[:, :, :], t0[:, :, :], ALU.mult))
                                link(TS(t0[:, :, :], oh[:, j, :, :], -3.0e38, None, ALU.mult))
                                link(TT(sel[:, :, :], sel[:, :, :], t0[:, :, :], ALU.add))
                        link(TT(mask[:, :, :], oh[:, 0, :, :], oh[:, 1, :, :], ALU.add))
                        assert done[0] == MASK_AT, done
                        for j in range(TOPK):
                            link(TT(t0[:, :, :], logits[:, :, :], oh[:, j, :, :], ALU.mult))
                            link(RED(gl[:, j, :], t0[:, :, :], AX.X, ALU.add))
                        link(TT(top[:, :], gl[:, 0, :], gl[:, 1, :], ALU.max))
                        link(TT(gl[:, :, :], gl[:, :, :], top[:, :].unsqueeze(1).broadcast_to([P, TOPK, NB]), ALU.subtract))
                        assert done[0] == GATE_AT, done

                    def place():
                        dve.wait_ge(s_e, 1)
                        link(TT(top[:, :], gl[:, 0, :], gl[:, 1, :], ALU.add))
                        link(nc.vector.reciprocal(top[:, :], top[:, :]))
                        link(TT(gate[:, :, :], gl[:, :, :], top[:, :].unsqueeze(1).broadcast_to([P, TOPK, NB]), ALU.mult))
                        dve.wait_ge(s_mm, 1)
                        link(nc.vector.tensor_copy(tot[:, :, :], R[:, 1, :, :].rearrange("p b e -> p e b")))
                        link(nc.vector.tensor_tensor_scan(cum[:, :, :].rearrange("p e b -> p (e b)"),
                                                          tot[:, :, :].rearrange("p e b -> p (e b)"),
                                                          zb[:, :], 0.0, ALU.add, ALU.add))
                        link(nc.vector.memset(start[:, 0:1], 0.0))
                        link(nc.vector.tensor_copy(start[:, 1:E], cum[:, 0:E - 1, NB - 1]))
                        link(TT(cnt[:, :], cum[:, :, NB - 1], start[:, :], ALU.subtract))
                        link(TT(cum[:, :, :], cum[:, :, :], tot[:, :, :], ALU.subtract))
                        link(TS(cnti[:, :], cnt[:, :], float(P - 1), None, ALU.add))
                        link(TS(cnti[:, :], cnti[:, :], P.bit_length() - 1, None, ALU.logical_shift_right))
                        link(nc.vector.tensor_copy(tiles[:, :], cnti[:, :]))
                        link(nc.vector.tensor_tensor_scan(ctile[:, :], tiles[:, :], zb[:, 0:E], 0.0, ALU.add, ALU.add))
                        link(TT(off[:, :], ctile[:, :], tiles[:, :], ALU.subtract))
                        link(TS(off[:, :], off[:, :], float(P), None, ALU.mult))
                        link(TT(off[:, :], off[:, :], start[:, :], ALU.subtract))
                        link(TT(sel[:, :, :], R[:, 0, :, :], cum[:, :, :].rearrange("p e b -> p b e"), ALU.add))
                        link(TT(sel[:, :, :], sel[:, :, :], over_b(off[:, :]), ALU.add))
                        for j in range(TOPK):
                            link(TT(t0[:, :, :], sel[:, :, :], oh[:, j, :, :], ALU.mult))
                            link(RED(slotf[:, j, :], t0[:, :, :], AX.X, ALU.add))
                        link(nc.vector.tensor_copy(slot[:, :, :], slotf[:, :, :]))
                        link(TT(le[:, :, :], ctile[0:1, :].unsqueeze(1).broadcast_to([1, NT, E]),
                                tid[:, :].unsqueeze(2).broadcast_to([1, NT, E]), ALU.is_le))
                        link(RED(tef[:, :], le[:, :, :], AX.X, ALU.add))
                        link(TS(tile_expert[:, :], tef[:, :], float(E - 1), None, ALU.min))
                        assert done[0] == ROUTED_AT, done

                    def mul(t, k, h):
                        if onp(t):
                            dve.wait_ge(s_sl, 2 * t + h + 1)
                            if due(2 * t - 1 + h):
                                dve.wait_ge(s_fh, 2 * t - 1 + h)
                            nc.vector.scalar_tensor_tensor(hf[:, h, :, :], U[h][:, :, :], ES / (XS * WS),
                                                           sg[:, h, :, :], ALU.mult, ALU.mult).then_inc(s_ml, 1)

                    def rest(t, k, h):
                        if onp(t):
                            dve.wait_ge(s_fh, 2 * t + h + 1)
                            nc.vector.tensor_tensor(hh[:, k % 2, LO, 2 * h:2 * h + 2, :], hf[:, h, :, :],
                                                    hh[:, k % 2, HI, 2 * h:2 * h + 2, :], ALU.subtract).then_inc(s_fl, 1)

                    def add(t, k, j):
                        if onp(t):
                            dve.wait_ge(s_dn, 2 * t + j + 1)
                            if due((t - k % 2) * 8):
                                dve.wait_ge(s_ast[k % 2], (t - k % 2) * 8)
                            nc.vector.scalar_tensor_tensor(ao[:, k % 2, j, :], Y[j][:, :], 1 / (ES * WS),
                                                           xr[:, k, j, :], ALU.mult, ALU.add).then_inc(s_ad, 1)

                    def body(t, k):
                        if onp(t + 1):
                            a = (k + 1) % 4
                            dve.wait_ge(s_xh3, t + 2)
                            nc.vector.scalar_tensor_tensor(hp[:, a % 2, LO, :, :, :], hs[:, a, :, :, :], XS,
                                                           hp[:, a % 2, HI, :, :, :], ALU.mult,
                                                           ALU.subtract).then_inc(s_xl3, 1)
                        if onp(t - 1):
                            for n2, kind, e in matrices(t - 1, (k - 1) % 4):
                                dve.wait_ge(s_wh, n2 + 2)
                                nc.vector.scalar_tensor_tensor(
                                    wm[:, kind, one(e), LO, :].rearrange("p o n -> p (o n)"), stage[:, kind, :], WS,
                                    wm[:, kind, one(e), HI, :].rearrange("p o n -> p (o n)"), ALU.mult,
                                    ALU.subtract).then_inc(s_wl, 2)
                        mul(t, k, 0)
                        rest(t, k, 0)
                        add(t - 1, (k - 1) % 4, 0)
                        mul(t, k, 1)
                        rest(t, k, 1)
                        add(t - 1, (k - 1) % 4, 1)
                        if isinstance(t, int) and t == -1:
                            choose()
                        if isinstance(t, int) and t == 0:
                            place()

                    steps(dve, -4, *RANGE3[1:], body)

                @block.gpsimd
                def _(pool):
                    nc.gpsimd.iota(revi[:, :], pattern=[[-1, E]], base=E, channel_multiplier=0,
                                   allow_small_or_imprecise_dtypes=True).then_inc(s_i, 1)
                    nc.gpsimd.iota(tid[:, :], pattern=[[1, NT]], base=0, channel_multiplier=0,
                                   allow_small_or_imprecise_dtypes=True).then_inc(s_i, 1)
                    nc.gpsimd.memset(zb[:, :], 0.0).then_inc(s_i, 1)
                    nc.gpsimd.memset(upper[:, :], 1.0).then_inc(s_i, 1)
                    pool.wait_ge(s_i, 4)
                    nc.gpsimd.affine_select(out=upper[:, :], in_=upper[:, :], compare_op=ALU.is_gt, fill=0.0,
                                            base=0, pattern=[[1, P]], channel_multiplier=-1).then_inc(s_i, 1)
                    pool.wait_ge(s_zero, 16 * (NT // 2))
                    pool.wait_ge(s_v, ROUTED_AT)

                    def rows(t, k):
                        if onp(t):
                            if due((t - k) * 16):
                                pool.wait_ge(s_scat[k], (t - k) * 16)
                            take_wait(nc.gpsimd)
                            nc.gpsimd.tensor_copy(ix[:, k, :, :], slot[:, :, bass.ds(t * 2, 2)]).then_inc(s_ix, 1)

                    def body(t, k):
                        rows(t + 1, (k + 1) % 4)
                        if onp(t):
                            pool.wait_ge(s_ix, t + 1)
                            pool.wait_ge(s_ht[k], (t - k) * 4 + 16)
                            take_wait(nc.gpsimd)
                            for i in range(2):
                                for j in range(TOPK):
                                    nc.gpsimd.indirect_dma_start(
                                        out=xs_d[:, :],
                                        out_offset=bass.IndirectOffsetOnAxis(ap=ix[:, k, j, i:i + 1], axis=0),
                                        in_=ht[:, k, i, :], in_offset=None).then_inc(s_scat[k], 16)

                    steps(pool, -1, NP, 4, NP - 4, 4, body)
                    for k in range(4):
                        pool.wait_ge(s_scat[k], 64 * (NP // 4))

        shared.close()
        per = lambda name, shape, dt=F32: ctx.enter_context(nc.sbuf_tensor(name, shape, dt))
        wut = per("wut", [P, FC, D + 1])
        wdn = per("wdn", [P, FC, D])
        bup = per("bup", [P, FC])
        wl = per("wl", [P, 4 * C, D])
        wmax = per("wmax", [P, 4])
        wexp = per("wexp", [P, 3, 2], I32)
        wscale = per("wscale", [P, 2, 2], I32)
        wdesc = per("wdesc", [P, 2])
        with ExitStack() as ph:
            sb = lambda name, shape, dt=F32: ph.enter_context(nc.sbuf_tensor(name, shape, dt))
            xe = sb("xe", [P, 4, D])
            xT = sb("xT", [P, 2, 2, C, P], F16)
            sg4 = sb("sg4", [P, 2, H])
            he = sb("he", [P, 2, H])
            hT = sb("hT", [P, 2, 2, HC, P], F16)
            ye = sb("ye", [P, 2, D])
            bw = sb("bw", [P, 2, F // 2, 4])
            bt = sb("bt", [P, 2, F // 2])
            by = sb("by", [P, 2, F // 2])
            bdiag = sb("bdiag", [P, 2, F])
            big = sb("big", [P, 2, 3, FC // 2, 4])
            bt4 = sb("bt4", [P, 4, D + 1])
            ub = sb("ub", [P, FC])
            Ue = [ph.enter_context(nc.psum_tensor(f"Ue{i}", [P, H], F32)) for i in range(2)]
            Ge = [ph.enter_context(nc.psum_tensor(f"Ge{i}", [P, H], F32)) for i in range(2)]
            XB = ph.enter_context(nc.psum_tensor("XB", [P, 4, P], F32))
            HT = ph.enter_context(nc.psum_tensor("HT", [P, HC, P], F32))
            YB = [ph.enter_context(nc.psum_tensor(f"YB{i}", [P, 2, D], F32)) for i in range(2)]
            XT, Ye = XB[:, 0:C, :], [y[:, 0, :] for y in YB]
            Wf, Bf = [y[:, 1, :] for y in YB], XB[:, C, 0:FC]
            s_xe = sems("s_xe", 4)
            s_xt, s_xte, s_g, s_u, s_sl4, s_he = (sem(n) for n in ("s_xt", "s_xte", "s_g", "s_u", "s_sl4", "s_he"))
            s_hT, s_hTe, s_ye, s_yc = (sem(n) for n in ("s_hT", "s_hTe", "s_ye", "s_yc"))
            s_yst = sems("s_yst", 2)
            s_xh4, s_hh4 = sem("s_xh4"), sem("s_hh4")
            s_bl, s_bo = sem("s_bl"), sem("s_bo")
            s_bm, s_bv = sem("s_bm"), sem("s_bv")
            FOLD_AT = 2 + 14 * 6 + 3 * FC // 2 * 6
            FOLDED_AT = FOLD_AT + 3 * FC // 2 * 6 + 1
            LATE = 64
            MID = 44
            s_bw = sems("s_bw", 2)
            on4 = stage_on(NT)
            RANGE4 = (-4, NT + 2, 4, NT - 4, 4)
            with nc.Block() as block:
                @block.sync
                def _(sp):
                    def body(t, k):
                        if on4(t + 4):
                            if due(t + 1):
                                sp.wait_ge(s_xt, t + 1)
                            sp.dma_start(xe[:, k, :], xs_d[bass.ds((t + 4) * P, P), :]).then_inc(s_xe[k], 16)
                        if on4(t - 1):
                            j = (k - 1) % 2
                            sp.wait_ge(s_yc, t)
                            sp.dma_start(ys_d[bass.ds((t - 1) * P, P), :], ye[:, j, :]).then_inc(s_yst[j], 16)

                    steps(sp, *RANGE4, body)
                    for j in range(2):
                        sp.wait_ge(s_yst[j], 16 * (NT // 2))

                @block.tensor
                def _(pe):
                    def xtr(t, k):
                        if on4(t):
                            pe.wait_ge(s_xe[k % 4], (t - k % 4) * 4 + 16)
                            if due(t):
                                pe.wait_ge(s_xte, t)
                            for c in range(C):
                                last = nc.tensor.transpose(XT[:, c, :], xe[:, k % 4, c * P:(c + 1) * P], ident[:, :])
                            last.then_inc(s_xt, 1)

                    experts = {}
                    expert = lambda t: pe.value_load(tile_expert[0:1, bass.ds(t, 1)], min_val=0, max_val=E - 1)

                    def product(bank, left, kind, e, chunks, width):
                        for i, (xp, wp) in enumerate(PARTS):
                            for c in range(chunks):
                                last = nc.tensor.matmul(bank, left[:, xp, c, :],
                                                        wm[:, kind, bass.ds(e, 1), wp, c * width:(c + 1) * width],
                                                        start=i == 0 and c == 0, stop=i == 2 and c == chunks - 1)
                        return last

                    def body(t, k):
                        if isinstance(t, int) and t < 0:
                            if t == -1:
                                xtr(0, 0)
                            return
                        a, b = k % 2, (k - 1) % 2
                        before = experts.get(k - 1)
                        if before is None and on4(t - 1):
                            before = expert(t - 1)
                        experts.clear()
                        e = experts[k] = expert(t) if on4(t) else None
                        if on4(t - 1):
                            pe.wait_ge(s_he, t)
                            if due(t - 1):
                                pe.wait_ge(s_hTe, t - 1)
                            for c in range(HC):
                                last = nc.tensor.transpose(HT[:, c, :], he[:, b, c * P:(c + 1) * P], ident[:, :])
                            last.then_inc(s_hT, 1)
                        if on4(t):
                            pe.wait_ge(s_xte, t + 1)
                            if due(t - 1):
                                pe.wait_ge(s_sl4, t - 1)
                            product(Ge[a][:, :], xT[:, a, :, :, :], 0, e, C, H).then_inc(s_g, 1)
                        xtr(t + 1, k + 1)
                        if on4(t):
                            if due(t - 1):
                                pe.wait_ge(s_he, t - 1)
                            product(Ue[a][:, :], xT[:, a, :, :, :], 1, e, C, H).then_inc(s_u, 1)
                        if on4(t - 1):
                            pe.wait_ge(s_hTe, t)
                            if due(t - 2):
                                pe.wait_ge(s_yc, t - 2)
                            product(Ye[b], hT[:, b, :, :, :], 2, before, HC, D).then_inc(s_ye, 1)

                    steps(pe, RANGE4[0], MID, RANGE4[2], MID, 4, body)
                    pe.wait_ge(s_bo, FOLD_AT)
                    pe.wait_ge(s_xte, MID + 1)
                    pe.wait_ge(s_yc, MID - 1)
                    for b in range(FC):
                        nc.tensor.matmul(Bf[:, b:b + 1], bdiag[:, 0, b * P:(b + 1) * P], wut[:, b, D:D + 1],
                                         start=True, stop=True).then_inc(s_bm, 1)
                    for i in range(2 * FC):
                        b, w = i % FC, (wut, wdn)[i // FC]
                        if i >= 2:
                            pe.wait_ge(s_bv, i - 1)
                        nc.tensor.matmul(Wf[i % 2], bdiag[:, i // FC, b * P:(b + 1) * P], w[:, b, 0:D],
                                         start=True, stop=True).then_inc(s_bm, 1)
                    pe.wait_ge(s_bv, 2 * FC + 1)
                    steps(pe, MID, RANGE4[1], MID, RANGE4[3], 4, body)

                @block.scalar
                def _(act):
                    def body(t, k):
                        if on4(t - 1):
                            act.wait_ge(s_hT, t)
                            if due(t - 2):
                                act.wait_ge(s_ye, t - 2)
                            nc.scalar.copy(hT[:, (k - 1) % 2, HI, :, :], HT[:, :, :]).then_inc(s_hh4, 1)
                        if on4(t):
                            act.wait_ge(s_g, t + 1)
                            if due(t - 1):
                                act.wait_ge(s_he, t - 1)
                            nc.scalar.activation(sg4[:, k % 2, :], Ge[k % 2][:, :], ACT.Silu,
                                                 scale=1 / (XS * WS)).then_inc(s_sl4, 1)
                        if on4(t + 1):
                            act.wait_ge(s_xt, t + 2)
                            if due(t):
                                act.wait_ge(s_u, t)
                            nc.scalar.mul(xT[:, (k + 1) % 2, HI, :, :], XT, XS).then_inc(s_xh4, 1)

                    steps(act, *RANGE4, body)

                @block.vector
                def _(dve):
                    STT = nc.vector.scalar_tensor_tensor

                    def body(t, k):
                        if on4(t - 1):
                            j = (k - 1) % 2
                            dve.wait_ge(s_hh4, t)
                            nc.vector.tensor_tensor(hT[:, j, LO, :, :], HT[:, :, :], hT[:, j, HI, :, :],
                                                    ALU.subtract).then_inc(s_hTe, 1)
                        if on4(t + 1):
                            j = (k + 1) % 2
                            dve.wait_ge(s_xh4, t + 2)
                            STT(xT[:, j, LO, :, :], XT, XS, xT[:, j, HI, :, :],
                                ALU.mult, ALU.subtract).then_inc(s_xte, 1)
                        if on4(t):
                            dve.wait_ge(s_sl4, t + 1)
                            dve.wait_ge(s_u, t + 1)
                            if due(t - 1):
                                dve.wait_ge(s_hT, t - 1)
                            STT(he[:, k % 2, :], Ue[k % 2][:, :], ES / (XS * WS), sg4[:, k % 2, :],
                                ALU.mult, ALU.mult).then_inc(s_he, 1)
                        if on4(t - 1):
                            j = (k - 1) % 2
                            dve.wait_ge(s_ye, t)
                            if due((t - 1 - j) * 8):
                                dve.wait_ge(s_yst[j], (t - 1 - j) * 8)
                            nc.vector.tensor_scalar(ye[:, j, :], Ye[j], 1 / (ES * WS), None,
                                                    ALU.mult).then_inc(s_yc, 1)

                    steps(dve, RANGE4[0], MID, RANGE4[2], MID, 4, body)
                    for i in range(2 * FC):
                        b, w = i % FC, (wut, wdn)[i // FC]
                        dve.wait_ge(s_bm, FC + i + 1)
                        nc.vector.tensor_copy(w[:, b, 0:D], Wf[i % 2]).then_inc(s_bv, 1)
                    nc.vector.tensor_copy(wut[:, :, D], Bf).then_inc(s_bv, 1)
                    steps(dve, MID, LATE, MID, LATE, 4, body)
                    dve.wait_ge(s_bo, FOLDED_AT)
                    for i, w in enumerate((wut, wdn)):
                        nc.vector.tensor_reduce(wmax[:, i:i + 1], w[:, :, 0:D], AX.XY, ALU.max,
                                                apply_absolute_value=True).then_inc(s_bv, 1)
                    steps(dve, LATE, RANGE4[1], LATE, RANGE4[3], 4, body)

                @block.gpsimd
                def _(pool):
                    cols = lambda a: a.rearrange("(c p) -> p c", p=P)
                    pool.dma_start(wut[:, :, 0:D], WexpT.rearrange("(c p) d -> p c d", p=P)).then_inc(s_bl, 16)
                    pool.dma_start(wut[:, :, D], cols(b_exp), allow_slow_non_contiguous=True).then_inc(s_bl, 16)
                    pool.dma_start(ub[:, :], cols(up_bias), allow_slow_non_contiguous=True).then_inc(s_bl, 16)
                    pool.dma_start(wdn[:, :, :], W_con.rearrange("(c p) d -> p c d", p=P)).then_inc(s_bl, 16)
                    pool.dma_start(wl[:, :, :], WlT.rearrange("(c p) d -> p c d", p=P)).then_inc(s_bl, 16)
                    NS = P.bit_length() - 1
                    for j, w in enumerate((up_w, dn_w)):
                        for i in range(3):
                            pool.dma_start(big[:, j, i, :, :], w[NS + i].rearrange("(q p) i j -> p q (i j)", p=P),
                                           allow_slow_non_contiguous=True).then_inc(s_bl, 16)
                    plan = [(up_w, s, 0) for s in range(NS)] + [(dn_w, s, 1) for s in reversed(range(NS))]
                    count = [0]
                    TT = nc.gpsimd.tensor_tensor

                    def load(n):
                        w, s, _ = plan[n]
                        pool.dma_start(bw[:, n % 2, :, :].rearrange("p k f -> p (k f)"),
                                       w[s].rearrange("k i j -> (k i j)").unsqueeze(0).broadcast_to([P, 2 * F])
                                       ).then_inc(s_bw[n % 2], 16)

                    def link(ins):
                        count[0] += 1
                        ins.then_inc(s_bo, 1)
                        pool.wait_ge(s_bo, count[0])

                    def rotate(a, b, w, flip, t):
                        aa, ab, ba, bb = (0, 2, 1, 3) if flip else (0, 1, 2, 3)
                        TT(out=t[0], in0=w(aa), in1=a, op=ALU.mult).then_inc(s_bo, 1)
                        TT(out=t[1], in0=w(ab), in1=b, op=ALU.mult).then_inc(s_bo, 1)
                        TT(out=t[2], in0=w(ba), in1=a, op=ALU.mult).then_inc(s_bo, 1)
                        count[0] += 3
                        link(TT(out=t[3], in0=w(bb), in1=b, op=ALU.mult))
                        TT(out=a, in0=t[0], in1=t[1], op=ALU.add).then_inc(s_bo, 1)
                        count[0] += 1
                        link(TT(out=b, in0=t[2], in1=t[3], op=ALU.add))

                    def between_blocks(mat, width, j, i):
                        st = 2 ** i
                        for q in range(FC // 2):
                            a = q // st * 2 * st + q % st
                            rotate(mat[:, a, :], mat[:, a + st, :],
                                   lambda f: big[:, j, i, q, f:f + 1].broadcast_to([P, width]), j == 1,
                                   [bt4[:, x, 0:width] for x in range(4)])

                    load(0)
                    load(1)
                    pool.wait_ge(s_bl, 16 * 11)
                    for j in range(2):
                        link(TT(out=bdiag[:, j, :].rearrange("p (b n) -> p b n", n=P),
                                in0=ident[:, :].unsqueeze(1).broadcast_to([P, FC, P]),
                                in1=ones[:, :].unsqueeze(1).broadcast_to([P, FC, P]), op=ALU.mult))
                    for n, (w, s, j) in enumerate(plan):
                        st = 2 ** s
                        pool.wait_ge(s_bw[n % 2], 16 * (n // 2 + 1))
                        v = bdiag[:, j, :].rearrange("p (k i s) -> p k i s", i=2, s=st)
                        c = bw[:, n % 2, :, :].rearrange("p (k s) f -> p k s f", s=st)
                        rotate(v[:, :, 0, :], v[:, :, 1, :], lambda f: c[:, :, :, f], j == 1,
                               [x[:, y, :].rearrange("p (k s) -> p k s", s=st) for x in (bt, by) for y in range(2)])
                        if n + 2 < len(plan):
                            load(n + 2)
                    for i in reversed(range(3)):
                        between_blocks(wdn, D, 1, i)
                    assert count[0] == FOLD_AT, count
                    pool.wait_ge(s_bv, 2 * FC + 1)
                    for i in range(3):
                        between_blocks(wut, D + 1, 0, i)
                    link(TT(out=bup[:, :], in0=wut[:, :, D], in1=ub[:, :], op=ALU.add))
                    assert count[0] == FOLDED_AT, count
                    for i in range(2):
                        pool.wait_ge(s_bv, 2 * FC + 2 + i)
                        nc.gpsimd.partition_all_reduce(wmax[:, 2 + i:3 + i], wmax[:, i:i + 1], P,
                                                       bass.bass_isa.ReduceOp.max).then_inc(s_bo, 1)

        with ExitStack() as ph:
            sb = lambda name, shape, dt=F32: ph.enter_context(nc.sbuf_tensor(name, shape, dt))
            ax = sb("ax", [P, 4, D])
            cx = sb("cx", [P, 4, D])
            yg = sb("yg", [P, 4, TOPK, D])
            ix5 = sb("ix5", [P, 4, TOPK, 1], I32)
            x2 = sb("x2", [P, 4, D])
            st5 = sb("st5", [P, 4, 6])
            mv5 = sb("mv5", [P, 4, 2])
            rs5 = sb("rs5", [P, 4, 2])
            c5 = sb("c5", [P, 4, D])
            cT = sb("cT", [P, 4, C, P])
            cw = sb("cw", [P, 2, C, P])
            qT = sb("qT", [P, 2, C, P])
            dots = sb("dots", [P, D])
            rr = sb("rr", [P, 4, 1])
            m5 = sb("m5", [P, 4, 1])
            xbl = sb("xbl", [P, 2, D])
            nm5 = sb("nm5", [P, 4, 2])
            pa = sb("pa", [P, 2, P])
            ps = sb("ps", [P, 4, 2])
            aT = sb("aT", [P, 2, P])
            gmax = sb("gmax", [P, 4, 1])
            be = sb("be", [P, 4, 1])
            q2 = sb("q2", [P, 4, 4])
            wz = sb("wz", [P, 2, C, D])
            uT = sb("uT", [P, 2, C, P])
            vT = sb("vT", [P, 2, C, P])
            x3 = sb("x3", [P, 2, D])
            wcq = sb("wcq", [P, 2, C])
            wcb = sb("wcb", [P, D])
            bias3 = sb("bias3", [P, 4])
            blb = sb("blb", [P, D])
            T5 = ph.enter_context(nc.psum_tensor("T5", [P, 2 * C, P], F32))
            S5 = ph.enter_context(nc.psum_tensor("S5", [P, P], F32))
            A5 = ph.enter_context(nc.psum_tensor("A5", [P, P], F32))
            U5 = ph.enter_context(nc.psum_tensor("U5", [P, C, P], F32))
            Q5 = ph.enter_context(nc.psum_tensor("Q5", [P, 4], F32))
            Z5 = [ph.enter_context(nc.psum_tensor(f"Z5{i}", [P, D], F32)) for i in range(2)]
            s_w5, s_b5 = sem("s_w5"), sem("s_b5")
            s_l5, s_g5 = sems("s_l5", 4), sems("s_g5", 4)
            s_x3st = sems("s_x3st", 2)
            (s_ix5, s_y1, s_x2, s_mv5, s_rs5, s_c5, s_t5, s_q5, s_ct, s_cw, s_dt, s_rr, s_s5, s_nm,
             s_M, s_gm, s_p5, s_pr5, s_an, s_a5, s_at, s_be, s_Q, s_qc, s_qr, s_qn, s_wz, s_u5, s_ut, s_vt, s_z, s_xb,
             s_x3) = (sem(f"s5_{i}") for i in range(33))
            wup, wdp = wm[:, 0, 0:C, :, :], wm[:, 1, 0:2, :, :]
            s_wt6, s_we6 = sem("s_wt6"), sem("s_we6")
            s_wch, BASE_C = s_wl, 2 * 3 * E
            s_whi, BASE_H = s_wh, 2 * 3 * E
            HALF = FC // 2 * D
            half = lambda w, i: w[:, i * FC // 2:(i + 1) * FC // 2, :].rearrange("p b d -> p (b d)")
            SCALED_AT = 7
            s_a5l, BASE_A = s_hl, 32 * (NP // 4)
            RANGE5 = (-6, NB + 3, 4, NB - 8, 4)
            with nc.Block() as block:
                @block.sync
                def _(sp):
                    as_col = lambda a: a.rearrange("(c p) -> p c", p=P)
                    as_rows = lambda a, n: a.rearrange("(o d) -> o d", o=1).broadcast_to([P, n])
                    sp.dma_start(wcq[:, 0, :], as_col(w_cq), allow_slow_non_contiguous=True).then_inc(s_w5, 16)
                    sp.dma_start(wcq[:, 1, :], as_col(w_q), allow_slow_non_contiguous=True).then_inc(s_w5, 16)
                    sp.dma_start(wcb[:, :], as_rows(w_c, D)).then_inc(s_w5, 16)
                    sp.dma_start(blb[:, :], as_rows(b_l, D)).then_inc(s_w5, 16)
                    for i, b in enumerate((b_cq, b_c, b_q)):
                        sp.dma_start(bias3[:, i:i + 1], as_rows(b, 1)).then_inc(s_w5, 16)

                    def body(t, k):
                        if on(t + 6):
                            if due(t + 3):
                                sp.wait_ge(s_x2, t + 3)
                            sp.dma_start(ax[:, (k + 2) % 4, :], acc_d[t + 6, :, :]).then_inc(s_a5l[(k + 2) % 4], 16)
                        if on(t + 4):
                            if due(t + 1):
                                sp.wait_ge(s_u5, t + 1)
                            sp.dma_start(cx[:, k, :], ctx_in[t + 4, :, :]).then_inc(s_l5[k], 16)
                        if on(t):
                            sp.wait_ge(s_x3, t + 1)
                            sp.dma_start(x3_d[t, :, :], x3[:, k % 2, :]).then_inc(s_x3st[k % 2], 16)

                    steps(sp, *RANGE5, body)
                    for j in range(2):
                        sp.wait_ge(s_x3st[j], 16 * (NB // 2))

                @block.gpsimd
                def _(pool):
                    def gather(t, k):
                        if on(t):
                            if due(t - 3):
                                pool.wait_ge(s_x2, t - 3)
                            take_wait(nc.gpsimd)
                            nc.gpsimd.tensor_copy(ix5[:, k, :, :], slot[:, :, bass.ds(t, 1)]).then_inc(s_ix5, 1)
                            pool.wait_ge(s_ix5, t + 1)
                            take_wait(nc.gpsimd)
                            for j in range(TOPK):
                                nc.gpsimd.indirect_dma_start(
                                    out=yg[:, k, j, :], out_offset=None, in_=ys_d[:, :],
                                    in_offset=bass.IndirectOffsetOnAxis(ap=ix5[:, k, j, :], axis=0)
                                ).then_inc(s_g5[k], 16)

                    def body(t, k):
                        gather(t + 5, (k + 1) % 4)
                        if isinstance(t, int) and t == -5:
                            pool.wait_ge(s_w5, 16 * 7)
                            nc.gpsimd.tensor_tensor(out=bias3[:, 3:4], in0=bias3[:, 0:1], in1=bias3[:, 1:2],
                                                    op=ALU.add).then_inc(s_b5, 1)
                            pool.wait_ge(s_b5, 1)
                            nc.gpsimd.tensor_tensor(out=bias3[:, 0:1], in0=bias3[:, 3:4], in1=bias3[:, 2:3],
                                                    op=ALU.add).then_inc(s_b5, 1)
                        if on(t + 1):
                            a = (k + 1) % 4
                            pool.wait_ge(s_x2, t + 2)
                            if due(t):
                                pool.wait_ge(s_x3, t)
                            nc.gpsimd.tensor_tensor(out=xbl[:, a % 2, :], in0=x2[:, a, :], in1=blb[:, :],
                                                    op=ALU.add).then_inc(s_xb, 1)
                        if on(t + 2):
                            pool.wait_ge(s_M, t + 3)
                            a = (k + 2) % 4
                            take_wait(nc.gpsimd)
                            nc.gpsimd.partition_all_reduce(gmax[:, a, :], m5[:, a, :], P,
                                                           bass.bass_isa.ReduceOp.max).then_inc(s_gm, 1)
                        if on(t + 4):
                            a = k
                            pool.wait_ge(s_mv5, 2 * t + 10)
                            nc.gpsimd.tensor_tensor(out=rs5[:, a, 0:1], in0=mv5[:, a, 1:2], in1=epsc[:, :],
                                                    op=ALU.add).then_inc(s_rs5, 1)
                            pool.wait_ge(s_rs5, 2 * t + 9)
                            nc.gpsimd.tensor_tensor(out=rs5[:, a, 1:2], in0=rs5[:, a, 0:1], in1=mhalf[:, :],
                                                    op=ALU.pow).then_inc(s_rs5, 1)
                    steps(pool, *RANGE5, body)

                @block.vector
                def _(dve):
                    TT, TS, STT = nc.vector.tensor_tensor, nc.vector.tensor_scalar, nc.vector.scalar_tensor_tensor
                    chain = [0]

                    def link(ins):
                        chain[0] += 1
                        ins.then_inc(s_wch, 1)
                        dve.wait_ge(s_wch, BASE_C + chain[0])

                    EXP, BIAS = 23, 127
                    link(TS(wexp[:, 0, :], wmax[:, 2:4].bitcast(I32), EXP, None, ALU.logical_shift_right))
                    link(TS(wexp[:, 1, :], wexp[:, 0, :], -1.0, float(2 * BIAS + 12), ALU.mult, ALU.add))
                    link(TS(wexp[:, 1, :], wexp[:, 1, :], float(2 * BIAS), None, ALU.min))
                    link(TS(wexp[:, 2, :], wexp[:, 1, :], -1.0, float(2 * BIAS), ALU.mult, ALU.add))
                    link(TS(wscale[:, :, :], wexp[:, 1:3, :], EXP, None, ALU.logical_shift_left))
                    link(TS(wdesc[:, 0:1], wscale[:, 1, 0:1].bitcast(F32), 1 / XS, None, ALU.mult))
                    link(TS(wdesc[:, 1:2], wscale[:, 1, 1:2].bitcast(F32), 1 / GS, None, ALU.mult))
                    assert chain[0] == SCALED_AT, chain
                    for i in range(FC):
                        c, n = i * 2 // FC, i * 2 % FC * P
                        dve.wait_ge(s_whi, BASE_H + i + 1)
                        STT(wup[:, c, LO, n:n + 2 * P], Z5[i % 2][:, :], wscale[:, 0, 0:1].bitcast(F32),
                            wup[:, c, HI, n:n + 2 * P], ALU.mult, ALU.subtract).then_inc(s_we6, 1)
                    dve.wait_ge(s_b5, 2)

                    def residual(t, k):
                        if on(t):
                            dve.wait_ge(s_a5l[k], (t - k) * 4 + 16 + BASE_A)
                            dve.wait_ge(s_g5[k], (t - k) * 8 + 32)
                            if due(t - 3):
                                dve.wait_ge(s_xb, t - 3)
                            STT(ax[:, k, :], yg[:, k, 0, :], gate[:, 0, bass.ds(t, 1)], ax[:, k, :],
                                ALU.mult, ALU.add).then_inc(s_y1, 1)
                            dve.wait_ge(s_y1, t + 1)
                            STT(x2[:, k, :], yg[:, k, 1, :], gate[:, 1, bass.ds(t, 1)], ax[:, k, :],
                                ALU.mult, ALU.add).then_inc(s_x2, 1)
                            dve.wait_ge(s_x2, t + 1)
                            nc.vector.bn_stats(st5[:, k, :], x2[:, k, :]).then_inc(s_mv5, 1)
                            dve.wait_ge(s_mv5, 2 * t + 1)
                            take_wait(nc.vector)
                            nc.vector.bn_aggr(mv5[:, k, :], st5[:, k, :]).then_inc(s_mv5, 1)

                    def normed(t, k):
                        if on(t):
                            dve.wait_ge(s_rs5, 2 * t + 2)
                            if due(t - 3):
                                dve.wait_ge(s_z, t - 3)
                            TS(c5[:, k, :], x2[:, k, :], mv5[:, k, 0:1], rs5[:, k, 1:2],
                               ALU.subtract, ALU.mult).then_inc(s_c5, 1)
                            dve.wait_ge(s_c5, t + 1)
                            if due(t):
                                dve.wait_ge(s_dt, t)
                            STT(dots[:, :], c5[:, k, :], 1.0, wcb[:, :], ALU.mult, ALU.mult,
                                accum_out=rr[:, k, :]).then_inc(s_dt, 1)

                    def row_max(t, k):
                        if on(t):
                            dve.wait_ge(s_s5, t + 1)
                            dve.wait_ge(s_dt, t + 1)
                            nc.vector.tensor_reduce(nm5[:, k, 0:1], S5[:, :], AX.X, ALU.max,
                                                    negate=True).then_inc(s_nm, 1)
                            dve.wait_ge(s_nm, t + 1)
                            STT(m5[:, k, :], rr[:, k, :], bias3[:, 0:1], nm5[:, k, 0:1],
                                ALU.add, ALU.subtract).then_inc(s_M, 1)

                    def weights(t, k):
                        if on(t):
                            dve.wait_ge(s_p5, t + 1)
                            nc.vector.reciprocal(ps[:, k, 1:2], ps[:, k, 0:1]).then_inc(s_pr5, 1)

                    def gmax_neg(t, k):
                        if on(t):
                            dve.wait_ge(s_gm, t + 1)
                            TS(nm5[:, k, 1:2], gmax[:, k, :], -1.0, None, ALU.mult).then_inc(s_qn, 1)

                    def q2c(t, k):
                        if on(t):
                            dve.wait_ge(s_Q, t + 1)
                            nc.vector.reciprocal(q2[:, k, 3:4], Q5[:, 2:3]).then_inc(s_qr, 1)
                            dve.wait_ge(s_qr, t + 1)
                            TS(q2[:, k, 0:2], Q5[:, 0:2], q2[:, k, 3:4], None, ALU.mult).then_inc(s_qc, 1)
                            dve.wait_ge(s_qc, t + 1)
                            if due(t - 1):
                                dve.wait_ge(s_z, t - 1)
                            for c in range(C):
                                STT(wz[:, k % 2, c, :], wl[:, 3 * C + c, :], q2[:, k, c:c + 1], wl[:, c, :],
                                    ALU.mult, ALU.add).then_inc(s_wz, 1)

                    def attended(t, k):
                        if on(t):
                            dve.wait_ge(s_ut, t + 1)
                            if due(t - 1):
                                dve.wait_ge(s_z, t - 1)
                            TT(vT[:, k % 2, :, :], cT[:, k, :, :], uT[:, k % 2, :, :], ALU.mult).then_inc(s_vt, 1)

                    def finish(t, k):
                        if on(t):
                            dve.wait_ge(s_z, t + 1)
                            if due((t - k % 2) * 8):
                                dve.wait_ge(s_x3st[k % 2], (t - k % 2) * 8)
                            dve.wait_ge(s_xb, t + 1)
                            TT(x3[:, k % 2, :], Z5[k % 2][:, :], xbl[:, k % 2, :], ALU.add).then_inc(s_x3, 1)

                    def body(t, k):
                        q = lambda n: (k + n) % 4
                        normed(t + 3, q(3))
                        q2c(t, k)
                        row_max(t + 2, q(2))
                        residual(t + 4, k)
                        attended(t + 1, q(1))
                        weights(t + 2, q(2))
                        gmax_neg(t + 2, q(2))
                        finish(t, k)

                    steps(dve, *RANGE5, body)
                    for i in range(2):
                        dve.wait_ge(s_whi, BASE_H + FC + i + 1)
                        STT(wdp[:, i, LO, :], half(wdn, i), wscale[:, 0, 1:2].bitcast(F32), wdp[:, i, HI, :],
                            ALU.mult, ALU.subtract).then_inc(s_we6, 1)

                @block.scalar
                def _(act):
                    act.wait_ge(s_wch, BASE_C + SCALED_AT)
                    for i in range(FC):
                        c, n = i * 2 // FC, i * 2 % FC * P
                        act.wait_ge(s_wt6, i + 1)
                        nc.scalar.mul(wup[:, c, HI, n:n + 2 * P], Z5[i % 2][:, :],
                                      wscale[:, 0, 0:1].bitcast(F32)).then_inc(s_whi, 1)

                    def body(t, k):
                        q = lambda n: (k + n) % 4
                        if on(t + 1):
                            a = q(1)
                            act.wait_ge(s_a5, t + 2)
                            if due(t):
                                act.wait_ge(s_u5, t)
                            nc.scalar.copy(aT[:, a % 2, :], A5[:, :]).then_inc(s_at, 1)
                        if on(t + 2):
                            a = q(2)
                            act.wait_ge(s_nm, t + 3)
                            if due(t + 1):
                                act.wait_ge(s_a5, t + 1)
                            nc.scalar.activation(pa[:, a % 2, :], S5[:, :], ACT.Exp, bias=nm5[:, a, 0:1],
                                                 accum_out=ps[:, a, 0:1]).then_inc(s_p5, 1)
                        if on(t + 1):
                            a = q(1)
                            act.wait_ge(s_u5, t + 2)
                            if due(t):
                                act.wait_ge(s_z, t)
                            if due(t):
                                act.wait_ge(s_vt, t)
                            nc.scalar.copy(uT[:, a % 2, :, :], U5[:, :, :]).then_inc(s_ut, 1)
                        if on(t + 3):
                            a = q(3)
                            act.wait_ge(s_t5, t + 4)
                            if due(t + 2):
                                act.wait_ge(s_s5, t + 2)
                            if due(t):
                                act.wait_ge(s_z, t)
                            for c in range(C):
                                nc.scalar.activation(cw[:, a % 2, c, :], T5[:, c, :], ACT.Identity,
                                                     scale=wcq[:, 0, c:c + 1], bias=wcq[:, 1, c:c + 1]).then_inc(s_cw, 1)
                            nc.scalar.copy(cT[:, a, :, :], T5[:, 0:C, :]).then_inc(s_ct, 1)
                            nc.scalar.copy(qT[:, a % 2, :, :], T5[:, C:2 * C, :]).then_inc(s_q5, 1)
                        if on(t + 2):
                            a = q(2)
                            act.wait_ge(s_pr5, t + 3)
                            nc.scalar.mul(pa[:, a % 2, :], pa[:, a % 2, :], ps[:, a, 1:2]).then_inc(s_an, 1)
                            act.wait_ge(s_qn, t + 3)
                            nc.scalar.activation(be[:, a, :], m5[:, a, :], ACT.Exp, bias=nm5[:, a, 1:2]).then_inc(s_be, 1)

                    steps(act, *RANGE5, body)
                    for i in range(2):
                        nc.scalar.mul(wdp[:, i, HI, :], half(wdn, i), wscale[:, 0, 1:2].bitcast(F32)).then_inc(s_whi, 1)

                @block.tensor
                def _(pe):
                    for i in range(FC):
                        c, b = i * 2 // FC, i * 2 % FC
                        if i >= 2:
                            pe.wait_ge(s_we6, i - 1)
                        for j in range(2):
                            last = nc.tensor.transpose(Z5[i % 2][:, j * P:(j + 1) * P], wut[:, b + j, c * P:(c + 1) * P],
                                                       ident[:, :])
                        last.then_inc(s_wt6, 1)
                    pe.wait_ge(s_we6, FC)

                    def project(t, k, operand, chunk, first=False, final=False):
                        for c in range(C):
                            last = nc.tensor.matmul(Z5[k % 2][:, :], operand[c], chunk[c],
                                                    start=first and c == 0, stop=final and c == C - 1)
                        return last

                    def body(t, k):
                        q = lambda n: (k + n) % 4
                        if on(t + 2):
                            a = q(2)
                            pe.wait_ge(s_cw, 2 * t + 6)
                            pe.wait_ge(s_q5, t + 3)
                            if due(t + 2):
                                pe.wait_ge(s_p5, t + 2)
                            for c in range(C):
                                last = nc.tensor.matmul(S5[:, :], cw[:, a % 2, c, :], qT[:, a % 2, c, :],
                                                        start=c == 0, stop=c == C - 1)
                            last.then_inc(s_s5, 1)
                        if on(t + 1):
                            a = q(1)
                            pe.wait_ge(s_an, t + 2)
                            if due(t + 1):
                                pe.wait_ge(s_at, t + 1)
                            nc.tensor.transpose(A5[:, :], pa[:, a % 2, :], ident[:, :]).then_inc(s_a5, 1)
                        if on(t):
                            if due(t - 1):
                                pe.wait_ge(s_x3, t - 1)
                            pe.wait_ge(s_ut, t + 1)
                            project(t, k, [uT[:, k % 2, c, :] for c in range(C)], [wl[:, C + c, :] for c in range(C)],
                                    first=True)
                            pe.wait_ge(s_vt, t + 1)
                            project(t, k, [vT[:, k % 2, c, :] for c in range(C)], [wl[:, 2 * C + c, :] for c in range(C)])
                        if on(t + 1):
                            a = q(1)
                            pe.wait_ge(s_at, t + 2)
                            if due(t + 1):
                                pe.wait_ge(s_ut, t + 1)
                            for c in range(C):
                                last = nc.tensor.matmul(U5[:, c, :], cx[:, a, c * P:(c + 1) * P], aT[:, a % 2, :],
                                                        start=True, stop=True)
                            last.then_inc(s_u5, 1)
                        if on(t + 3):
                            a = q(3)
                            pe.wait_ge(s_l5[a], (t + 3 - a) * 4 + 16)
                            pe.wait_ge(s_c5, t + 4)
                            if due(t + 3):
                                pe.wait_ge(s_q5, t + 3)
                            for c in range(C):
                                nc.tensor.transpose(T5[:, c, :], c5[:, a, c * P:(c + 1) * P], ident[:, :])
                            for c in range(C):
                                last = nc.tensor.transpose(T5[:, C + c, :], cx[:, a, c * P:(c + 1) * P], ident[:, :])
                            last.then_inc(s_t5, 1)
                        if on(t):
                            pe.wait_ge(s_wz, 2 * t + 2)
                            project(t, k, [cT[:, k, c, :] for c in range(C)], [wz[:, k % 2, c, :] for c in range(C)],
                                    final=True).then_inc(s_z, 1)
                        if on(t + 1):
                            a = q(1)
                            pe.wait_ge(s_be, t + 2)
                            if due(t + 1):
                                pe.wait_ge(s_qc, t + 1)
                            for c in range(C):
                                nc.tensor.matmul(Q5[:, c:c + 1], c5[:, a, c * P:(c + 1) * P], be[:, a, :],
                                                 start=True, stop=True)
                            nc.tensor.matmul(Q5[:, C:C + 1], ones[:, :], be[:, a, :], start=True, stop=True
                                             ).then_inc(s_Q, 1)

                    steps(pe, *RANGE5, body)

        with ExitStack() as ph:
            sb = lambda name, shape, dt=F32: ph.enter_context(nc.sbuf_tensor(name, shape, dt))
            x6 = sb("x6", [P, 4, 2, D])
            st6 = sb("st6", [P, 4, 2, 6])
            mv6 = sb("mv6", [P, 4, 2, 2])
            rs6 = sb("rs6", [P, 4, 2, 2])
            n6 = sb("n6", [P, 2, 2, D])
            T6s = sb("T6s", [P, 2, 2, C, 2, P], F16)
            gf = sb("gf", [P, 4, 2, 2 * P])
            g6 = sb("g6", [P, 2, 2, FC, 2 * P], F16)
            o6 = sb("o6", [P, 2, 2, D])
            bo6 = sb("bo6", [P, 3, D])
            T6 = [ph.enter_context(nc.psum_tensor(f"T6{i}", [P, C, P], F32)) for i in range(2)]
            H6 = [ph.enter_context(nc.psum_tensor(f"H6{i}", [P, 2 * P], F32)) for i in range(4)]
            Y6 = [ph.enter_context(nc.psum_tensor(f"Y6{i}", [P, D], F32)) for i in range(2)]
            s_b6 = sem("s_b6")
            s_w6, BASE_W = s_ws, 48
            s_l6, BASE_L = s_ld, 32 * (NB // 4)
            s_mv6, s_rs6, s_n6, s_t6, s_e6, s_h6, s_g6, s_y6, s_a6, s_o6 = (
                sem(f"s6_{i}") for i in range(10))
            s_ost, BASE_S = s_x1st, 16 * (NB // 2)
            s_x6h, BASE_X = s_xh3, NP
            s_gh, s_gl, BASE_G = s_fh, s_fl, 2 * NP
            RANGE6 = (-4, NP + 1, 4, NP - 4, 4)
            with nc.Block() as block:
                @block.sync
                def _(sp):
                    as_rows = lambda a: a.rearrange("(o d) -> o d", o=1).broadcast_to([P, D])

                    def body(t, k):
                        if onp(t + 4):
                            if due(2 * t + 2):
                                sp.wait_ge(s_o6, 2 * t + 2)
                            sp.dma_start(x6[:, k, :, :], x3_d[bass.ds((t + 4) * 2, 2), :, :].rearrange("t p n -> p t n")
                                         ).then_inc(s_l6[k], 16)
                        if isinstance(t, int) and t == -2:
                            sp.dma_start(bo6[:, 0, :], as_rows(b_con)).then_inc(s_w6, 16)
                            sp.dma_start(bo6[:, 1, :], as_rows(dn_bias)).then_inc(s_w6, 16)
                        if onp(t):
                            sp.wait_ge(s_o6, 2 * t + 2)
                            sp.dma_start(out[bass.ds(t * 2, 2), :, :].rearrange("t p n -> p t n"),
                                         o6[:, k % 2, :, :]).then_inc(s_ost[k % 2], 16)

                    steps(sp, *RANGE6, body)
                    for j in range(2):
                        sp.wait_ge(s_ost[j], 16 * (NP // 2) + BASE_S)

                @block.gpsimd
                def _(pool):
                    def body(t, k):
                        if onp(t + 2):
                            a = (k + 2) % 4
                            pool.wait_ge(s_mv6, 4 * t + 12)
                            nc.gpsimd.tensor_tensor(out=rs6[:, a, :, 0:1], in0=mv6[:, a, :, 1:2],
                                                    in1=epsc[:, :].unsqueeze(1).broadcast_to([P, 2, 1]), op=ALU.add).then_inc(s_rs6, 1)
                            pool.wait_ge(s_rs6, 2 * t + 5)
                            nc.gpsimd.tensor_tensor(out=rs6[:, a, :, 1:2], in0=rs6[:, a, :, 0:1],
                                                    in1=mhalf[:, :].unsqueeze(1).broadcast_to([P, 2, 1]),
                                                    op=ALU.pow).then_inc(s_rs6, 1)
                        if isinstance(t, int) and t == -1:
                            pool.wait_ge(s_w6, 32 + BASE_W)
                            nc.gpsimd.tensor_tensor(out=bo6[:, 2, :], in0=bo6[:, 0, :], in1=bo6[:, 1, :],
                                                    op=ALU.add).then_inc(s_b6, 1)

                    steps(pool, *RANGE6, body)

                @block.vector
                def _(dve):

                    def stats(t, a):
                        if onp(t):
                            dve.wait_ge(s_l6[a], (t - a) * 4 + 16 + BASE_L)
                            for j in range(2):
                                nc.vector.bn_stats(st6[:, a, j, :], x6[:, a, j, :]).then_inc(s_mv6, 1)
                            for j in range(2):
                                dve.wait_ge(s_mv6, 4 * t + 1 + j)
                                take_wait(nc.vector)
                                nc.vector.bn_aggr(mv6[:, a, j, :], st6[:, a, j, :]).then_inc(s_mv6, 1)

                    def finish(t, a, j):
                        if onp(t):
                            dve.wait_ge(s_y6, 2 * t + 1 + j)
                            dve.wait_ge(s_ost[a % 2], (t - a % 2) * 8 + BASE_S)
                            nc.vector.scalar_tensor_tensor(o6[:, a % 2, j, :], Y6[j][:, :], wdesc[:, 1:2],
                                                           x6[:, a, j, :], ALU.mult, ALU.add).then_inc(s_a6, 1)
                            dve.wait_ge(s_a6, 2 * t + 1 + j)
                            nc.vector.tensor_tensor(o6[:, a % 2, j, :], o6[:, a % 2, j, :], bo6[:, 2, :],
                                                    ALU.add).then_inc(s_o6, 1)

                    def body(t, k):
                        if isinstance(t, int) and t == 1:
                            dve.wait_ge(s_b6, 1)
                        q = lambda n: (k + n) % 4
                        if onp(t + 1):
                            a = q(1)
                            dve.wait_ge(s_rs6, 2 * t + 4)
                            if due(2 * t):
                                dve.wait_ge(s_t6, 2 * t)
                            for j in range(2):
                                nc.vector.tensor_scalar(n6[:, a % 2, j, :], x6[:, a, j, :], mv6[:, a, j, 0:1],
                                                        rs6[:, a, j, 1:2], ALU.subtract, ALU.mult).then_inc(s_n6, 1)
                        for q in range(FC // 2):
                            if q == 2 and onp(t + 1):
                                for j in range(2):
                                    a = (k + 1) % 2
                                    dve.wait_ge(s_x6h, 2 * t + 3 + j + BASE_X)
                                    nc.vector.scalar_tensor_tensor(T6s[:, a, LO, :, j, :], T6[j][:, :, :], XS,
                                                                   T6s[:, a, HI, :, j, :], ALU.mult,
                                                                   ALU.subtract).then_inc(s_e6, 1)
                            if onp(t):
                                dve.wait_ge(s_gh, FC // 2 * t + q + 1 + BASE_G)
                                nc.vector.scalar_tensor_tensor(
                                    g6[:, k % 2, LO, 2 * q:2 * q + 2, :], gf[:, q, :, :], GS,
                                    g6[:, k % 2, HI, 2 * q:2 * q + 2, :], ALU.mult, ALU.subtract).then_inc(s_gl, 1)
                            if q == 1:
                                finish(t - 1, (k - 1) % 4, 0)
                                stats(t + 2, (k + 2) % 4)
                        finish(t - 1, (k - 1) % 4, 1)

                    steps(dve, *RANGE6, body)

                @block.scalar
                def _(act):
                    nc.scalar.activation(spare[:, 2, 0:1], ones[0:1, 0:1], ACT.Gelu)

                    def body(t, k):
                        for q in range(FC // 2):
                            if q == 2 and onp(t + 1):
                                for j in range(2):
                                    act.wait_ge(s_t6, 2 * t + 3 + j)
                                    if due(FC * t):
                                        act.wait_ge(s_h6, FC * t)
                                    nc.scalar.mul(T6s[:, (k + 1) % 2, HI, :, j, :], T6[j][:, :, :], XS).then_inc(s_x6h, 1)
                            if onp(t):
                                for j in range(2):
                                    b = 2 * q + j
                                    act.wait_ge(s_h6, FC * t + b + 1)
                                    act.wait_ge(s_gl, FC // 2 * (t - 1) + q + 1 + BASE_G)
                                    nc.scalar.activation(gf[:, q, j, :], H6[b % 4][:, :], ACT.Gelu, bias=bup[:, b:b + 1],
                                                         scale=wdesc[:, 0:1]).then_inc(s_g6, 1)
                                act.wait_ge(s_g6, FC * t + 2 * q + 2)
                                if due(2 * t - 2):
                                    act.wait_ge(s_y6, 2 * t - 2)
                                nc.scalar.mul(g6[:, k % 2, HI, 2 * q:2 * q + 2, :], gf[:, q, :, :], GS).then_inc(s_gh, 1)

                    steps(act, *RANGE6, body)

                @block.tensor
                def _(pe):
                    def tr(t, k):
                        if onp(t):
                            pe.wait_ge(s_n6, 2 * t + 2)
                            if due(2 * t):
                                pe.wait_ge(s_e6, 2 * t)
                            for j in range(2):
                                for c in range(C):
                                    last = nc.tensor.transpose(T6[j][:, c, :], n6[:, k % 2, j, c * P:(c + 1) * P], ident[:, :])
                                last.then_inc(s_t6, 1)

                    def up(t, k, b):
                        if onp(t):
                            pe.wait_ge(s_e6, 2 * t + 2)
                            if due(FC * t + b - 3):
                                pe.wait_ge(s_g6, FC * t + b - 3)
                            for i, (wp, xp) in enumerate(PARTS):
                                for c in range(C):
                                    last = nc.tensor.matmul(H6[b % 4][:, :], wup[:, c, wp, b * P:(b + 1) * P],
                                                            T6s[:, k % 2, xp, c, :, :], start=i == 0 and c == 0,
                                                            stop=i == 2 and c == C - 1)
                            last.then_inc(s_h6, 1)

                    def down(t, k, j, half):
                        if onp(t):
                            pe.wait_ge(s_gl, FC // 2 * (t + 1) + BASE_G)
                            if due(2 * t - 1 + j):
                                pe.wait_ge(s_a6, 2 * t - 1 + j)
                            for i, (xp, wp) in enumerate(PARTS):
                                for b in range(FC // 2):
                                    last = nc.tensor.matmul(
                                        Y6[j][:, :], g6[:, k % 2, xp, half * FC // 2 + b, j * P:(j + 1) * P],
                                        wdp[:, half, wp, b * D:(b + 1) * D], start=half == 0 and i == 0 and b == 0,
                                        stop=half == 1 and i == 2 and b == FC // 2 - 1)
                            if half:
                                last.then_inc(s_y6, 1)

                    def body(t, k):
                        up(t, k, 0)
                        up(t, k, 1)
                        down(t - 1, k + 1, 0, 0)
                        up(t, k, 2)
                        up(t, k, 3)
                        tr(t + 1, k + 1)
                        down(t - 1, k + 1, 0, 1)
                        up(t, k, 4)
                        up(t, k, 5)
                        down(t - 1, k + 1, 1, 0)
                        up(t, k, 6)
                        up(t, k, 7)
                        down(t - 1, k + 1, 1, 1)

                    steps(pe, *RANGE6, body)


_INS = ['x', 'ctx_1024', 'L0_ffn_Wr', 'L0_ffn_rb', 'L0_ffn_W1', 'L0_ffn_W2', 'L0_ffn_W3', 'L0_ffn_Ws1', 'L0_ffn_Ws2',
        'L0_ffn_Ws3', 'L1_xattn_w_cq', 'L1_xattn_b_cq', 'L1_xattn_w_c', 'L1_xattn_b_c', 'L1_xattn_w_q', 'L1_xattn_b_q',
        'L1_xattn_W_l', 'L1_xattn_b_l', 'L1_ffn_W_exp', 'L1_ffn_b_exp', 'L1_ffn_up_weights', 'L1_ffn_up_bias',
        'L1_ffn_down_weights', 'L1_ffn_W_con', 'L1_ffn_b_con', 'L1_ffn_down_bias']
_TRANSPOSED = ('L1_xattn_W_l', 'L1_ffn_W_exp')


def kernel(**inputs):
    import numpy as _np
    import concourse.bacc as _bacc
    from concourse import mybir as _mybir
    from concourse.bass_utils import run_bass_kernel_spmd as _run

    nc = _bacc.Bacc("TRN2", target_bir_lowering=False, num_devices=1)
    arrays, args = {}, []
    for name in _INS:
        a = _np.asarray(inputs[name])
        a = _np.ascontiguousarray(a.T if name in _TRANSPOSED else a)
        if a.ndim == 0:
            a = a.reshape(1)
        arrays[f"in_{name}_dram"] = a
        args.append(nc.dram_tensor(f"in_{name}_dram", a.shape, _mybir.dt.from_np(a.dtype), kind="ExternalInput").ap())
    shape = tuple(inputs['x'].shape)
    args.append(nc.dram_tensor("out_dram", shape, _mybir.dt.float32, kind="ExternalOutput").ap())
    build_program(nc, *args)
    r = _run(nc, [arrays], core_ids=[0])
    return r.results[0]["out_dram"]
```
